# Optimizing a Trainium2 kernel written in Bass

```python
import numpy as np
import jax
import jax.numpy as jnp

def _softmax(x, axis=-1):
    return jax.nn.softmax(x, axis=axis)

def _gelu(x):
    return jax.nn.gelu(x, approximate=True)

def _silu(x):
    return jax.nn.silu(x)

def _sigmoid(x):
    return jax.nn.sigmoid(x)

def _layernorm(x, axis=-1, eps=1e-05):
    m = jnp.mean(x, axis=axis, keepdims=True)
    v = jnp.var(x, axis=axis, keepdims=True)
    return (x - m) / jnp.sqrt(v + eps)

def _scatter_add(tgt, idx, src, axis=0):
    return tgt.at[idx].add(src)

def _segment_sum(src, seg, n):
    return jax.ops.segment_sum(src, seg, n)
kernel_name = 'mk_gps_d4_gnn_r8_796019'

def setup_inputs(seed: int=0):
    np.random.seed(seed)
    _w = jnp.asarray

    def _rec_inputs():
        import jax
        import jax.numpy as jnp
        _gk = jax.random.key(seed)
        x = -0.0002117 + 1 * jax.random.normal(jax.random.fold_in(_gk, 1), (1250, 512), jnp.float32)
        src = jax.random.randint(jax.random.fold_in(_gk, 2), (40000,), 0, 1250, jnp.int32)
        dst = jnp.minimum((1250 * jax.random.uniform(jax.random.fold_in(_gk, 3), (40000,)) ** 2.0).astype(jnp.int32), 9999)
        _o = jnp.argsort(dst, stable=True)
        src = src[_o]
        dst = dst[_o]
        edge_type_8 = jax.random.randint(jax.random.fold_in(_gk, 13), (40000,), 0, 8, jnp.int32)
        edge_weight1 = jax.random.uniform(jax.random.fold_in(_gk, 14), (40000, 1), jnp.float32, 0.0, 0.999994)
        return (x, src, dst, edge_type_8, edge_weight1)
    x, src, dst, edge_type_8, edge_weight1 = _rec_inputs()

    def _L0_gnn_setup():
        import jax, jax.numpy as jnp
        import numpy as np
        N_NODES = 6250
        N_EDGES = 100000
        D = 512
        N_LAYERS = 3
        EPS = 1e-12
        key = jax.random.key(seed)
        ks = jax.random.split(key, 6)
        x = jax.random.normal(ks[0], (N_NODES, D), dtype=jnp.float32)
        src = jax.random.randint(ks[1], (N_EDGES,), 0, N_NODES, dtype=jnp.int64)
        dst = jax.random.randint(ks[2], (N_EDGES,), 0, N_NODES, dtype=jnp.int64)
        scale = 1.0 / np.sqrt(D)
        W_self = jax.random.normal(ks[3], (N_LAYERS, D, D), dtype=jnp.float32) * scale
        W_neigh = jax.random.normal(ks[4], (N_LAYERS, D, D), dtype=jnp.float32) * scale
        b = jax.random.normal(ks[5], (N_LAYERS, D), dtype=jnp.float32) * 0.01
        return {'x': x, 'src': src, 'dst': dst, 'W_self': W_self, 'W_neigh': W_neigh, 'b': b}
    _L0_gnn_all = _L0_gnn_setup()
    _L0_gnn_in = {k: v for k, v in _L0_gnn_all.items() if k in ('W_self', 'W_neigh', 'b')}
    del _L0_gnn_all

    def _L0_mix_setup():
        import jax, jax.numpy as jnp
        import numpy as np
        NUM_HEADS = 8
        EPS = 1e-06
        key = jax.random.key(seed)
        k1, k2, k3 = jax.random.split(key, 3)
        B, N, C = (8, 512, 512)
        x = jax.random.normal(k1, (B, N, C), dtype=jnp.float32)
        Wq = jax.random.normal(k2, (C, C), dtype=jnp.float32) * (1.0 / np.sqrt(C))
        Wkv = jax.random.normal(k3, (2 * C, C), dtype=jnp.float32) * (1.0 / np.sqrt(C))
        return {'x': x, 'Wq': Wq, 'Wkv': Wkv}
    _L0_mix_all = _L0_mix_setup()
    _L0_mix_in = {k: v for k, v in _L0_mix_all.items() if k in ('Wq', 'Wkv')}
    del _L0_mix_all

    def _L0_ffn_setup():
        import jax, jax.numpy as jnp
        import numpy as np
        SINKHORN_ITERS = 8
        TEMPERATURE = 1.0
        EPS = 1e-10

        def sinkhorn(gates):
            t = jnp.log(jnp.clip(gates, EPS)) / TEMPERATURE

            def body(t, _):
                t = t - jax.nn.logsumexp(t, axis=-2, keepdims=True)
                t = t - jax.nn.logsumexp(t, axis=-1, keepdims=True)
                return (t, None)
            t, _ = jax.lax.scan(body, t, None, length=SINKHORN_ITERS)
            return jnp.exp(t)
        key = jax.random.key(seed)
        k1, k2, k3 = jax.random.split(key, 3)
        b, n, d, e, h = (4, 1024, 512, 8, 1)
        x = jax.random.normal(k1, (b, n, d), dtype=jnp.float32)
        gate_w = jax.random.normal(k2, (h, d, e), dtype=jnp.float32)
        experts = jax.random.normal(k3, (e, d, d), dtype=jnp.float32) / np.sqrt(d)
        return {'x': x, 'gate_w': gate_w, 'experts': experts}
    _L0_ffn_all = _L0_ffn_setup()
    _L0_ffn_in = {k: v for k, v in _L0_ffn_all.items() if k in ('gate_w', 'experts')}
    del _L0_ffn_all

    def _L1_gnn_setup():
        import jax, jax.numpy as jnp
        import numpy as np
        N_NODES = 1250
        N_EDGES = 20000
        D = 512
        key = jax.random.key(seed)
        k_h, k_e, k_w1, k_w2 = jax.random.split(key, 4)
        h = jax.random.normal(k_h, (N_NODES, D), dtype=jnp.float32)
        edge_index = jax.random.randint(k_e, (2, N_EDGES), 0, N_NODES, dtype=jnp.int64)
        scale = 1.0 / np.sqrt(D)
        W1 = jax.random.normal(k_w1, (D, D), dtype=jnp.float32) * scale
        b1 = jnp.zeros((D,), dtype=jnp.float32)
        W2 = jax.random.normal(k_w2, (D, D), dtype=jnp.float32) * scale
        b2 = jnp.zeros((D,), dtype=jnp.float32)
        return {'h': h, 'edge_index': edge_index, 'W1': W1, 'b1': b1, 'W2': W2, 'b2': b2}
    _L1_gnn_all = _L1_gnn_setup()
    _L1_gnn_in = {k: v for k, v in _L1_gnn_all.items() if k in ('W1', 'b1', 'W2', 'b2')}
    del _L1_gnn_all

    def _L1_mix_setup():
        import jax, jax.numpy as jnp
        import numpy as np
        NUM_HEADS = 8
        key = jax.random.key(seed)
        k1, k2, k3 = jax.random.split(key, 3)
        B, N, C = (4, 512, 512)
        x = jax.random.normal(k1, (B, N, C), dtype=jnp.float32)
        w_qkv = jax.random.normal(k2, (C, 3 * C), dtype=jnp.float32) * (1.0 / np.sqrt(C))
        w_proj = jax.random.normal(k3, (C, C), dtype=jnp.float32) * (1.0 / np.sqrt(C))
        b_proj = jnp.zeros((C,), dtype=jnp.float32)
        return {'x': x, 'w_qkv': w_qkv, 'w_proj': w_proj, 'b_proj': b_proj}
    _L1_mix_all = _L1_mix_setup()
    _L1_mix_in = {k: v for k, v in _L1_mix_all.items() if k in ('w_qkv', 'w_proj', 'b_proj')}
    del _L1_mix_all

    def _L1_ffn_setup():
        import jax, jax.numpy as jnp
        import numpy as np
        S, B, D, F, E, K = (1024, 2, 512, 256, 8, 2)
        key = jax.random.key(seed)
        ks = jax.random.split(key, 12)
        s = lambda *sh: 1.0 / np.sqrt(sh[0])
        inp = {'x': jax.random.normal(ks[0], (S, B, D), dtype=jnp.float32), 'Wg': jax.random.normal(ks[1], (D, E), dtype=jnp.float32) * s(D), 'bg': jnp.zeros((E,), dtype=jnp.float32), 'W1': jax.random.normal(ks[2], (E, D, F), dtype=jnp.float32) * s(D), 'b1': jnp.zeros((E, F), dtype=jnp.float32), 'W2': jax.random.normal(ks[3], (E, F, D), dtype=jnp.float32) * s(F), 'b2': jnp.zeros((E, D), dtype=jnp.float32), 'Ws1': jax.random.normal(ks[4], (D, F), dtype=jnp.float32) * s(D), 'bs1': jnp.zeros((F,), dtype=jnp.float32), 'Ws2': jax.random.normal(ks[5], (F, D), dtype=jnp.float32) * s(F), 'bs2': jnp.zeros((D,), dtype=jnp.float32)}
        return inp
    _L1_ffn_all = _L1_ffn_setup()
    _L1_ffn_in = {k: v for k, v in _L1_ffn_all.items() if k in ('Wg', 'bg', 'W1', 'b1', 'W2', 'b2', 'Ws1', 'bs1', 'Ws2', 'bs2')}
    del _L1_ffn_all

    def _L2_gnn_setup():
        import jax, jax.numpy as jnp
        import numpy as np
        N_NODES = 2500
        N_EDGES = 40000
        N_REL = 8
        D_IN = 512
        D_OUT = 512
        key = jax.random.key(seed)
        k1, k2, k3, k4, k5 = jax.random.split(key, 5)
        x = jax.random.normal(k1, (N_NODES, D_IN), dtype=jnp.float32)
        W_self = jax.random.normal(k2, (D_OUT, D_IN), dtype=jnp.float32) * 0.05
        W_rel = jax.random.normal(k3, (N_REL, D_OUT, D_IN), dtype=jnp.float32) * 0.05
        bias = jnp.zeros((D_OUT,), dtype=jnp.float32)
        edge_index = jax.random.randint(k4, (2, N_EDGES), 0, N_NODES, dtype=jnp.int64)
        edge_type = jax.random.randint(k5, (N_EDGES,), 0, N_REL, dtype=jnp.int64)
        return {'x': x, 'W_self': W_self, 'W_rel': W_rel, 'bias': bias, 'edge_index': edge_index, 'edge_type': edge_type}
    _L2_gnn_all = _L2_gnn_setup()
    _L2_gnn_in = {k: v for k, v in _L2_gnn_all.items() if k in ('W_self', 'W_rel', 'bias')}
    del _L2_gnn_all

    def _L2_mix_setup():
        import jax, jax.numpy as jnp
        import numpy as np
        HEADS = 8
        EPS_LN = 1e-05
        EPS_NORM = 1e-08
        key = jax.random.key(seed)
        ks = jax.random.split(key, 3)
        B, N, C = (4, 1024, 512)
        x = jax.random.normal(ks[0], (B, N, C), dtype=jnp.float32)
        qkv_w = jax.random.normal(ks[1], (3 * C, C), dtype=jnp.float32) / np.sqrt(C)
        qkv_b = jnp.zeros((3 * C,), dtype=jnp.float32)
        out_w = jax.random.normal(ks[2], (C, C), dtype=jnp.float32) / np.sqrt(C)
        out_b = jnp.zeros((C,), dtype=jnp.float32)
        ln_gamma = jnp.ones((C,), dtype=jnp.float32)
        ln_beta = jnp.zeros((C,), dtype=jnp.float32)
        return {'x': x, 'qkv_w': qkv_w, 'qkv_b': qkv_b, 'out_w': out_w, 'out_b': out_b, 'ln_gamma': ln_gamma, 'ln_beta': ln_beta}
    _L2_mix_all = _L2_mix_setup()
    _L2_mix_in = {k: v for k, v in _L2_mix_all.items() if k in ('qkv_w', 'qkv_b', 'out_w', 'out_b', 'ln_gamma', 'ln_beta')}
    del _L2_mix_all

    def _L2_ffn_setup():
        import jax, jax.numpy as jnp
        import numpy as np
        B, S, D, F, E = (8, 512, 512, 256, 8)
        INIT_LAMBDA = 0.2
        LN_EPS = 1e-05
        LN_MERGE = 0.03
        key = jax.random.key(seed)
        ks = jax.random.split(key, 12)
        n = lambda k, shp, s=1.0: jax.random.normal(k, shp, dtype=jnp.float32) * s
        return {'hidden_states': n(ks[0], (B, S, D)), 'gfc1_w': n(ks[1], (D, D), 0.01), 'gfc1_b': jnp.zeros((D,), jnp.float32), 'gfc2_w': n(ks[2], (E, D), 0.01), 'gfc2_b': jnp.full((E,), INIT_LAMBDA, dtype=jnp.float32), 'W1': n(ks[3], (F, D), 0.02), 'b1': jnp.zeros((F,), jnp.float32), 'W2': n(ks[4], (D, F), 0.02), 'b2': jnp.zeros((D,), jnp.float32), 'ln_g': jnp.ones((D,), jnp.float32), 'ln_b': jnp.zeros((D,), jnp.float32), 'tv_W1': n(ks[5], (E, F, D), 0.02), 'tv_b1': n(ks[6], (E, F), 0.02), 'tv_W2': n(ks[7], (E, D, F), 0.02), 'tv_b2': n(ks[8], (E, D), 0.02), 'tv_ln_g': n(ks[9], (E, D), 0.02), 'tv_ln_b': n(ks[10], (E, D), 0.02)}
    _L2_ffn_all = _L2_ffn_setup()
    _L2_ffn_in = {k: v for k, v in _L2_ffn_all.items() if k in ('gfc1_w', 'gfc1_b', 'gfc2_w', 'gfc2_b', 'W1', 'b1', 'W2', 'b2', 'ln_g', 'ln_b', 'tv_W1', 'tv_b1', 'tv_W2', 'tv_b2', 'tv_ln_g', 'tv_ln_b')}
    del _L2_ffn_all

    def _L3_gnn_setup():
        import jax, jax.numpy as jnp
        import numpy as np
        N_NODES = 6250
        N_EDGES = 20000
        D_IN = 512
        D_OUT = 512
        key = jax.random.key(seed)
        k1, k2, k3, k4, k5, k6 = jax.random.split(key, 6)
        feature = jax.random.normal(k1, (N_NODES, D_IN), dtype=jnp.float32)
        edge_w = jax.random.uniform(k2, (N_EDGES, 1), dtype=jnp.float32)
        W = jax.random.normal(k3, (D_OUT, D_IN), dtype=jnp.float32) / np.sqrt(D_IN)
        b = jax.random.normal(k4, (D_OUT,), dtype=jnp.float32) * 0.01
        src = jax.random.randint(k5, (N_EDGES,), 0, N_NODES, dtype=jnp.int32)
        dst = jax.random.randint(k6, (N_EDGES,), 0, N_NODES, dtype=jnp.int32)
        return {'feature': feature, 'edge_w': edge_w, 'W': W, 'b': b, 'src': src, 'dst': dst}
    _L3_gnn_all = _L3_gnn_setup()
    _L3_gnn_in = {k: v for k, v in _L3_gnn_all.items() if k in ('W', 'b')}
    del _L3_gnn_all

    def _L3_mix_setup():
        import jax, jax.numpy as jnp
        import numpy as np
        B, T, DIM = (32, 392, 512)
        EMB = 512
        M = 256
        EPS_ATTN = 1e-08
        EPS_LN = 0.001

        def layernorm(x, g, b):
            mu = jnp.mean(x, axis=-1, keepdims=True)
            var = jnp.var(x, axis=-1, keepdims=True)
            return (x - mu) / jnp.sqrt(var + EPS_LN) * g + b

        def prm_exp(x, w):
            xd = jnp.sum(x * x, axis=-1, keepdims=True) / 2.0
            wtx = jnp.einsum('bti,mi->btm', x, w)
            return jnp.exp(wtx - xd) / jnp.sqrt(jnp.float32(M))
        key = jax.random.key(seed)
        ks = jax.random.split(key, 16)
        s_in = 1.0 / np.sqrt(DIM)
        s_emb = 1.0 / np.sqrt(EMB)
        x = jax.random.normal(ks[0], (B, T, DIM), dtype=jnp.float32)
        kqv_w = jax.random.normal(ks[1], (DIM, 3 * EMB), dtype=jnp.float32) * s_in
        kqv_b = jnp.zeros((3 * EMB,), dtype=jnp.float32)
        proj_w = jax.random.normal(ks[2], (EMB, EMB), dtype=jnp.float32) * s_emb
        proj_b = jnp.zeros((EMB,), dtype=jnp.float32)
        n1_g = jnp.ones((DIM,), dtype=jnp.float32)
        n1_b = jnp.zeros((DIM,), dtype=jnp.float32)
        n2_g = jnp.ones((EMB,), dtype=jnp.float32)
        n2_b = jnp.zeros((EMB,), dtype=jnp.float32)
        mlp_w1 = jax.random.normal(ks[3], (EMB, EMB), dtype=jnp.float32) * s_emb
        mlp_b1 = jnp.zeros((EMB,), dtype=jnp.float32)
        mlp_w2 = jax.random.normal(ks[4], (EMB, EMB), dtype=jnp.float32) * s_emb
        mlp_b2 = jnp.zeros((EMB,), dtype=jnp.float32)
        a = jax.random.normal(ks[5], (EMB, M), dtype=jnp.float32)
        q, _ = jnp.linalg.qr(a)
        w = q.T * jnp.sqrt(jnp.float32(M))
        return {'x': x, 'kqv_w': kqv_w, 'kqv_b': kqv_b, 'proj_w': proj_w, 'proj_b': proj_b, 'n1_g': n1_g, 'n1_b': n1_b, 'n2_g': n2_g, 'n2_b': n2_b, 'mlp_w1': mlp_w1, 'mlp_b1': mlp_b1, 'mlp_w2': mlp_w2, 'mlp_b2': mlp_b2, 'w': w}
    _L3_mix_all = _L3_mix_setup()
    _L3_mix_in = {k: v for k, v in _L3_mix_all.items() if k in ('kqv_w', 'kqv_b', 'proj_w', 'proj_b', 'n1_g', 'n1_b', 'n2_g', 'n2_b', 'mlp_w1', 'mlp_b1', 'mlp_w2', 'mlp_b2', 'w')}
    del _L3_mix_all

    def _L3_ffn_setup():
        import jax, jax.numpy as jnp
        import numpy as np
        E = 8
        TOP_K = 2
        D = 512
        H = 1024
        B, S = (16, 512)
        key = jax.random.key(seed)
        ks = jax.random.split(key, 10)
        sd = lambda fan_in: 1.0 / np.sqrt(fan_in)
        x = jax.random.normal(ks[0], (B, S, D), dtype=jnp.float32)
        gw1 = jax.random.uniform(ks[1], (D, D // 2), jnp.float32, -sd(D), sd(D))
        gb1 = jnp.zeros((D // 2,), jnp.float32)
        gw2 = jax.random.uniform(ks[2], (D // 2, E), jnp.float32, -sd(D // 2), sd(D // 2))
        gb2 = jnp.zeros((E,), jnp.float32)
        we1 = jax.random.uniform(ks[3], (E, D, H), jnp.float32, -sd(D), sd(D))
        be1 = jnp.zeros((E, H), jnp.float32)
        we2 = jax.random.uniform(ks[4], (E, H, D), jnp.float32, -sd(H), sd(H))
        be2 = jnp.zeros((E, D), jnp.float32)
        return {'x': x, 'gw1': gw1, 'gb1': gb1, 'gw2': gw2, 'gb2': gb2, 'we1': we1, 'be1': be1, 'we2': we2, 'be2': be2}
    _L3_ffn_all = _L3_ffn_setup()
    _L3_ffn_in = {k: v for k, v in _L3_ffn_all.items() if k in ('gw1', 'gb1', 'gw2', 'gb2', 'we1', 'be1', 'we2', 'be2')}
    del _L3_ffn_all
    return {'x': x, 'src': src, 'dst': dst, 'edge_type_8': edge_type_8, 'edge_weight1': edge_weight1, 'L0_gnn_W_self': _L0_gnn_in['W_self'], 'L0_gnn_W_neigh': _L0_gnn_in['W_neigh'], 'L0_gnn_b': _L0_gnn_in['b'], 'L0_mix_Wq': _L0_mix_in['Wq'], 'L0_mix_Wkv': _L0_mix_in['Wkv'], 'L0_ffn_gate_w': _L0_ffn_in['gate_w'], 'L0_ffn_experts': _L0_ffn_in['experts'], 'L1_gnn_W1': _L1_gnn_in['W1'], 'L1_gnn_b1': _L1_gnn_in['b1'], 'L1_gnn_W2': _L1_gnn_in['W2'], 'L1_gnn_b2': _L1_gnn_in['b2'], 'L1_mix_w_qkv': _L1_mix_in['w_qkv'], 'L1_mix_w_proj': _L1_mix_in['w_proj'], 'L1_mix_b_proj': _L1_mix_in['b_proj'], 'L1_ffn_Wg': _L1_ffn_in['Wg'], 'L1_ffn_bg': _L1_ffn_in['bg'], 'L1_ffn_W1': _L1_ffn_in['W1'], 'L1_ffn_b1': _L1_ffn_in['b1'], 'L1_ffn_W2': _L1_ffn_in['W2'], 'L1_ffn_b2': _L1_ffn_in['b2'], 'L1_ffn_Ws1': _L1_ffn_in['Ws1'], 'L1_ffn_bs1': _L1_ffn_in['bs1'], 'L1_ffn_Ws2': _L1_ffn_in['Ws2'], 'L1_ffn_bs2': _L1_ffn_in['bs2'], 'L2_gnn_W_self': _L2_gnn_in['W_self'], 'L2_gnn_W_rel': _L2_gnn_in['W_rel'], 'L2_gnn_bias': _L2_gnn_in['bias'], 'L2_mix_qkv_w': _L2_mix_in['qkv_w'], 'L2_mix_qkv_b': _L2_mix_in['qkv_b'], 'L2_mix_out_w': _L2_mix_in['out_w'], 'L2_mix_out_b': _L2_mix_in['out_b'], 'L2_mix_ln_gamma': _L2_mix_in['ln_gamma'], 'L2_mix_ln_beta': _L2_mix_in['ln_beta'], 'L2_ffn_gfc1_w': _L2_ffn_in['gfc1_w'], 'L2_ffn_gfc1_b': _L2_ffn_in['gfc1_b'], 'L2_ffn_gfc2_w': _L2_ffn_in['gfc2_w'], 'L2_ffn_gfc2_b': _L2_ffn_in['gfc2_b'], 'L2_ffn_W1': _L2_ffn_in['W1'], 'L2_ffn_b1': _L2_ffn_in['b1'], 'L2_ffn_W2': _L2_ffn_in['W2'], 'L2_ffn_b2': _L2_ffn_in['b2'], 'L2_ffn_ln_g': _L2_ffn_in['ln_g'], 'L2_ffn_ln_b': _L2_ffn_in['ln_b'], 'L2_ffn_tv_W1': _L2_ffn_in['tv_W1'], 'L2_ffn_tv_b1': _L2_ffn_in['tv_b1'], 'L2_ffn_tv_W2': _L2_ffn_in['tv_W2'], 'L2_ffn_tv_b2': _L2_ffn_in['tv_b2'], 'L2_ffn_tv_ln_g': _L2_ffn_in['tv_ln_g'], 'L2_ffn_tv_ln_b': _L2_ffn_in['tv_ln_b'], 'L3_gnn_W': _L3_gnn_in['W'], 'L3_gnn_b': _L3_gnn_in['b'], 'L3_mix_kqv_w': _L3_mix_in['kqv_w'], 'L3_mix_kqv_b': _L3_mix_in['kqv_b'], 'L3_mix_proj_w': _L3_mix_in['proj_w'], 'L3_mix_proj_b': _L3_mix_in['proj_b'], 'L3_mix_n1_g': _L3_mix_in['n1_g'], 'L3_mix_n1_b': _L3_mix_in['n1_b'], 'L3_mix_n2_g': _L3_mix_in['n2_g'], 'L3_mix_n2_b': _L3_mix_in['n2_b'], 'L3_mix_mlp_w1': _L3_mix_in['mlp_w1'], 'L3_mix_mlp_b1': _L3_mix_in['mlp_b1'], 'L3_mix_mlp_w2': _L3_mix_in['mlp_w2'], 'L3_mix_mlp_b2': _L3_mix_in['mlp_b2'], 'L3_mix_w': _L3_mix_in['w'], 'L3_ffn_gw1': _L3_ffn_in['gw1'], 'L3_ffn_gb1': _L3_ffn_in['gb1'], 'L3_ffn_gw2': _L3_ffn_in['gw2'], 'L3_ffn_gb2': _L3_ffn_in['gb2'], 'L3_ffn_we1': _L3_ffn_in['we1'], 'L3_ffn_be1': _L3_ffn_in['be1'], 'L3_ffn_we2': _L3_ffn_in['we2'], 'L3_ffn_be2': _L3_ffn_in['be2']}

def reference(x, src, dst, edge_type_8, edge_weight1, L0_gnn_W_self, L0_gnn_W_neigh, L0_gnn_b, L0_mix_Wq, L0_mix_Wkv, L0_ffn_gate_w, L0_ffn_experts, L1_gnn_W1, L1_gnn_b1, L1_gnn_W2, L1_gnn_b2, L1_mix_w_qkv, L1_mix_w_proj, L1_mix_b_proj, L1_ffn_Wg, L1_ffn_bg, L1_ffn_W1, L1_ffn_b1, L1_ffn_W2, L1_ffn_b2, L1_ffn_Ws1, L1_ffn_bs1, L1_ffn_Ws2, L1_ffn_bs2, L2_gnn_W_self, L2_gnn_W_rel, L2_gnn_bias, L2_mix_qkv_w, L2_mix_qkv_b, L2_mix_out_w, L2_mix_out_b, L2_mix_ln_gamma, L2_mix_ln_beta, L2_ffn_gfc1_w, L2_ffn_gfc1_b, L2_ffn_gfc2_w, L2_ffn_gfc2_b, L2_ffn_W1, L2_ffn_b1, L2_ffn_W2, L2_ffn_b2, L2_ffn_ln_g, L2_ffn_ln_b, L2_ffn_tv_W1, L2_ffn_tv_b1, L2_ffn_tv_W2, L2_ffn_tv_b2, L2_ffn_tv_ln_g, L2_ffn_tv_ln_b, L3_gnn_W, L3_gnn_b, L3_mix_kqv_w, L3_mix_kqv_b, L3_mix_proj_w, L3_mix_proj_b, L3_mix_n1_g, L3_mix_n1_b, L3_mix_n2_g, L3_mix_n2_b, L3_mix_mlp_w1, L3_mix_mlp_b1, L3_mix_mlp_w2, L3_mix_mlp_b2, L3_mix_w, L3_ffn_gw1, L3_ffn_gb1, L3_ffn_gw2, L3_ffn_gb2, L3_ffn_we1, L3_ffn_be1, L3_ffn_we2, L3_ffn_be2):
    import jax
    import jax.numpy as jnp

    def _L0_gnn_ref(x, src, dst, W_self, W_neigh, b):
        import jax, jax.numpy as jnp
        import numpy as np
        N_NODES = 6250
        N_EDGES = 100000
        D = 512
        N_LAYERS = 3
        EPS = 1e-12
        n = x.shape[0]
        deg = jax.ops.segment_sum(jnp.ones_like(dst, dtype=x.dtype), dst, num_segments=n)
        deg = jnp.maximum(deg, 1.0)[:, None]
        h = x
        for l in range(N_LAYERS):
            h_neigh = jax.ops.segment_sum(h[src], dst, num_segments=n) / deg
            rst = h @ W_self[l] + h_neigh @ W_neigh[l] + b[l]
            rst = jax.nn.relu(rst)
            nrm = jnp.sqrt(jnp.sum(rst * rst, axis=-1, keepdims=True))
            h = rst / jnp.maximum(nrm, EPS)
        return h

    def _L0_mix_ref(x, Wq, Wkv):
        import jax, jax.numpy as jnp
        import numpy as np
        NUM_HEADS = 8
        EPS = 1e-06
        B, N, C = x.shape
        h = NUM_HEADS
        d = C // h
        q = (x @ Wq.T).reshape(B, N, h, d)
        kv = (x @ Wkv.T).reshape(B, N, 2, h, d)
        k = kv[:, :, 0]
        v = kv[:, :, 1]
        Q = jax.nn.elu(q) + 1.0
        K = jax.nn.elu(k) + 1.0
        v_length = v.shape[1]
        v = v / v_length
        KV = jnp.einsum('nshd,nshv->nhdv', K, v)
        Z = 1.0 / (jnp.einsum('nlhd,nhd->nlh', Q, K.sum(axis=1)) + EPS)
        out = jnp.einsum('nlhd,nhdv,nlh->nlhv', Q, KV, Z) * v_length
        return out.reshape(B, N, C)

    def _L0_ffn_ref(x, gate_w, experts):
        import jax, jax.numpy as jnp
        import numpy as np
        SINKHORN_ITERS = 8
        TEMPERATURE = 1.0
        EPS = 1e-10

        def sinkhorn(gates):
            t = jnp.log(jnp.clip(gates, EPS)) / TEMPERATURE

            def body(t, _):
                t = t - jax.nn.logsumexp(t, axis=-2, keepdims=True)
                t = t - jax.nn.logsumexp(t, axis=-1, keepdims=True)
                return (t, None)
            t, _ = jax.lax.scan(body, t, None, length=SINKHORN_ITERS)
            return jnp.exp(t)
        b, n, d = x.shape
        h = gate_w.shape[0]
        e = experts.shape[0]
        N = b * n
        m = n // e
        x4 = x[:, None]
        gates = jnp.einsum('bhnd,hde->bhne', x4, gate_w)
        xf = jnp.transpose(x4, (1, 0, 2, 3)).reshape(h, N, d)
        gf = jnp.transpose(gates, (1, 0, 2, 3)).reshape(h, N, e)
        cg = sinkhorn(gf)
        vals, idx = jax.lax.top_k(jnp.transpose(cg, (0, 2, 1)), m)
        gate_values = (vals > 0.5).astype(x.dtype)
        gate_values = jnp.transpose(gate_values, (0, 2, 1))
        idx = jnp.transpose(idx, (0, 2, 1))
        routed = xf[jnp.arange(h)[:, None, None], idx]
        outputs = jnp.einsum('hmei,eio->hmeo', routed, experts)
        outputs = outputs * gate_values[..., None]
        o_dim = outputs.shape[-1]
        src = outputs.reshape(h, m * e, o_dim)
        idx_flat = idx.reshape(h, m * e)

        def combine(idxf, srcf):
            s = jnp.zeros((N, o_dim), srcf.dtype).at[idxf].add(srcf)
            c = jnp.zeros((N,), srcf.dtype).at[idxf].add(1.0)
            return s / (c + 1.0)[:, None]
        out = jax.vmap(combine)(idx_flat, src)
        out = out.reshape(h, b, n, o_dim)
        out = jnp.transpose(out, (1, 0, 2, 3))[:, 0]
        return out

    def _L1_gnn_ref(h, edge_index, W1, b1, W2, b2):
        import jax, jax.numpy as jnp
        import numpy as np
        N_NODES = 1250
        N_EDGES = 20000
        D = 512
        send, rec = (edge_index[0], edge_index[1])
        agg = jax.ops.segment_sum(h[send], rec, num_segments=h.shape[0])
        x = h + agg
        x = jax.nn.relu(x @ W1 + b1)
        x = x @ W2 + b2
        return x

    def _L1_mix_ref(x, w_qkv, w_proj, b_proj):
        import jax, jax.numpy as jnp
        import numpy as np
        NUM_HEADS = 8
        B, N, C = x.shape
        H = NUM_HEADS
        D = C // H
        qkv = (x @ w_qkv).reshape(B, N, 3, H, D)
        qkv = jnp.transpose(qkv, (2, 0, 3, 1, 4))
        q, k, v = (qkv[0], qkv[1], qkv[2])
        q = jax.nn.softmax(q, axis=-1)
        k = jax.nn.softmax(jax.nn.elu(k) + 1.0, axis=-2)
        context = jnp.einsum('bhnd,bhne->bhde', k, v)
        out = jnp.einsum('bhnd,bhde->bhne', q, context)
        out = jnp.transpose(out, (0, 2, 1, 3)).reshape(B, N, C)
        return out @ w_proj + b_proj

    def _L1_ffn_ref(x, Wg, bg, W1, b1, W2, b2, Ws1, bs1, Ws2, bs2):
        import jax, jax.numpy as jnp
        import numpy as np
        S, B, D, F, E, K = (1024, 2, 512, 256, 8, 2)
        gate_logits = jnp.einsum('sbd,de->sbe', x, Wg) + bg
        weights, selected = jax.lax.top_k(gate_logits, K)
        weights = jax.nn.softmax(weights.astype(jnp.float32), axis=-1)
        onehot = jax.nn.one_hot(selected, E, dtype=weights.dtype)
        comb = jnp.einsum('sbk,sbke->sbe', weights, onehot)
        h = jax.nn.relu(jnp.einsum('sbd,edf->sbef', x, W1) + b1)
        y = jnp.einsum('sbef,efd->sbed', h, W2) + b2
        out = jnp.einsum('sbe,sbed->sbd', comb, y)
        hs = jax.nn.relu(jnp.einsum('sbd,df->sbf', x, Ws1) + bs1)
        shared = jnp.einsum('sbf,fd->sbd', hs, Ws2) + bs2
        out = out + 1.0 / K * shared
        return out

    def _L2_gnn_ref(x, W_self, W_rel, bias, edge_index, edge_type):
        import jax, jax.numpy as jnp
        import numpy as np
        N_NODES = 2500
        N_EDGES = 40000
        N_REL = 8
        D_IN = 512
        D_OUT = 512
        N = x.shape[0]
        R, d_out, _ = W_rel.shape
        src, dst = (edge_index[0], edge_index[1])
        out = jnp.einsum('ni,oi->no', x, W_self)
        h_rel = jnp.einsum('ni,roi->rno', x, W_rel)
        msg = h_rel[edge_type, src]
        seg = edge_type * N + dst
        agg = jax.ops.segment_sum(msg, seg, num_segments=R * N).reshape(R, N, d_out)
        cnt = jax.ops.segment_sum(jnp.ones((msg.shape[0],), dtype=x.dtype), seg, num_segments=R * N).reshape(R, N, 1)
        cnt = jnp.maximum(cnt, 1.0)
        out = out + jnp.sum(agg / cnt, axis=0)
        return out + bias

    def _L2_mix_ref(x, qkv_w, qkv_b, out_w, out_b, ln_gamma, ln_beta):
        import jax, jax.numpy as jnp
        import numpy as np
        HEADS = 8
        EPS_LN = 1e-05
        EPS_NORM = 1e-08
        B, N, C = x.shape
        h = HEADS
        d = C // h
        residual = x
        mu = jnp.mean(x, axis=-1, keepdims=True)
        var = jnp.var(x, axis=-1, keepdims=True)
        xn = (x - mu) / jnp.sqrt(var + EPS_LN) * ln_gamma + ln_beta
        qkv = xn @ qkv_w.T + qkv_b
        qkv = qkv.reshape(B, N, 3, h, d).transpose(2, 0, 3, 1, 4)
        q, k, v = (qkv[0], qkv[1], qkv[2])
        q = jax.nn.elu(q) + 1.0
        k = jax.nn.elu(k) + 1.0
        kv = jnp.einsum('bhnd,bhne->bhde', k, v)
        k_sum = jnp.sum(k, axis=2)
        out = jnp.einsum('bhnd,bhde->bhne', q, kv)
        normalizer = jnp.einsum('bhnd,bhd->bhn', q, k_sum)
        out = out / (normalizer[..., None] + EPS_NORM)
        out = out.transpose(0, 2, 1, 3).reshape(B, N, C)
        out = out @ out_w.T + out_b
        return out + residual

    def _L2_ffn_ref(hidden_states, gfc1_w, gfc1_b, gfc2_w, gfc2_b, W1, b1, W2, b2, ln_g, ln_b, tv_W1, tv_b1, tv_W2, tv_b2, tv_ln_g, tv_ln_b):
        import jax, jax.numpy as jnp
        import numpy as np
        B, S, D, F, E = (8, 512, 512, 256, 8)
        INIT_LAMBDA = 0.2
        LN_EPS = 1e-05
        LN_MERGE = 0.03
        x = hidden_states
        gh = jax.nn.relu(jnp.einsum('bsd,hd->bsh', x, gfc1_w) + gfc1_b)
        g = (jnp.einsum('bsh,eh->bse', gh, gfc2_w) + gfc2_b).mean(axis=1)
        W1m = W1 + jnp.einsum('be,efd->bfd', g, tv_W1)
        b1m = b1 + g @ tv_b1
        W2m = W2 + jnp.einsum('be,edf->bdf', g, tv_W2)
        b2m = b2 + g @ tv_b2
        lng = ln_g + LN_MERGE * (tv_ln_g - ln_g).sum(axis=0)
        lnb = ln_b + LN_MERGE * (tv_ln_b - ln_b).sum(axis=0)
        h = jax.nn.relu(jnp.einsum('bsd,bfd->bsf', x, W1m) + b1m[:, None, :])
        out = jnp.einsum('bsf,bdf->bsd', h, W2m) + b2m[:, None, :]
        res = x + out
        mu = res.mean(axis=-1, keepdims=True)
        var = res.var(axis=-1, keepdims=True)
        return (res - mu) * jax.lax.rsqrt(var + LN_EPS) * lng + lnb

    def _L3_gnn_ref(feature, edge_w, W, b, src, dst):
        import jax, jax.numpy as jnp
        import numpy as np
        N_NODES = 6250
        N_EDGES = 20000
        D_IN = 512
        D_OUT = 512
        m = feature[src] * edge_w
        agg = jax.ops.segment_sum(m, dst, num_segments=feature.shape[0])
        return agg @ W.T + b

    def _L3_mix_ref(x, kqv_w, kqv_b, proj_w, proj_b, n1_g, n1_b, n2_g, n2_b, mlp_w1, mlp_b1, mlp_w2, mlp_b2, w):
        import jax, jax.numpy as jnp
        import numpy as np
        B, T, DIM = (32, 392, 512)
        EMB = 512
        M = 256
        EPS_ATTN = 1e-08
        EPS_LN = 0.001

        def layernorm(x, g, b):
            mu = jnp.mean(x, axis=-1, keepdims=True)
            var = jnp.var(x, axis=-1, keepdims=True)
            return (x - mu) / jnp.sqrt(var + EPS_LN) * g + b

        def prm_exp(x, w):
            xd = jnp.sum(x * x, axis=-1, keepdims=True) / 2.0
            wtx = jnp.einsum('bti,mi->btm', x, w)
            return jnp.exp(wtx - xd) / jnp.sqrt(jnp.float32(M))
        h = layernorm(x, n1_g, n1_b)
        kqv = h @ kqv_w + kqv_b
        k, q, v = jnp.split(kqv, 3, axis=-1)
        kp = prm_exp(k, w)
        qp = prm_exp(q, w)
        D = jnp.einsum('btm,bm->bt', qp, jnp.sum(kp, axis=1))[..., None]
        kptv = jnp.einsum('btn,btm->bnm', v, kp)
        y = jnp.einsum('btm,bnm->btn', qp, kptv) / (D + EPS_ATTN)
        y = v + (y @ proj_w + proj_b)
        h2 = layernorm(y, n2_g, n2_b)
        h2 = jax.nn.gelu(h2 @ mlp_w1 + mlp_b1, approximate=False)
        h2 = h2 @ mlp_w2 + mlp_b2
        return y + h2

    def _L3_ffn_ref(x, gw1, gb1, gw2, gb2, we1, be1, we2, be2):
        import jax, jax.numpy as jnp
        import numpy as np
        E = 8
        TOP_K = 2
        D = 512
        H = 1024
        B, S = (16, 512)
        b, s, d = x.shape
        xf = x.reshape(-1, d)
        T = xf.shape[0]
        gate_logits = jax.nn.relu(xf @ gw1 + gb1) @ gw2 + gb2
        gate_weights = jax.nn.softmax(gate_logits, axis=-1)
        top_w, top_idx = jax.lax.top_k(gate_weights, TOP_K)
        top_w = jax.nn.softmax(top_w, axis=-1)
        combine = jnp.zeros((T, E), dtype=xf.dtype)
        combine = combine.at[jnp.arange(T)[:, None], top_idx].add(top_w)
        out = jnp.zeros_like(xf)
        for e in range(E):
            h = jax.nn.gelu(xf @ we1[e] + be1[e], approximate=False)
            y = h @ we2[e] + be2[e]
            out = out + combine[:, e:e + 1] * y
        return out.reshape(b, s, d)
    edge_index = jnp.stack([src, dst])
    xn = _layernorm(x, axis=-1)
    x = x + _L0_gnn_ref(xn, src, dst, L0_gnn_W_self, L0_gnn_W_neigh, L0_gnn_b) + _L0_mix_ref(xn[None], L0_mix_Wq, L0_mix_Wkv)[0]
    x = x + _L0_ffn_ref(_layernorm(x, axis=-1)[None], L0_ffn_gate_w, L0_ffn_experts)[0]
    xn = _layernorm(x, axis=-1)
    x = x + _L1_gnn_ref(xn, edge_index, L1_gnn_W1, L1_gnn_b1, L1_gnn_W2, L1_gnn_b2) + _L1_mix_ref(xn[None], L1_mix_w_qkv, L1_mix_w_proj, L1_mix_b_proj)[0]
    x = x + _L1_ffn_ref(_layernorm(x, axis=-1)[None], L1_ffn_Wg, L1_ffn_bg, L1_ffn_W1, L1_ffn_b1, L1_ffn_W2, L1_ffn_b2, L1_ffn_Ws1, L1_ffn_bs1, L1_ffn_Ws2, L1_ffn_bs2)[0]
    xn = _layernorm(x, axis=-1)
    x = x + _L2_gnn_ref(xn, L2_gnn_W_self, L2_gnn_W_rel, L2_gnn_bias, edge_index, edge_type_8) + _L2_mix_ref(xn[None], L2_mix_qkv_w, L2_mix_qkv_b, L2_mix_out_w, L2_mix_out_b, L2_mix_ln_gamma, L2_mix_ln_beta)[0]
    x = x + _L2_ffn_ref(_layernorm(x, axis=-1)[None], L2_ffn_gfc1_w, L2_ffn_gfc1_b, L2_ffn_gfc2_w, L2_ffn_gfc2_b, L2_ffn_W1, L2_ffn_b1, L2_ffn_W2, L2_ffn_b2, L2_ffn_ln_g, L2_ffn_ln_b, L2_ffn_tv_W1, L2_ffn_tv_b1, L2_ffn_tv_W2, L2_ffn_tv_b2, L2_ffn_tv_ln_g, L2_ffn_tv_ln_b)[0]
    xn = _layernorm(x, axis=-1)
    x = x + _L3_gnn_ref(xn, edge_weight1, L3_gnn_W, L3_gnn_b, src, dst) + _L3_mix_ref(xn[None], L3_mix_kqv_w, L3_mix_kqv_b, L3_mix_proj_w, L3_mix_proj_b, L3_mix_n1_g, L3_mix_n1_b, L3_mix_n2_g, L3_mix_n2_b, L3_mix_mlp_w1, L3_mix_mlp_b1, L3_mix_mlp_w2, L3_mix_mlp_b2, L3_mix_w)[0]
    x = x + _L3_ffn_ref(_layernorm(x, axis=-1)[None], L3_ffn_gw1, L3_ffn_gb1, L3_ffn_gw2, L3_ffn_gb2, L3_ffn_we1, L3_ffn_be1, L3_ffn_we2, L3_ffn_be2)[0]
    return x

_drawn_inputs = setup_inputs


def setup_inputs(seed=0):
    import zlib

    import numpy as np

    out = dict(_drawn_inputs(seed))
    spreads = {'L1_gnn_b1': (0.0, 0.349),
     'L1_gnn_b2': (0.0, 0.1),
     'L1_mix_b_proj': (0.0, 0.1),
     'L1_ffn_bg': (0.0, 0.551),
     'L1_ffn_b1': (0.0, 0.617),
     'L1_ffn_b2': (0.0, 0.362),
     'L1_ffn_bs1': (0.0, 0.646),
     'L1_ffn_bs2': (0.0, 0.403),
     'L2_gnn_bias': (0.0, 0.283),
     'L2_mix_qkv_b': (0.0, 0.312),
     'L2_mix_out_b': (0.0, 0.291),
     'L2_mix_ln_gamma': (1.0, 0.2),
     'L2_mix_ln_beta': (0.0, 0.1),
     'L2_ffn_gfc1_b': (0.0, 0.8),
     'L2_ffn_gfc2_b': (0.20000000298023224, 0.6),
     'L2_ffn_b1': (0.0, 2.0),
     'L2_ffn_b2': (0.0, 2.0),
     'L2_ffn_ln_g': (1.0, 0.6),
     'L2_ffn_ln_b': (0.0, 0.421),
     'L3_mix_kqv_b': (0.0, 0.8),
     'L3_mix_proj_b': (0.0, 0.8),
     'L3_mix_n1_g': (1.0, 0.6),
     'L3_mix_n1_b': (0.0, 0.8),
     'L3_mix_n2_g': (1.0, 0.6),
     'L3_mix_n2_b': (0.0, 0.8),
     'L3_mix_mlp_b1': (0.0, 0.8),
     'L3_mix_mlp_b2': (0.0, 0.8),
     'L3_ffn_gb1': (0.0, 0.8),
     'L3_ffn_gb2': (0.0, 0.8),
     'L3_ffn_be1': (0.0, 0.8),
     'L3_ffn_be2': (0.0, 0.8)}
    factors = {'L0_mix_Wq': 5.883,
     'L2_ffn_gfc1_w': 8.0,
     'L2_ffn_gfc2_w': 8.0,
     'L2_ffn_W1': 3.697,
     'L2_ffn_tv_W1': 7.264,
     'L2_ffn_tv_b1': 26.469,
     'L2_ffn_tv_W2': 3.575,
     'L2_ffn_tv_b2': 49.295,
     'L2_ffn_tv_ln_g': 29.875,
     'L2_ffn_tv_ln_b': 57.92,
     'L3_gnn_b': 21.845,
     'L3_ffn_gw1': 8.0,
     'L3_ffn_gw2': 7.156,
     'L3_ffn_we1': 7.587,
     'L3_ffn_we2': 6.721}
    for name, (base, spread) in spreads.items():
        noise = np.random.default_rng([zlib.crc32(name.encode()), seed]).standard_normal(out[name].shape)
        drawn = base * np.exp(spread * noise) if base else spread * noise
        out[name] = jnp.asarray(drawn.astype(out[name].dtype))
    for name, factor in factors.items():
        out[name] = (out[name] * factor).astype(out[name].dtype)
    return out
```

```python
from contextlib import ExitStack

import concourse.bass as bass
from concourse import mybir

F32 = mybir.dt.float32
BF16 = mybir.dt.bfloat16
F16 = mybir.dt.float16
I32 = mybir.dt.int32
ALU = mybir.AluOpType
ACT = mybir.ActivationFunctionType
AX = mybir.AxisListType.X

N, D = 1250, 512
TP, NT = 125, 10
KD = D // 128
H, HD = 8, 64
NE = 8
E = 40000
EC = E // TP
GJ = 4
NG = (E + NT * (128 * GJ - 1)) // (128 * GJ)
NG += NG % 2
NC = NG * GJ
AW = 1260
CW = AW // 3
R = 8
F_DST, F_SRC, F_TYPE, F_W, F_RELSRC, F_DSTREL, F_SRCI = range(7)
CHUNKS = ((0, 417), (417, 417), (834, 416))
RING = 4
CAP = NE and N // NE

ROWS = ["L0_b0", "L0_b1", "L0_b2", "L1_gnn_b2", "L1_mix_b", "L1_bs2", "L2_bias", "L2_kb", "L2_vb", "L2_out_b",
        "L2_b2", "L2_ln_g", "L2_ln_b", "L3_gnn_b", "L3_kb", "L3_qb", "L3_vb", "L3_proj_b", "L3_mlp_b2"]
NR = len(ROWS)
COLS = {"L1_gnn_b1": 4, "L1_ffn_b1": 16, "L1_bs1": 2, "L2_qb": 4, "L2_g": 4, "L2_bt": 4, "L2_gfc1_b": 4, "L2_b1": 2,
        "L2_tv_b1": 16, "L3_n1_g": 4, "L3_n1_b": 4, "L3_n2_g": 4, "L3_n2_b": 4, "L3_mlp_b1": 4, "L3_gb1": 2,
        "L3_be1": 64}
COL0 = {}
for _n, _c in COLS.items():
    COL0[_n] = sum(COLS[m] for m in COL0)
NCOL = sum(COLS.values())
GATES = {"L0_gate": 4, "L1_Wg": 4, "L2_gfc2": 4, "L3_gw2": 2}
GATE0 = {}
for _n, _c in GATES.items():
    GATE0[_n] = sum(GATES[m] for m in GATE0)
NGATE = sum(GATES.values())


class Ring:

    def __init__(self, nc, ctx, loads):
        self.buf = ctx.enter_context(nc.sbuf_tensor("weight_ring", [128, RING, 4 * D], F32))
        self.loaded = [ctx.enter_context(nc.semaphore(f"weights_loaded{s}")) for s in range(RING)]
        self.freed = ctx.enter_context(nc.semaphore("weights_freed"))
        self.loads = loads
        self.issued = 0
        self.used = 0
        self.count = []
        per = [0] * RING
        for n, parts in enumerate(loads):
            per[n % RING] += 16 * len(parts)
            self.count.append(per[n % RING])

    def dma(self, sp, n, parts):
        for lo, hi, k, ap in parts:
            dst = self.buf[:, n % RING, lo:hi].rearrange("p (k n) -> p k n", k=k)
            sp.dma_start(dst, ap).then_inc(self.loaded[n % RING], 16)

    def issue(self, sp, upto):
        for n in range(self.issued, min(upto, len(self.loads))):
            if n >= RING:
                sp.wait_ge(self.freed, n - RING + 1)
            self.dma(sp, n, self.loads[n])
        self.issued = max(self.issued, min(upto, len(self.loads)))

    def wait(self, eng, n):
        eng.wait_ge(self.loaded[n % RING], self.count[n])

    def mat(self, n, lo=0, hi=4 * D, k=4):
        return self.buf[:, n % RING, lo:hi].rearrange("p (k n) -> p k n", k=k)


def build(nc, ins, out):
    with ExitStack() as ctx:
        names = {}

        def sbuf(c, name, shape, dt=F32):
            names[name] = names.get(name, 0) + 1
            if names[name] > 1:
                name = f"{name}_{names[name]}"
            return c.enter_context(nc.sbuf_tensor(name, shape, dt))

        def mats(t, order=None):
            w = t.shape[1] // D
            return [[(0, 4 * D, 4, t[:, m * D:(m + 1) * D].rearrange("(k p) n -> p k n", p=128))]
                    for m in (order or range(w))]

        def pairs(a, b):
            return [[(0, 2 * D, 4, a.rearrange("(k p) n -> p k n", p=128)),
                     (2 * D, 4 * D, 2, b.rearrange("(k p) n -> p k n", p=128))]]

        loads, first = [], {}

        def plan(name, items):
            first[name] = len(loads)
            loads.extend(items)

        I = ins
        plan("L0_q", mats(I["L0_mix_Wq"]))
        plan("L0_kv", mats(I["L0_mix_Wkv"]))
        for l in range(3):
            plan(f"L0_self{l}", mats(I["L0_gnn_W_self"][l]))
            plan(f"L0_neigh{l}", mats(I["L0_gnn_W_neigh"][l]))
        plan("L0_exp", [m for e in range(NE) for m in mats(I["L0_ffn_experts"][e])])
        plan("L1_W1", mats(I["L1_gnn_W1"]))
        plan("L1_W2", mats(I["L1_gnn_W2"]))
        plan("L1_qkv", mats(I["L1_mix_w_qkv"]))
        plan("L1_proj", mats(I["L1_mix_w_proj"]))
        plan("L1_exp", [m for e in range(NE) for m in pairs(I["L1_ffn_W1"][e], I["L1_ffn_W2"][e])])
        plan("L1_shared", pairs(I["L1_ffn_Ws1"], I["L1_ffn_Ws2"]))
        plan("L2_self", mats(I["L2_gnn_W_self"]))
        plan("L2_rel", [m for e in range(NE) for m in mats(I["L2_gnn_W_rel"][e])])
        plan("L2_qkv", mats(I["L2_mix_qkv_w"]))
        plan("L2_out", mats(I["L2_mix_out_w"]))
        plan("L2_gfc1", mats(I["L2_ffn_gfc1_w"]))
        plan("L2_base", pairs(I["L2_ffn_W1"], I["L2_ffn_W2"]))
        plan("L2_tv", [m for e in range(NE) for m in pairs(I["L2_ffn_tv_W1"][e], I["L2_ffn_tv_W2"][e])])
        plan("L3_gnn", mats(I["L3_gnn_W"]))
        plan("L3_kqv", mats(I["L3_mix_kqv_w"]))
        plan("L3_w", [[(0, 2 * D, 4, I["L3_mix_w"].rearrange("(k p) n -> p k n", p=128))]])
        plan("L3_proj", mats(I["L3_mix_proj_w"]))
        plan("L3_mlp1", mats(I["L3_mix_mlp_w1"]))
        plan("L3_mlp2", mats(I["L3_mix_mlp_w2"]))
        plan("L3_gw1", [[(0, 2 * D, 4, I["L3_ffn_gw1"].rearrange("(k p) n -> p k n", p=128))]])
        plan("L3_exp", [m for e in range(NE) for m in
                        mats(I["L3_ffn_we1"][e]) +
                        [[(0, 4 * D, 4, I["L3_ffn_we2"][e, h * D:(h + 1) * D, :].rearrange("(k p) n -> p k n", p=128))]
                         for h in range(2)]])

        x = sbuf(ctx, "x", [TP, NT, D])
        xn = sbuf(ctx, "xn", [TP, NT, D])
        xT = sbuf(ctx, "xT", [128, KD, N])
        ring = Ring(nc, ctx, loads)
        rows = sbuf(ctx, "rows", [NR, D])
        pick = sbuf(ctx, "pick", [NR, NR, TP])
        cols = sbuf(ctx, "cols", [128, NCOL])
        gatew = sbuf(ctx, "gatew", [128, NGATE, NE])
        gateb = sbuf(ctx, "gateb", [128, 3, NE])
        expert_b2 = sbuf(ctx, "expert_b2", [NE, 2, D])
        gfc2_col = sbuf(ctx, "gfc2_col", [NE, 1])
        ident = sbuf(ctx, "ident", [128, 128])
        ones = sbuf(ctx, "ones", [128, 128])
        below = sbuf(ctx, "below", [TP, TP])
        stats = sbuf(ctx, "stats", [TP, NT, 6])
        mv = sbuf(ctx, "mv", [TP, NT, 2])
        rstd = sbuf(ctx, "rstd", [TP, NT])
        rdeg = sbuf(ctx, "rdeg", [TP, NT])
        group_tile = sbuf(ctx, "group_tile", [1, NG], I32)
        iota_tile = sbuf(ctx, "iota_tile", [128, TP])
        ps = ctx.enter_context(nc.psum_tensor("ps", [128, 8, 512], F32))

        edge_table = nc.dram_tensor("edge_table", (128 * NC, R), F32, kind="Internal").ap()
        count_table = nc.dram_tensor("count_table", (N * NE, 1), F32, kind="Internal").ap()
        rel_table = nc.dram_tensor("rel_table", (NE * N, D), F32, kind="Internal").ap()
        xn_table = nc.dram_tensor("xn_table", (N, D), F32, kind="Internal").ap()

        class Stage:

            def __init__(self, *names):
                self.names = names

            def __enter__(self):
                self.c = ExitStack()
                sems = [self.c.enter_context(nc.semaphore(n)) for n in self.names]
                self.sems = sems
                self.b = nc.Block()
                block = self.b.__enter__()
                return (block, *sems)

            def __exit__(self, *a):
                self.b.__exit__(*a)
                if a[0] is None:
                    for s in self.sems:
                        nc.sync.sem_clear(s)
                    nc.all_engine_barrier(sem_only=True)
                return self.c.__exit__(*a)

        def chain(eng, sem, before=0):
            n = [0]

            def link(ins):
                n[0] += 1
                ins.then_inc(sem, 1)
                eng.wait_ge(sem, before + n[0])
            return link

        def tile_of(t):
            return slice(t * TP, (t + 1) * TP)

        def bank(b, p=TP, w=D):
            return ps[0:p, b, 0:w]

        def tok_product(pe, dst, srcT, t, w, k_blocks, row=None, start=True, stop=True):
            if row is not None:
                r = ROWS.index(row)
                pe.matmul(dst, pick[:, r, :], rows[:, :], start=start, stop=False)
                start = False
            for k in range(k_blocks):
                last = pe.matmul(dst, srcT[:, k, tile_of(t)], w[:, k, :],
                                 start=start and k == 0, stop=stop and k == k_blocks - 1)
            return last

        def feat_product(pe, dst, w, f, srcT, lo, n, k_blocks):
            for k in range(k_blocks):
                last = pe.matmul(dst, w[:, k, f * 128:(f + 1) * 128], srcT[:, k, lo:lo + n],
                                 start=k == 0, stop=k == k_blocks - 1)
            return last

        def gemm(units, products, evac, finish=None, evac_on="scalar", weights=None, frees=None, extra=None, nb=4):
            weights, frees = weights or {}, frees or {}
            total = sum(frees.values())
            with Stage("product_ready", "bank_drained", "evac_chain", "finish_chain", "finished") as (
                    block, product_ready, bank_drained, evac_chain, finish_chain, finished):
                @block.sync
                def _(sp):
                    ring.issue(sp, ring.used + total + RING)

                @block.tensor
                def _(pe):
                    for u in range(units):
                        for n in weights.get(u, ()):
                            ring.wait(pe, n)
                        if u >= nb:
                            pe.wait_ge(bank_drained, u - nb + 1)
                        products(pe, u, u % nb).then_inc(product_ready, 1)

                def drain(eng):
                    link = chain(eng, evac_chain)
                    for u in range(units):
                        eng.wait_ge(product_ready, u + 1)
                        if finish and u >= 4:
                            eng.wait_ge(finished, u - 3)
                        evac(eng, u, u % nb, link).then_inc(bank_drained, 1)
                        if frees.get(u):
                            eng.sem_inc(ring.freed, frees[u])

                def complete(eng):
                    link = chain(eng, finish_chain)
                    for u in range(units):
                        eng.wait_ge(bank_drained, u + 1)
                        finish(eng, u, link).then_inc(finished, 1)

                if evac_on == "scalar":
                    block.scalar(drain)
                    if finish:
                        block.vector(complete)
                else:
                    block.vector(drain)
                    if finish:
                        block.scalar(complete)
                if extra:
                    extra(block)
            ring.used += total

        def transposes(src, dstT, blocks, scale=None, bias=None):
            def products(pe, t, b):
                for k in range(blocks):
                    last = pe.transpose(ps[:, b, k * TP:(k + 1) * TP], src[:, t, k * 128:(k + 1) * 128], ident[0:TP, 0:TP])
                return last

            def evac(act, t, b, link):
                v = ps[:, b, 0:blocks * TP].rearrange("p (k n) -> p k n", k=blocks)
                if scale is None:
                    return act.activation(dstT[:, 0:blocks, tile_of(t)], v, ACT.Copy)
                for k in range(blocks):
                    last = act.activation(dstT[:, k, tile_of(t)], v[:, k, :], ACT.Identity,
                                          bias=cols[:, bias + k:bias + k + 1], scale=cols[:, scale + k:scale + k + 1])
                return last
            gemm(NT, products, evac)

        def layernorm(src, dst, eps):
            with Stage("stats_ready", "std_ready", "dve_chain") as (block, stats_ready, std_ready, dve_chain):
                @block.vector
                def _(dve):
                    link = chain(dve, dve_chain)
                    for t in range(NT):
                        last = dve.bn_stats(stats[:, t, :], src[:, t, :])
                    link(last)
                    for t in range(NT):
                        last = dve.bn_aggr(mv[:, t, :], stats[:, t, :])
                    link(last)
                    dve.tensor_scalar(rstd[:], mv[:, :, 1], eps, None, ALU.add).then_inc(stats_ready, 1)
                    dve.wait_ge(std_ready, 1)
                    link(dve.reciprocal(rstd[:], rstd[:]))
                    for t in range(NT):
                        last = dve.tensor_scalar(dst[:, t, :], src[:, t, :], mv[:, t, 0:1], rstd[:, t:t + 1],
                                                 ALU.subtract, ALU.mult)

                @block.scalar
                def _(act):
                    act.wait_ge(stats_ready, 1)
                    act.activation(rstd[:], rstd[:], ACT.Sqrt).then_inc(std_ready, 1)

                @block.sync
                def _(sp):
                    ring.issue(sp, ring.used + RING)

        def layernorm_T(src, dst, dstT, eps=1e-5, scale=None, bias=None):
            layernorm(src, dst, eps)
            transposes(dst, dstT, KD, scale, bias)

        def add_to_x(dve, t, b, link):
            return dve.tensor_tensor(x[:, t, :], bank(b), x[:, t, :], ALU.add)

        with Stage("consts_in", "pool_step", "x_in") as (block, consts_in, pool_step, x_in):
            @block.sync
            def _(sp):
                sp.dma_start(x[:], I["x"].rearrange("(t p) d -> p t d", p=TP)).then_inc(x_in, 16)
                sp.dma_start(rows[:], I["rows"]).then_inc(consts_in, 16)
                sp.dma_start(cols[:], I["cols"]).then_inc(consts_in, 16)
                sp.dma_start(gatew[:], I["gatew"]).then_inc(consts_in, 16)
                sp.dma_start(gateb[:], I["gateb"].rearrange("(o g) e -> o g e", o=1).to_broadcast([128, 3, NE])
                             ).then_inc(consts_in, 16)
                sp.dma_start(gfc2_col[:], I["gfc2_col"]).then_inc(consts_in, 16)
                sp.dma_start(expert_b2[:, 0, :], I["L1_ffn_b2"]).then_inc(consts_in, 16)
                sp.dma_start(expert_b2[:, 1, :], I["L3_ffn_be2"]).then_inc(consts_in, 16)
                ring.issue(sp, RING)
                sp.wait_ge(x_in, 16)
                sp.wait_ge(consts_in, 112)

            @block.gpsimd
            def _(pool):
                link = chain(pool, pool_step)
                link(pool.memset(ones[:], 1.0))
                pool.affine_select(out=ident[:], in_=ones[:], compare_op=ALU.is_equal, fill=0.0, base=0,
                                   pattern=[[-1, 128]], channel_multiplier=1)
                pool.affine_select(out=below[:], in_=ones[0:TP, 0:TP], compare_op=ALU.is_gt, fill=0.0, base=0,
                                   pattern=[[1, TP]], channel_multiplier=-1)
                link(pool.memset(pick[:], 1.0))
                link(pool.affine_select(out=pick[:], in_=pick[:], compare_op=ALU.is_equal, fill=0.0, base=0,
                                        pattern=[[-1, NR], [0, TP]], channel_multiplier=1))
                link(pool.iota(iota_tile[:], [[1, TP]], 0, 0, allow_small_or_imprecise_dtypes=True))

        c0 = ExitStack()
        records = sbuf(c0, "records", [TP, EC, R])
        slot = sbuf(c0, "slot", [TP, EC], I32)
        with ExitStack() as c:
            esrc = sbuf(c, "esrc", [TP, EC], I32)
            edst = sbuf(c, "edst", [TP, EC], I32)
            etype = sbuf(c, "etype", [TP, EC], I32)
            eweight = sbuf(c, "eweight", [TP, EC])
            dstf = sbuf(c, "dstf", [TP, EC])
            tile_f = sbuf(c, "tile_f", [TP, EC])
            one_row = sbuf(c, "one_row", [TP, EC])
            mask = sbuf(c, "mask", [TP, NT, EC])
            rank = sbuf(c, "rank", [TP, NT, EC])
            pos = sbuf(c, "pos", [TP, EC], I32)
            lane = sbuf(c, "lane", [TP, EC], I32)
            totals = sbuf(c, "totals", [TP, NT])
            ngroups_i = sbuf(c, "ngroups_i", [TP, NT], I32)
            ngroups = sbuf(c, "ngroups", [TP, NT])
            group_end = sbuf(c, "group_end", [TP, NT])
            offset = sbuf(c, "offset", [TP, NT])
            iota_g = sbuf(c, "iota_g", [1, NG])
            tile_acc = sbuf(c, "tile_acc", [1, NG])
            blank = sbuf(c, "blank", [128, NC, R])
            ri = records[:].bitcast(I32)
            with Stage("edges_in", "dve_chain", "pool_step", "totals_ready", "prefix_ready", "table_blank") as (
                    block, edges_in, dve_chain, pool_step, totals_ready, prefix_ready, table_blank):
                @block.sync
                def _(sp):
                    for dst, name in ((esrc, "src"), (edst, "dst"), (etype, "edge_type_8")):
                        sp.dma_start(dst[:], I[name].rearrange("(p c) -> p c", c=EC)).then_inc(edges_in, 16)
                    sp.dma_start(eweight[:], I["edge_weight1"].rearrange("(p c) o -> p (c o)", c=EC)).then_inc(edges_in, 16)
                    sp.wait_ge(pool_step, 2)
                    sp.dma_start(edge_table.rearrange("(p c) r -> p c r", c=NC), blank[:]).then_inc(table_blank, 16)
                    sp.wait_ge(table_blank, 16)

                @block.gpsimd
                def _(pool):
                    link = chain(pool, pool_step)
                    link(pool.memset(blank[:], 0.0))
                    link(pool.memset(blank[:, :, F_DST], -1.0))
                    link(pool.iota(iota_g[:], [[1, NG]], 0, 0, allow_small_or_imprecise_dtypes=True))

                @block.vector
                def _(dve):
                    link = chain(dve, dve_chain)
                    dve.memset(one_row[:], 1.0)
                    dve.memset(records[:], 0.0)
                    link(dve.memset(tile_acc[:], 0.0))
                    dve.wait_ge(edges_in, 64)
                    dve.tensor_copy(dstf[:], edst[:])
                    dve.tensor_copy(records[:, :, F_SRC], esrc[:])
                    dve.tensor_copy(ri[:, :, F_SRCI], esrc[:])
                    dve.tensor_copy(records[:, :, F_W], eweight[:])
                    link(dve.tensor_copy(records[:, :, F_TYPE], etype[:]))
                    dve.scalar_tensor_tensor(out=ri[:, :, F_RELSRC], in0=records[:, :, F_TYPE], scalar=float(N),
                                             in1=records[:, :, F_SRC], op0=ALU.mult, op1=ALU.add)
                    link(dve.scalar_tensor_tensor(out=ri[:, :, F_DSTREL], in0=dstf[:], scalar=float(NE),
                                                  in1=records[:, :, F_TYPE], op0=ALU.mult, op1=ALU.add))
                    link(dve.tensor_scalar(tile_f[:], dstf[:], float(TP), None, ALU.is_ge))
                    for b in range(2, NT):
                        link(dve.scalar_tensor_tensor(out=tile_f[:], in0=dstf[:], scalar=float(TP * b),
                                                      in1=tile_f[:], op0=ALU.is_ge, op1=ALU.add))
                    dve.scalar_tensor_tensor(out=records[:, :, F_DST], in0=tile_f[:], scalar=-float(TP),
                                             in1=dstf[:], op0=ALU.mult, op1=ALU.add)
                    for b in range(NT):
                        last = dve.tensor_scalar(mask[:, b, :], tile_f[:], float(b), None, ALU.is_equal)
                    link(last)
                    for b in range(NT):
                        last = dve.tensor_tensor_scan(out=rank[:, b, :], data0=one_row[:], data1=mask[:, b, :],
                                                      initial=0.0, op0=ALU.mult, op1=ALU.add)
                    link(last)
                    dve.tensor_copy(totals[:], rank[:, :, EC - 1]).then_inc(totals_ready, 1)
                    dve.wait_ge(prefix_ready, 1)
                    link(dve.tensor_scalar(ngroups_i[:], ps[0:TP, 1, 0:NT], float(128 * GJ - 1), None, ALU.add))
                    link(dve.tensor_scalar(ngroups_i[:], ngroups_i[:], 9, None, ALU.arith_shift_right))
                    link(dve.tensor_copy(ngroups[:], ngroups_i[:]))
                    link(dve.tensor_tensor_scan(out=group_end[:], data0=one_row[:, 0:NT], data1=ngroups[:],
                                                initial=0.0, op0=ALU.mult, op1=ALU.add))
                    link(dve.tensor_tensor(offset[:], group_end[:], ngroups[:], ALU.subtract))
                    link(dve.tensor_scalar(offset[:], offset[:], float(128 * GJ), -1.0, ALU.mult, ALU.add))
                    link(dve.tensor_tensor(offset[:], offset[:], ps[0:TP, 0, 0:NT], ALU.add))
                    for b in range(NT):
                        last = dve.scalar_tensor_tensor(out=rank[:, b, :], in0=rank[:, b, :], scalar=offset[:, b:b + 1],
                                                        in1=mask[:, b, :], op0=ALU.add, op1=ALU.mult)
                    link(last)
                    link(dve.tensor_reduce(dstf[:], rank[:].rearrange("p b c -> p c b"), AX.X, ALU.add))
                    link(dve.tensor_copy(pos[:], dstf[:]))
                    dve.tensor_scalar(lane[:], pos[:], 127, None, ALU.bitwise_and)
                    link(dve.tensor_scalar(pos[:], pos[:], 7, None, ALU.arith_shift_right))
                    dve.scalar_tensor_tensor(out=slot[:], in0=lane[:], scalar=float(NC), in1=pos[:],
                                             op0=ALU.mult, op1=ALU.add)
                    dve.wait_ge(pool_step, 3)
                    for b in range(NT - 1):
                        link(dve.scalar_tensor_tensor(out=tile_acc[:], in0=iota_g[:], scalar=group_end[0:1, b:b + 1],
                                                      in1=tile_acc[:], op0=ALU.is_ge, op1=ALU.add))
                    dve.tensor_copy(group_tile[:], tile_acc[:])

                @block.tensor
                def _(pe):
                    pe.wait_ge(totals_ready, 1)
                    pe.matmul(ps[0:TP, 0, 0:NT], below[:], totals[:], start=True, stop=True)
                    pe.matmul(ps[0:TP, 1, 0:NT], ones[0:TP, 0:TP], totals[:], start=True, stop=True).then_inc(prefix_ready, 1)

        layernorm_T(x, xn, xT)

        def elu1(dst, exp_buf, src_of, bias=None):
            def evac(act, u, b, link):
                d = dst(u)
                e = exp_buf[0:d.shape[0], u % 4, 0:d.shape[1]]
                plus = {} if bias is None else {"bias": bias(u)[0]}
                minus = {} if bias is None else {"bias": bias(u)[1]}
                link(act.activation(e, src_of(u, b), ACT.Relu, scale=-1.0, **minus))
                act.activation(e, e, ACT.Exp, scale=-1.0)
                return act.activation(d, src_of(u, b), ACT.Relu, **plus)

            def finish(dve, u, link):
                d = dst(u)
                return dve.tensor_tensor(d, exp_buf[0:d.shape[0], u % 4, 0:d.shape[1]], d, ALU.add)
            return evac, finish

        def feat_units(n_load, dstT, srcT, k_blocks):
            def products(pe, u, b):
                f, (lo, n) = u // 3, CHUNKS[u % 3]
                return feat_product(pe, ps[:, b, 0:n], ring.mat(n_load), f, srcT, lo, n, k_blocks)

            def dst(u):
                f, (lo, n) = u // 3, CHUNKS[u % 3]
                return dstT[:, f, lo:lo + n]

            def src_of(u, b):
                return ps[:, b, 0:CHUNKS[u % 3][1]]
            return products, dst, src_of

        VW = 129

        def kv_and_apply(c, qT, k, vo, eps, to=None, col_scale=None, den_ones=False):
            bd = sbuf(c, "kv_blocks", [128, 4, 130])
            den = sbuf(c, "att_den", [TP, 2, H])
            att = sbuf(c, "att", [TP, 2, D])
            with Stage("kv_ready", "blocks_zero", "blocks_ready", "product_ready", "drained", "dve_chain") as (
                    block, kv_ready, blocks_zero, blocks_ready, product_ready, drained, dve_chain):
                @block.gpsimd
                def _(pool):
                    pool.memset(bd[:], 0.0).then_inc(blocks_zero, 1)

                @block.tensor
                def _(pe):
                    for g in range(4):
                        for t in range(NT):
                            last = pe.matmul(ps[:, g, 0:VW], k[:, t, g * 128:(g + 1) * 128], vo[:, t, g, :],
                                             start=t == 0, stop=t == NT - 1)
                    last.then_inc(kv_ready, 1)
                    pe.wait_ge(blocks_ready, 1)
                    for t in range(NT):
                        if t >= 2:
                            pe.wait_ge(drained, t - 1)
                        for g in range(4):
                            last = pe.matmul(ps[0:TP, 4 + 2 * (t % 2) + g // 2, (g % 2) * 130:(g % 2) * 130 + 130],
                                             qT[:, g, tile_of(t)], bd[:, g, :], start=True, stop=True)
                        last.then_inc(product_ready, 1)

                @block.vector
                def _(dve):
                    link = chain(dve, dve_chain)
                    dve.wait_ge(blocks_zero, 1)
                    dve.wait_ge(kv_ready, 1)
                    for g in range(4):
                        for h in range(2):
                            pr = slice(64 * h, 64 * h + 64)
                            if col_scale is None:
                                dve.tensor_copy(bd[pr, g, 64 * h:64 * h + 64], ps[pr, g, 64 * h:64 * h + 64])
                            else:
                                dve.tensor_scalar(bd[pr, g, 64 * h:64 * h + 64], ps[pr, g, 64 * h:64 * h + 64],
                                                  col_scale[pr, g:g + 1], None, ALU.mult)
                            if den_ones:
                                last = dve.tensor_copy(bd[pr, g, 128 + h:129 + h], ones[pr, 0:1])
                            else:
                                last = dve.tensor_copy(bd[pr, g, 128 + h:129 + h], ps[pr, g, 128:129])
                    last.then_inc(blocks_ready, 1)
                    for t in range(NT):
                        dve.wait_ge(product_ready, t + 1)
                        v = ps[0:TP, 4 + 2 * (t % 2):6 + 2 * (t % 2), 0:260].rearrange("p b (g w) -> p b g w", g=2)
                        dn = den[:, t % 2, :].rearrange("p (b g h) -> p b g h", b=2, g=2)
                        link(dve.tensor_scalar(dn, v[:, :, :, 128:130], eps, None, ALU.add))
                        link(dve.reciprocal(den[:, t % 2, :], den[:, t % 2, :]))
                        for bb in range(2):
                            a = (att[:, t % 2] if to is None else to[:, t])[:, bb * 256:(bb + 1) * 256].rearrange("p (g h d) -> p g h d", g=2, h=2)
                            vv = v[:, bb, :, 0:128].rearrange("p g (h d) -> p g h d", h=2)
                            dd = dn[:, bb].rearrange("p g (h o) -> p g h o", o=1).to_broadcast([TP, 2, 2, 64])
                            last = dve.tensor_tensor(a, vv, dd, ALU.mult)
                        if to is None:
                            link(last)
                            last = dve.tensor_tensor(x[:, t, :], att[:, t % 2, :], x[:, t, :], ALU.add)
                        last.then_inc(drained, 1)

                @block.sync
                def _(sp):
                    ring.issue(sp, ring.used + RING)

        def scatter_edges(block, staged_done, pool_step, loop_turn):
            @block.gpsimd
            def _(pool):
                with pool.Fori(0, EC // 8) as i:
                    pool.tensor_copy(slot_stage[:], slot[:, bass.ds(8 * i, 8)])
                    pool.tensor_copy(record_stage[:], records[:, bass.ds(8 * i, 8), :]).then_inc(pool_step, 1)
                    pool.wait_ge(pool_step, i + 1)
                    pool.sem_inc(loop_turn, 1)
                    for j in range(8):
                        pool.indirect_dma_start(edge_table, bass.IndirectOffsetOnAxis(ap=slot_stage[:, j:j + 1], axis=0),
                                                record_stage[:, j, :], None).then_inc(staged_done, 16)
                    pool.wait_ge(staged_done, 128 * i + 128)
                    pool.sem_inc(loop_turn, 1)

        with ExitStack() as c:
            slot_stage = sbuf(c, "slot_stage", [TP, 8], I32)
            record_stage = sbuf(c, "record_stage", [TP, 8, R])
            records_out = ctx.enter_context(nc.semaphore("records_out"))
            with Stage("pool_step", "loop_turn") as (block, pool_step, loop_turn):
                scatter_edges(block, records_out, pool_step, loop_turn)
        c0.close()

        def elu_q(qT, ebuf, srcT, n, bias=None):
            pr, dst, src_of = feat_units(n, qT, srcT, KD)
            ev, fi = elu1(dst, ebuf, src_of, bias)
            gemm(12, pr, ev, fi, weights={0: [n]}, frees={11: 1})

        def elu_k(k, ebuf, srcT, n, row=None):
            ev, fi = elu1(lambda u: k[:, u, :], ebuf, lambda u, b: bank(b))
            gemm(NT, lambda pe, u, b: tok_product(pe, bank(b), srcT, u, ring.mat(n), KD, row), ev, fi,
                 weights={0: [n]}, frees={NT - 1: 1})

        def values(vo, srcT, n, row=None):
            def ones_column(block):
                @block.gpsimd
                def _(pool):
                    pool.memset(vo[:, :, :, 128:129], 1.0)
            gemm(NT, lambda pe, u, b: tok_product(pe, bank(b), srcT, u, ring.mat(n), KD, row),
                 lambda act, u, b, link: act.activation(vo[:, u, :, 0:128], bank(b).rearrange("p (g w) -> p g w", g=4),
                                                        ACT.Copy),
                 weights={0: [n]}, frees={NT - 1: 1}, extra=ones_column)

        def dense(srcT, n, dst, k_blocks=KD, row=None, add=None, scale=None):
            def evac(eng, u, b, link):
                if add is None:
                    return eng.activation(dst[:, u, :], bank(b), ACT.Copy)
                if scale is not None:
                    return eng.scalar_tensor_tensor(out=dst[:, u, :], in0=bank(b), scalar=scale, in1=add[:, u, :],
                                                    op0=ALU.mult, op1=ALU.add)
                return eng.tensor_tensor(dst[:, u, :], bank(b), add[:, u, :], ALU.add)
            w = ring.mat(n) if k_blocks == KD else ring.mat(n, 2 * D, 4 * D, 2)
            gemm(NT, lambda pe, u, b: tok_product(pe, bank(b), srcT, u, w, k_blocks, row), evac,
                 evac_on="scalar" if add is None else "vector", weights={0: [n]}, frees={NT - 1: 1})

        with ExitStack() as c:
            qT = sbuf(c, "qT", [128, KD, N])
            k = sbuf(c, "k", [TP, NT, D])
            vo = sbuf(c, "vo", [TP, NT, 4, VW])
            ebuf = sbuf(c, "ebuf", [128, 4, D])
            elu_q(qT, ebuf, xT, first["L0_q"])
            elu_k(k, ebuf, xT, first["L0_kv"])
            values(vo, xT, first["L0_kv"] + 1)
            kv_and_apply(c, qT, k, vo, 1e-6)

        with ExitStack() as c_adj:
            adj = sbuf(c_adj, "adj", [TP, NT, AW])
            with ExitStack() as c:
                edges = sbuf(c, "edges", [128, NC, R])
                iota_src = sbuf(c, "iota_src", [128, N], F16)
                dst_hot = sbuf(c, "dst_hot", [128, 2, GJ, TP], BF16)
                src_hot = sbuf(c, "src_hot", [128, 2, GJ, AW], BF16)
                with Stage("edges_in", "pool_step", "hot_ready", "sums_ready", "banks_free", "dve_chain") as (
                        block, edges_in, pool_step, hot_ready, sums_ready, banks_free, dve_chain):
                    @block.sync
                    def _(sp):
                        sp.dma_start(edges[:], edge_table.rearrange("(p c) r -> p c r", c=NC)).then_inc(edges_in, 16)

                    @block.gpsimd
                    def _(pool):
                        pool.iota(iota_src[:], [[1, N]], 0, 0, allow_small_or_imprecise_dtypes=True)
                        pool.memset(src_hot[:], 0.0)
                        pool.memset(adj[:], 0.0).then_inc(pool_step, 1)

                    @block.vector
                    def _(dve):
                        dve.wait_ge(edges_in, 16)
                        dve.wait_ge(pool_step, 1)
                        dve.sem_inc(banks_free, 2)
                        with dve.Fori(0, NG // 2) as i:
                            for s in range(2):
                                dve.wait_ge(sums_ready, 2 * i + s + 1)
                                ed = edges[:, bass.ds(GJ * (2 * i + s), GJ), :]
                                dve.tensor_tensor(
                                    dst_hot[:, s], iota_tile[:].rearrange("p (o n) -> p o n", o=1).to_broadcast([128, GJ, TP]),
                                    ed[:, :, F_DST:F_DST + 1].to_broadcast([128, GJ, TP]), ALU.is_equal)
                                dve.tensor_tensor(
                                    src_hot[:, s, :, N:N + NE],
                                    iota_tile[:, 0:NE].rearrange("p (o n) -> p o n", o=1).to_broadcast([128, GJ, NE]),
                                    ed[:, :, F_TYPE:F_TYPE + 1].to_broadcast([128, GJ, NE]), ALU.is_equal)
                                for j in range(GJ):
                                    last = dve.tensor_scalar(
                                        src_hot[:, s, j, 0:N], iota_src[:],
                                        edges[:, bass.ds(GJ * (2 * i + s) + j, 1), F_SRC:F_SRC + 1].rearrange("p a b -> p (a b)"),
                                        None, ALU.is_equal)
                                last.then_inc(hot_ready, 1)
                            for s in range(2):
                                dve.wait_ge(sums_ready, 2 * i + s + 3)
                                dve.wait_ge(banks_free, 2 * i + s + 2)
                                tile = dve.value_load(group_tile[0:1, bass.ds(2 * i + s, 1)], min_val=0, max_val=NT - 1)
                                a = adj[:, bass.ds(tile, 1), :].rearrange("p o (c w) -> p (o c) w", c=3)
                                dve.tensor_tensor(a, ps[0:TP, 3 * s:3 * s + 3, 0:CW], a, ALU.add).then_inc(banks_free, 1)

                    @block.tensor
                    def _(pe):
                        pe.sem_inc(sums_ready, 2)
                        with pe.Fori(0, NG // 2) as i:
                            for s in range(2):
                                pe.wait_ge(hot_ready, 2 * i + s + 1)
                                pe.wait_ge(banks_free, 2 * i + s + 1)
                                for w in range(3):
                                    for j in range(GJ):
                                        last = pe.matmul(ps[0:TP, 3 * s + w, 0:CW], dst_hot[:, s, j, :],
                                                         src_hot[:, s, j, w * CW:(w + 1) * CW],
                                                         start=j == 0, stop=j == GJ - 1)
                                last.then_inc(sums_ready, 1)

            counts = sbuf(c_adj, "counts", [TP, NT, NE])
            degree = sbuf(c_adj, "degree", [TP, NT])
            degree_all = sbuf(c_adj, "degree_all", [128, N])
            c_diag = ExitStack()
            degree_diag = sbuf(c_diag, "degree_diag", [TP, NT, TP])
            with Stage("dve_chain", "counts_ready", "counts_out", "diag_ready", "degree_ready") as (
                    block, dve_chain, counts_ready, counts_out, diag_ready, degree_ready):
                @block.vector
                def _(dve):
                    link = chain(dve, dve_chain)
                    dve.tensor_reduce(degree[:], adj[:, :, N:N + NE], AX.X, ALU.add)
                    link(dve.tensor_scalar(counts[:], adj[:, :, N:N + NE], 1.0, None, ALU.max))
                    dve.reciprocal(counts[:], counts[:]).then_inc(counts_ready, 1)
                    link(dve.tensor_scalar(degree[:], degree[:], 1.0, None, ALU.max))
                    link(dve.reciprocal(rdeg[:], degree[:]))
                    for t in range(NT):
                        last = dve.tensor_scalar(degree_diag[:, t, :], ident[0:TP, 0:TP], rdeg[:, t:t + 1], None, ALU.mult)
                    last.then_inc(diag_ready, 1)
                    dve.wait_ge(degree_ready, 1)
                    for t in range(NT):
                        dve.tensor_copy(degree_all[:, tile_of(t)], ps[:, t // 4, (t % 4) * TP:(t % 4 + 1) * TP])

                @block.tensor
                def _(pe):
                    pe.wait_ge(diag_ready, 1)
                    for t in range(NT):
                        last = pe.matmul(ps[:, t // 4, (t % 4) * TP:(t % 4 + 1) * TP], ones[0:TP, :], degree_diag[:, t, :],
                                         start=True, stop=True)
                    last.then_inc(degree_ready, 1)

                @block.sync
                def _(sp):
                    sp.wait_ge(counts_ready, 1)
                    sp.dma_start(count_table.rearrange("(t p r) o -> p t (r o)", p=TP, r=NE), counts[:]).then_inc(counts_out, 16)
                    sp.wait_ge(counts_out, 16)

            c_diag.close()
            swaps = [(i, j) for i in range(NT) for j in range(i, NT)]
            def swap_blocks(pe, u, b):
                i, j = swaps[u]
                last = pe.transpose(ps[0:TP, b, 0:TP], adj[:, i, tile_of(j)], ident[0:TP, 0:TP])
                if j > i:
                    last = pe.transpose(ps[0:TP, b, TP:2 * TP], adj[:, j, tile_of(i)], ident[0:TP, 0:TP])
                return last

            def put_blocks(act, u, b, link):
                i, j = swaps[u]
                last = act.activation(adj[:, j, tile_of(i)], ps[0:TP, b, 0:TP], ACT.Copy)
                if j > i:
                    last = act.activation(adj[:, i, tile_of(j)], ps[0:TP, b, TP:2 * TP], ACT.Copy)
                return last
            gemm(len(swaps), swap_blocks, put_blocks)

            def aggregate(src, dstT, other, op):
                def products(pe, u, b):
                    f, (lo, n) = u // 3, CHUNKS[u % 3]
                    for t in range(NT):
                        last = pe.matmul(ps[:, b, 0:n], src[:, t, f * 128:(f + 1) * 128], adj[:, t, lo:lo + n],
                                         start=t == 0, stop=t == NT - 1)
                    return last

                def evac(dve, u, b, link):
                    f, (lo, n) = u // 3, CHUNKS[u % 3]
                    return dve.tensor_tensor(dstT[:, f, lo:lo + n], ps[:, b, 0:n], other(f, lo, n), op)
                gemm(12, products, evac, evac_on="vector")

            with ExitStack() as c:
                aggT = sbuf(c, "aggT", [128, KD, N])
                squares = sbuf(c, "squares", [TP, 4, D])
                norm = sbuf(c, "norm", [TP, NT])
                for l in range(3):
                    ws, wn = first[f"L0_self{l}"], first[f"L0_neigh{l}"]
                    aggregate(xn, aggT, lambda f, lo, n: degree_all[:, lo:lo + n], ALU.mult)

                    def products(pe, t, b):
                        tok_product(pe, bank(b), xT, t, ring.mat(ws), KD, f"L0_b{l}", stop=False)
                        return tok_product(pe, bank(b), aggT, t, ring.mat(wn), KD, start=False)

                    gemm(NT, products, lambda act, t, b, link: act.activation(xn[:, t, :], bank(b), ACT.Relu),
                         lambda dve, t, link: dve.tensor_tensor_reduce(
                             out=squares[:, t % 4, :], in0=xn[:, t, :], in1=xn[:, t, :], scale=1.0, scalar=0.0,
                             op0=ALU.mult, op1=ALU.add, accum_out=norm[:, t:t + 1]),
                         weights={0: [ws, wn]}, frees={NT - 1: 2})
                    with Stage("root_ready", "dve_chain") as (block, root_ready, dve_chain):
                        @block.scalar
                        def _(act):
                            act.activation(norm[:], norm[:], ACT.Sqrt).then_inc(root_ready, 1)

                        @block.vector
                        def _(dve):
                            link = chain(dve, dve_chain)
                            dve.wait_ge(root_ready, 1)
                            link(dve.tensor_scalar(norm[:], norm[:], 1e-12, None, ALU.max))
                            link(dve.reciprocal(norm[:], norm[:]))
                            for t in range(NT):
                                if l < 2:
                                    dve.tensor_scalar(xn[:, t, :], xn[:, t, :], norm[:, t:t + 1], None, ALU.mult)
                                else:
                                    dve.scalar_tensor_tensor(out=x[:, t, :], in0=xn[:, t, :], scalar=norm[:, t:t + 1],
                                                             in1=x[:, t, :], op0=ALU.mult, op1=ALU.add)
                    if l < 2:
                        transposes(xn, xT, KD)

            layernorm_T(x, xn, xT)
            with ExitStack() as c:
                share = sbuf(c, "share", [TP, NT, NE])
                col_sum = sbuf(c, "col_sum", [TP, NE])
                row_sum = sbuf(c, "row_sum", [TP, NT])
                gT = sbuf(c, "gT", [NE, N])
                left = sbuf(c, "left", [NE, N])
                picked = sbuf(c, "picked", [NE, N])
                tied = sbuf(c, "tied", [NE, N])
                order = sbuf(c, "order", [NE, N])
                one_row = sbuf(c, "one_row8", [NE, N])
                top = sbuf(c, "top", [NE, 8])
                above = sbuf(c, "above", [NE, 1])
                n_picks = sbuf(c, "n_picks", [TP, NT])
                sel = sbuf(c, "sel", [TP, NT, 2, NE])
                wt = sbuf(c, "wt", [TP, NT, NE])
                g0 = GATE0["L0_gate"]
                gemm(NT, lambda pe, t, b: tok_product(pe, ps[0:TP, b, 0:NE], xT, t, gatew[:, g0:g0 + 4, :], KD),
                     lambda dve, t, b, link: dve.tensor_scalar(share[:, t, :], ps[0:TP, b, 0:NE], 1e-10, None, ALU.max),
                     evac_on="vector")
                with Stage("plan_ready", "sums_ready", "dve_chain") as (block, plan_ready, sums_ready, dve_chain):
                    @block.tensor
                    def _(pe):
                        with pe.Fori(0, 8) as i:
                            pe.wait_ge(plan_ready, i + 1)
                            pe.matmul(ps[0:TP, 0, 0:NT * NE], ones[0:TP, 0:TP], share[:].rearrange("p t e -> p (t e)"),
                                      start=True, stop=True).then_inc(sums_ready, 1)

                    @block.vector
                    def _(dve):
                        dve.sem_inc(plan_ready, 1)
                        with dve.Fori(0, 8) as i:
                            link = chain(dve, dve_chain, 5 * i)
                            dve.wait_ge(sums_ready, i + 1)
                            link(dve.tensor_reduce(col_sum[:], ps[0:TP, 0, 0:NT * NE].rearrange("p (t e) -> p e t", e=NE),
                                                   AX.X, ALU.add))
                            link(dve.reciprocal(col_sum[:], col_sum[:]))
                            link(dve.tensor_tensor(share[:], share[:], col_sum[:].rearrange("p (o e) -> p o e", o=1)
                                                   .to_broadcast([TP, NT, NE]), ALU.mult))
                            link(dve.tensor_reduce(row_sum[:], share[:], AX.X, ALU.add))
                            link(dve.reciprocal(row_sum[:], row_sum[:]))
                            dve.tensor_tensor(share[:], share[:], row_sum[:].rearrange("p (t o) -> p t o", o=1)
                                              .to_broadcast([TP, NT, NE]), ALU.mult).then_inc(plan_ready, 1)

                def plan_T(pe, t, b):
                    return pe.transpose(ps[0:NE, b, 0:TP], share[:, t, :], ident[0:TP, 0:TP])
                gemm(NT, plan_T, lambda act, t, b, link: act.activation(gT[:, tile_of(t)], ps[0:NE, b, 0:TP], ACT.Copy))
                with Stage("dve_chain",) as (block, dve_chain):
                    @block.vector
                    def _(dve):
                        link = chain(dve, dve_chain)
                        dve.memset(one_row[:], 1.0)
                        link(dve.tensor_copy(left[:], gT[:]))
                        for r in range((CAP - 1) // 8):
                            link(dve.max(top[:], left[:]))
                            link(dve.match_replace(left[:], top[:], left[:], -1e30))
                        link(dve.max(top[:], left[:]))
                        limit = top[:, (CAP - 1) % 8:(CAP - 1) % 8 + 1]
                        link(dve.tensor_scalar(picked[:], gT[:], limit, None, ALU.is_gt))
                        dve.tensor_reduce(above[:], picked[:], AX.X, ALU.add)
                        link(dve.tensor_scalar(tied[:], gT[:], limit, None, ALU.is_equal))
                        link(dve.tensor_scalar(above[:], above[:], -1.0, float(CAP), ALU.mult, ALU.add))
                        link(dve.tensor_tensor_scan(out=order[:], data0=one_row[:], data1=tied[:], initial=0.0,
                                                    op0=ALU.mult, op1=ALU.add))
                        link(dve.scalar_tensor_tensor(out=tied[:], in0=order[:], scalar=above[:, 0:1], in1=tied[:],
                                                      op0=ALU.is_le, op1=ALU.mult))
                        link(dve.tensor_tensor(picked[:], picked[:], tied[:], ALU.add))
                        dve.scalar_tensor_tensor(out=order[:], in0=gT[:], scalar=0.5, in1=picked[:],
                                                 op0=ALU.is_gt, op1=ALU.mult)

                def picks_back(pe, t, b):
                    pe.transpose(ps[0:TP, b, 0:NE], picked[:, tile_of(t)], ident[0:NE, 0:NE])
                    return pe.transpose(ps[0:TP, b, NE:2 * NE], order[:, tile_of(t)], ident[0:NE, 0:NE])
                gemm(NT, picks_back, lambda act, t, b, link: act.activation(
                    sel[:, t], ps[0:TP, b, 0:2 * NE].rearrange("p (a e) -> p a e", a=2), ACT.Copy))
                with Stage("dve_chain",) as (block, dve_chain):
                    @block.vector
                    def _(dve):
                        link = chain(dve, dve_chain)
                        link(dve.tensor_reduce(n_picks[:], sel[:, :, 0, :], AX.X, ALU.add))
                        link(dve.tensor_scalar(n_picks[:], n_picks[:], 1.0, None, ALU.add))
                        link(dve.reciprocal(n_picks[:], n_picks[:]))
                        dve.tensor_tensor(wt[:], sel[:, :, 1, :], n_picks[:].rearrange("p (t o) -> p t o", o=1)
                                          .to_broadcast([TP, NT, NE]), ALU.mult)

                def expert_products(n0, W, evac_on, evac, store=None, items=NE):
                    per = NT * RING
                    turns = items // RING
                    with Stage("product_ready", "banks_free", "stored0", "stored1", "stored2", "stored3") as (
                            block, product_ready, banks_free, *stored):
                        @block.sync
                        def _(sp):
                            ring.issue(sp, n0 + RING)
                            with sp.Fori(0, turns - 1) as i:
                                for j in range(RING):
                                    sp.wait_ge(ring.freed, n0 + 1 + j + RING * i)
                                    sp.dma_start(ring.mat(n0 + j), W[bass.ds(RING * i + RING + j, 1)].rearrange(
                                        "o (k p) n -> p (o k) n", p=128)).then_inc(ring.loaded[(n0 + j) % RING], 16)

                        @block.tensor
                        def _(pe):
                            with pe.Fori(0, turns) as i:
                                for j in range(RING):
                                    pe.wait_ge(ring.loaded[(n0 + j) % RING], ring.count[n0 + j] + 16 * i)
                                    for t in range(NT):
                                        u = NT * j + t
                                        pe.wait_ge(banks_free, per * i + u + 1)
                                        tok_product(pe, bank(u % 4), xT, t, ring.mat(n0 + j), KD).then_inc(product_ready, 1)

                        def drain(eng):
                            eng.sem_inc(banks_free, 4)
                            if store:
                                for q in stored:
                                    eng.sem_inc(q, 16)
                            with eng.Fori(0, turns) as i:
                                for j in range(RING):
                                    for t in range(NT):
                                        u = NT * j + t
                                        eng.wait_ge(product_ready, per * i + u + 1)
                                        evac(eng, t, u, RING * i + j, i, stored).then_inc(banks_free, 1)
                                        if store:
                                            store(eng, t, u, i, stored, banks_free)
                                    eng.sem_inc(ring.freed, 1)
                            if store:
                                for q in stored:
                                    eng.wait_ge(q, 16 * (NT * items // 4 + 1))
                        (block.vector if evac_on == "vector" else block.scalar)(drain)
                    ring.issued = n0 + items
                    ring.used = n0 + items

                def add_expert(dve, t, u, e, i, stored):
                    return dve.scalar_tensor_tensor(
                        out=x[:, t, :], in0=bank(u % 4), scalar=wt[:, t, bass.ds(e, 1)], in1=x[:, t, :],
                        op0=ALU.mult, op1=ALU.add)
                expert_products(first["L0_exp"], I["L0_ffn_experts"], "vector", add_expert)

            layernorm_T(x, xn, xT)
            with ExitStack() as c:
                sT = sbuf(c, "sT", [128, KD, N])
                hT = sbuf(c, "hT", [128, KD, N])
                aggregate(xn, sT, lambda f, lo, n: xT[:, f, lo:lo + n], ALU.add)
                n1 = first["L1_W1"]
                pr, dst, src_of = feat_units(n1, hT, sT, KD)
                cb = COL0["L1_gnn_b1"]
                gemm(12, pr, lambda act, u, b, link: act.activation(dst(u), src_of(u, b), ACT.Relu,
                                                                    bias=cols[:, cb + u // 3:cb + u // 3 + 1]),
                     weights={0: [n1]}, frees={11: 1})
                dense(hT, first["L1_W2"], x, row="L1_gnn_b2", add=x)

        with ExitStack() as c:
            qT = sbuf(c, "qT1", [128, KD, N])
            k = sbuf(c, "k1", [TP, NT, D])
            vo = sbuf(c, "vo1", [TP, NT, 4, VW])
            peak = sbuf(c, "peak", [128, KD])
            col_scale = sbuf(c, "col_scale", [128, KD])
            n0 = first["L1_qkv"]
            with ExitStack() as c2:
                q = sbuf(c2, "q1", [TP, NT, D])
                qmax = sbuf(c2, "qmax", [TP, NT, H])

                def q_minus_max(dve, t, b, link):
                    v = bank(b).rearrange("p (h d) -> p h d", h=H)
                    link(dve.tensor_reduce(qmax[:, t, :], v, AX.X, ALU.max))
                    return dve.tensor_tensor(q[:, t, :].rearrange("p (h d) -> p h d", h=H), v,
                                             qmax[:, t, :].rearrange("p (h o) -> p h o", o=1).to_broadcast([TP, H, HD]),
                                             ALU.subtract)
                gemm(NT, lambda pe, t, b: tok_product(pe, bank(b), xT, t, ring.mat(n0), KD), q_minus_max,
                     lambda act, t, link: act.activation(q[:, t, :], q[:, t, :], ACT.Exp),
                     evac_on="vector", weights={0: [n0]}, frees={NT - 1: 1})
                transposes(q, qT, KD)
            with ExitStack() as c2:
                kT = sbuf(c2, "kT1", [128, KD, N])
                ebuf = sbuf(c2, "ebuf1", [128, 4, D])
                pr, dst, src_of = feat_units(n0 + 1, kT, xT, KD)
                ev, fi = elu1(dst, ebuf, src_of)
                gemm(12, pr, ev, fi, weights={0: [n0 + 1]}, frees={11: 1})
                with Stage("peak_ready", "exp_ready", "dve_chain") as (block, peak_ready, exp_ready, dve_chain):
                    @block.vector
                    def _(dve):
                        link = chain(dve, dve_chain)
                        link(dve.tensor_reduce(peak[:], kT[:], AX.X, ALU.max))
                        dve.tensor_scalar(peak[:], peak[:], -1.0, None, ALU.mult).then_inc(peak_ready, 1)
                        dve.wait_ge(exp_ready, 1)
                        dve.reciprocal(col_scale[:], col_scale[:])

                    @block.scalar
                    def _(act):
                        act.wait_ge(peak_ready, 1)
                        for f in range(KD):
                            last = act.activation(kT[:, f, :], kT[:, f, :], ACT.Exp, bias=peak[:, f:f + 1],
                                                  accum_out=col_scale[:, f:f + 1])
                        last.then_inc(exp_ready, 1)

                def back(pe, t, b):
                    for f in range(KD):
                        last = pe.transpose(ps[0:TP, b, f * 128:(f + 1) * 128], kT[:, f, tile_of(t)], ident[:, :])
                    return last
                gemm(NT, back, lambda act, t, b, link: act.activation(k[:, t, :], bank(b), ACT.Copy))
            values(vo, xT, n0 + 2)
            kv_and_apply(c, qT, k, vo, 0.0, to=k, col_scale=col_scale, den_ones=True)
            transposes(k, qT, KD)
            dense(qT, first["L1_proj"], x, row="L1_mix_b", add=x)

        def top_two(c, gate, bias_row, srcT, blocks, comb, softmax_first):
            lg = sbuf(c, "logits", [TP, NT, NE])
            eq = sbuf(c, "tie", [TP, NT, NE])
            pre = sbuf(c, "ties_before", [TP, NT, NE])
            pk = sbuf(c, "picks", [TP, NT, 2, NE])
            m = sbuf(c, "top_values", [TP, 2, NT])
            w = sbuf(c, "pick_weights", [TP, 2, NT])
            g0 = GATE0[gate]
            gemm(NT, lambda pe, t, b: tok_product(pe, ps[0:TP, b, 0:NE], srcT, t, gatew[:, g0:g0 + blocks, :], blocks),
                 lambda dve, t, b, link: dve.tensor_tensor(lg[:, t, :], ps[0:TP, b, 0:NE], gateb[0:TP, bias_row, :], ALU.add),
                 evac_on="vector")

            def spread(v):
                return v.rearrange("p (t o) -> p t o", o=1).to_broadcast([TP, NT, NE])

            with Stage("dve_chain", "ready_for_exp", "exp_ready") as (block, dve_chain, ready_for_exp, exp_ready):
                @block.vector
                def _(dve):
                    link = chain(dve, dve_chain)
                    n_exp = 0
                    if softmax_first:
                        link(dve.tensor_reduce(m[:, 0, :], lg[:], AX.X, ALU.max))
                        dve.tensor_tensor(lg[:], lg[:], spread(m[:, 0, :]), ALU.subtract).then_inc(ready_for_exp, 1)
                        n_exp += 1
                        dve.wait_ge(exp_ready, n_exp)
                        link(dve.tensor_reduce(m[:, 0, :], lg[:], AX.X, ALU.add))
                        link(dve.reciprocal(m[:, 0, :], m[:, 0, :]))
                        link(dve.tensor_tensor(lg[:], lg[:], spread(m[:, 0, :]), ALU.mult))
                    for r in range(2):
                        link(dve.tensor_reduce(m[:, r, :], lg[:], AX.X, ALU.max))
                        dve.memset(pre[:], 0.0)
                        link(dve.tensor_tensor(eq[:], lg[:], spread(m[:, r, :]), ALU.is_equal))
                        for e in range(1, NE):
                            link(dve.tensor_tensor(pre[:, :, e], pre[:, :, e - 1], eq[:, :, e - 1], ALU.add))
                        link(dve.scalar_tensor_tensor(out=pk[:, :, r, :], in0=pre[:], scalar=0.0, in1=eq[:],
                                                      op0=ALU.is_equal, op1=ALU.mult))
                        if r == 0:
                            link(dve.scalar_tensor_tensor(out=lg[:], in0=pk[:, :, 0, :], scalar=-1e30, in1=lg[:],
                                                          op0=ALU.mult, op1=ALU.add))
                    dve.tensor_tensor(w[:, 1, :], m[:, 1, :], m[:, 0, :], ALU.subtract).then_inc(ready_for_exp, 1)
                    dve.wait_ge(exp_ready, n_exp + 1)
                    link(dve.tensor_scalar(w[:, 0, :], w[:, 1, :], 1.0, None, ALU.add))
                    link(dve.reciprocal(w[:, 0, :], w[:, 0, :]))
                    link(dve.tensor_tensor(w[:, 1, :], w[:, 1, :], w[:, 0, :], ALU.mult))
                    link(dve.tensor_tensor(comb[:], pk[:, :, 0, :], spread(w[:, 0, :]), ALU.mult))
                    link(dve.tensor_tensor(eq[:], pk[:, :, 1, :], spread(w[:, 1, :]), ALU.mult))
                    dve.tensor_tensor(comb[:], comb[:], eq[:], ALU.add)

                @block.scalar
                def _(act):
                    n_exp = 0
                    if softmax_first:
                        act.wait_ge(ready_for_exp, 1)
                        act.activation(lg[:], lg[:], ACT.Exp).then_inc(exp_ready, 1)
                        n_exp += 1
                    act.wait_ge(ready_for_exp, n_exp + 1)
                    act.activation(w[:, 1, :], w[:, 1, :], ACT.Exp).then_inc(exp_ready, 1)

        def add_expert_biases(c, comb, which):
            combT = sbuf(c, "combT", [NE, N])
            gemm(NT, lambda pe, t, b: pe.transpose(ps[0:NE, b, 0:TP], comb[:, t, :], ident[0:TP, 0:TP]),
                 lambda act, t, b, link: act.activation(combT[:, tile_of(t)], ps[0:NE, b, 0:TP], ACT.Copy))
            gemm(NT, lambda pe, t, b: pe.matmul(bank(b), combT[:, tile_of(t)], expert_b2[:, which, :], start=True, stop=True),
                 add_to_x, evac_on="vector")

        def experts(c, n0, comb, func, col, fb, per, first_of, second_of, reload):
            turn = 4 // per if per < 4 else 2
            turns = NE // turn
            hT = sbuf(c, "hidden", [128, 2, fb, N])
            units = 3 * fb
            n_parts = 2 if per == 1 else 1
            bias_now = sbuf(c, "bias_now", [128, turn, fb])
            with Stage("feat_ready", "feat_free", "out_ready", "out_free", "expert_begun", "bias_ready") as (
                    block, feat_ready, feat_free, out_ready, out_free, expert_begun, bias_ready):
                @block.sync
                def _(sp):
                    if per == 1:
                        ring.issue(sp, n0 + RING)
                        with sp.Fori(0, turns - 1) as i:
                            for s in range(turn):
                                sp.wait_ge(ring.freed, n0 + 1 + s + turn * i)
                                reload(sp, turn * i + turn + s, n0 + s)
                    else:
                        ring.issue(sp, n0 + 2 * per)
                        with sp.Fori(0, turns - 1) as i:
                            for s in range(turn):
                                for j in range(per):
                                    sp.wait_ge(ring.freed, n0 + per * s + j + 2 * per - RING + 1 + 2 * per * i)
                                    reload(sp, turn * i + turn + s, n0 + per * s + j, j)

                @block.tensor
                def _(pe):
                    pe.sem_inc(out_ready, 2 * NT)
                    with pe.Fori(0, turns) as i:
                        for s in range(turn):
                            n = n0 + per * s
                            for u in range(units):
                                f, (lo, w) = u // 3, CHUNKS[u % 3]
                                v = units * s + u
                                if u % (12 if per > 1 else units) == 0:
                                    m = n + f // 4 if per > 1 else n
                                    pe.wait_ge(ring.loaded[m % RING], ring.count[m] + 16 * n_parts * turn * per // RING * i)
                                pe.wait_ge(feat_free, units * turn * i + v + 1)
                                for k in range(KD):
                                    last = pe.matmul(ps[:, v % 4, 0:w], first_of(n, k, f), xT[:, k, lo:lo + w],
                                                     start=k == 0, stop=k == KD - 1)
                                last.then_inc(feat_ready, 1)
                            pe.wait_ge(feat_free, units * (turn * i + s) + units + 4)
                            for t in range(NT):
                                v = NT * s + t
                                if t == 0 and per > 1:
                                    for m in (n + 2, n + 3):
                                        pe.wait_ge(ring.loaded[m % RING], ring.count[m] + 16 * turn * per // RING * i)
                                pe.wait_ge(out_free, NT * turn * i + v + 1)
                                for k in range(fb):
                                    last = pe.matmul(bank(4 + v % 4), hT[:, s % 2, k, tile_of(t)], second_of(n, k),
                                                     start=k == 0, stop=k == fb - 1)
                                last.then_inc(out_ready, 1)

                @block.scalar
                def _(act):
                    act.sem_inc(feat_free, 4)
                    with act.Fori(0, turns) as i:
                        for s in range(turn):
                            act.wait_ge(out_ready, NT * (turn * i + s) + NT)
                            act.sem_inc(expert_begun, 1)
                            act.activation(bias_now[:, s, :], cols[:, bass.ds(fb * turn * i + (col + fb * s), fb)],
                                           ACT.Copy).then_inc(bias_ready, 1)
                            act.wait_ge(bias_ready, turn * i + s + 1)
                            for u in range(units):
                                f, (lo, w) = u // 3, CHUNKS[u % 3]
                                v = units * s + u
                                act.wait_ge(feat_ready, units * turn * i + v + 1)
                                act.activation(hT[:, s % 2, f, lo:lo + w], ps[:, v % 4, 0:w], func,
                                               bias=bias_now[:, s, f:f + 1]).then_inc(feat_free, 1)

                @block.vector
                def _(dve):
                    dve.sem_inc(out_free, 4)
                    with dve.Fori(0, turns) as i:
                        for s in range(turn):
                            for t in range(NT):
                                v = NT * s + t
                                dve.wait_ge(out_ready, NT * turn * i + v + 1 + 2 * NT)
                                dve.scalar_tensor_tensor(out=x[:, t, :], in0=bank(4 + v % 4),
                                                         scalar=comb[:, t, bass.ds(turn * i + s, 1)], in1=x[:, t, :],
                                                         op0=ALU.mult, op1=ALU.add).then_inc(out_free, 1)
                            dve.sem_inc(ring.freed, per)
            ring.issued = n0 + NE * per
            ring.used = n0 + NE * per

        layernorm_T(x, xn, xT)
        with ExitStack() as c:
            comb = sbuf(c, "comb1", [TP, NT, NE])
            top_two(c, "L1_Wg", 0, xT, 4, comb, False)
            add_expert_biases(c, comb, 0)

            def reload_pair(sp, e, n):
                for lo, hi, k, W in ((0, 2 * D, 4, I["L1_ffn_W1"]), (2 * D, 4 * D, 2, I["L1_ffn_W2"])):
                    sp.dma_start(ring.mat(n, lo, hi, k), W[bass.ds(e, 1)].rearrange("o (k p) n -> p (o k) n", p=128)
                                 ).then_inc(ring.loaded[n % RING], 16)
            experts(c, first["L1_exp"], comb, ACT.Relu, COL0["L1_ffn_b1"], 2, 1,
                    lambda n, k, f: ring.mat(n, 0, 2 * D)[:, k, f * 128:(f + 1) * 128],
                    lambda n, k: ring.mat(n, 2 * D, 4 * D, 2)[:, k, :], reload_pair)
        with ExitStack() as c:
            hT = sbuf(c, "shared_h", [128, 2, N])
            n = first["L1_shared"]
            cb = COL0["L1_bs1"]

            def shared_up(pe, u, b):
                f, (lo, w) = u // 3, CHUNKS[u % 3]
                return feat_product(pe, ps[:, b, 0:w], ring.mat(n, 0, 2 * D), f, xT, lo, w, KD)
            gemm(6, shared_up, lambda act, u, b, link: act.activation(
                hT[:, u // 3, CHUNKS[u % 3][0]:sum(CHUNKS[u % 3])], ps[:, b, 0:CHUNKS[u % 3][1]], ACT.Relu,
                bias=cols[:, cb + u // 3:cb + u // 3 + 1]), weights={0: [n]})
            dense(hT, n, x, k_blocks=2, row="L1_bs2", add=x, scale=0.5)

        def messages(table, word, dest, weight_word):
            with ExitStack() as c:
                edges = sbuf(c, "edges_m", [128, NC, R])
                index = sbuf(c, "index_stage", [128, 2, GJ, 2], I32)
                got = sbuf(c, "gathered", [128, 2, GJ, D])
                got_w = sbuf(c, "gathered_weight", [128, 2, GJ])
                hot = sbuf(c, "weighted_hot", [128, 2, GJ, TP])
                ei = edges[:].bitcast(I32)
                gather_w = weight_word is None
                layer = "L2" if gather_w else "L3"
                rows_in = [ctx.enter_context(nc.semaphore(f"{layer}_rows_in{s}")) for s in range(2)]
                weights_in = [ctx.enter_context(nc.semaphore(f"{layer}_weights_in{s}")) for s in range(2 * gather_w)]
                with Stage("edges_in", "index_ready", "loop_turn",
                           "hot_ready", "sums_ready", "banks_free", "dve_chain") as (
                        block, edges_in, index_ready, loop_turn, hot_ready, sums_ready,
                        banks_free, dve_chain):
                    @block.sync
                    def _(sp):
                        sp.dma_start(edges[:], edge_table.rearrange("(p c) r -> p c r", c=NC)).then_inc(edges_in, 16)
                        ring.issue(sp, ring.used + RING)

                    @block.gpsimd
                    def _(pool):
                        pool.wait_ge(edges_in, 16)
                        with pool.Fori(0, NG // 2) as i:
                            for s in range(2):
                                pool.wait_ge(sums_ready, 2 * i + s + 1)
                                pool.sem_inc(loop_turn, 1)
                                ed = ei[:, bass.ds(GJ * (2 * i + s), GJ), :]
                                pool.tensor_copy(index[:, s, :, 0:1], ed[:, :, word:word + 1])
                                pool.tensor_copy(index[:, s, :, 1:2], ed[:, :, F_DSTREL:F_DSTREL + 1]).then_inc(index_ready, 1)
                                pool.wait_ge(index_ready, 2 * i + s + 1)
                                pool.sem_inc(loop_turn, 1)
                                for j in range(GJ):
                                    if gather_w:
                                        pool.indirect_dma_start(
                                            got_w[:, s, j:j + 1], None, count_table,
                                            bass.IndirectOffsetOnAxis(ap=index[:, s, j, 1:2], axis=0)).then_inc(weights_in[s], 16)
                                    pool.indirect_dma_start(
                                        got[:, s, j, :], None, table,
                                        bass.IndirectOffsetOnAxis(ap=index[:, s, j, 0:1], axis=0)).then_inc(rows_in[s], 16)

                    @block.vector
                    def _(dve):
                        dve.wait_ge(edges_in, 16)
                        dve.sem_inc(banks_free, 2)
                        with dve.Fori(0, NG // 2) as i:
                            for s in range(2):
                                link = chain(dve, dve_chain, 2 * i + s)
                                dve.wait_ge(sums_ready, 2 * i + s + 1)
                                ed = edges[:, bass.ds(GJ * (2 * i + s), GJ), :]
                                link(dve.tensor_tensor(
                                    hot[:, s], iota_tile[:].rearrange("p (o n) -> p o n", o=1).to_broadcast([128, GJ, TP]),
                                    ed[:, :, F_DST:F_DST + 1].to_broadcast([128, GJ, TP]), ALU.is_equal))
                                if gather_w:
                                    dve.wait_ge(weights_in[s], 16 * GJ * i + 16 * GJ)
                                    w = got_w[:, s, :].rearrange("p (j o) -> p j o", o=1)
                                else:
                                    w = ed[:, :, weight_word:weight_word + 1]
                                dve.tensor_tensor(hot[:, s], hot[:, s], w.to_broadcast([128, GJ, TP]),
                                                  ALU.mult).then_inc(hot_ready, 1)
                            for s in range(2):
                                dve.wait_ge(sums_ready, 2 * i + s + 3)
                                dve.wait_ge(banks_free, 2 * i + s + 2)
                                tile = dve.value_load(group_tile[0:1, bass.ds(2 * i + s, 1)], min_val=0, max_val=NT - 1)
                                a = dest[:, bass.ds(tile, 1), :].rearrange("p o d -> p (o d)")
                                dve.tensor_tensor(a, bank(s), a, ALU.add).then_inc(banks_free, 1)

                    @block.tensor
                    def _(pe):
                        pe.sem_inc(sums_ready, 2)
                        with pe.Fori(0, NG // 2) as i:
                            for s in range(2):
                                pe.wait_ge(hot_ready, 2 * i + s + 1)
                                pe.wait_ge(banks_free, 2 * i + s + 1)
                                pe.wait_ge(rows_in[s], 16 * GJ * i + 16 * GJ)
                                for j in range(GJ):
                                    last = pe.matmul(bank(s), hot[:, s, j, :], got[:, s, j, :], start=j == 0, stop=j == GJ - 1)
                                last.then_inc(sums_ready, 1)

        layernorm_T(x, xn, xT)
        dense(xT, first["L2_self"], x, row="L2_bias", add=x)
        with ExitStack() as c:
            rel_out = sbuf(c, "rel_out", [TP, 4, D])

            def stage_rows(act, t, u, e, i, stored):
                act.wait_ge(stored[u % 4], 16 * (NT * RING // 4 * i + u // 4) + 16)
                return act.activation(rel_out[:, u % 4, :], bank(u % 4), ACT.Copy)

            def store_rows(act, t, u, i, stored, banks_free):
                act.wait_ge(banks_free, NT * RING * i + u + 5)
                act.dma_start(rel_table[bass.ds(N * RING * i + u * TP, TP), :], rel_out[:, u % 4, :]).then_inc(stored[u % 4], 16)
            expert_products(first["L2_rel"], I["L2_gnn_W_rel"], "scalar", stage_rows, store_rows)
        messages(rel_table, F_RELSRC, x, None)

        with ExitStack() as c:
            y = sbuf(c, "y", [TP, NT, D])
            yT = sbuf(c, "yT", [128, KD, N])
            layernorm_T(xn, y, yT, scale=COL0["L2_g"], bias=COL0["L2_bt"])
            qT = sbuf(c, "qT2", [128, KD, N])
            vo = sbuf(c, "vo2", [TP, NT, 4, VW])
            neg_qb = sbuf(c, "neg_qb", [128, KD])
            ebuf = sbuf(c, "ebuf2", [128, 4, D])
            cb = COL0["L2_qb"]
            with Stage("negated") as (block, negated):
                @block.vector
                def _(dve):
                    dve.tensor_scalar(neg_qb[:], cols[:, cb:cb + KD], -1.0, None, ALU.mult)
            n0 = first["L2_qkv"]
            elu_q(qT, ebuf, yT, n0, lambda u: (cols[:, cb + u // 3:cb + u // 3 + 1], neg_qb[:, u // 3:u // 3 + 1]))
            elu_k(y, ebuf, yT, n0 + 1, "L2_kb")
            values(vo, yT, n0 + 2, "L2_vb")
            kv_and_apply(c, qT, y, vo, 1e-8, to=y)
            transposes(y, yT, KD)
            dense(yT, first["L2_out"], x, row="L2_out_b", add=x)
            with Stage("added") as (block, added):
                @block.vector
                def _(dve):
                    for t in range(NT):
                        dve.tensor_tensor(x[:, t, :], x[:, t, :], xn[:, t, :], ALU.add)

        layernorm_T(x, xn, xT)
        with ExitStack() as c:
            gh = sbuf(c, "gh", [128, 12, CHUNKS[0][1]])
            gh_sums = sbuf(c, "gh_sums", [128, 12])
            gh_mean = sbuf(c, "gh_mean", [128, KD])
            gh_wide = sbuf(c, "gh_wide", [128, KD, 128])
            g_all = sbuf(c, "g_all", [128, NE])
            g_col = sbuf(c, "g_col", [NE, 1])
            g_wide = sbuf(c, "g_wide", [NE, TP])
            b1m = sbuf(c, "b1m", [128, 2])
            merged = sbuf(c, "merged", [128, 4 * D])
            tv_rows = sbuf(c, "tv_rows", [NE, 3, D])
            b2_all = sbuf(c, "b2_all", [TP, D])
            lng_all = sbuf(c, "lng_all", [TP, D])
            lnb_all = sbuf(c, "lnb_all", [TP, D])
            hT = sbuf(c, "h2T", [128, 2, N])
            res = sbuf(c, "res", [TP, NT, D])
            n0 = first["L2_gfc1"]
            cb = COL0["L2_gfc1_b"]
            pr, _dst, src_of = feat_units(n0, None, xT, KD)
            gemm(12, pr, lambda act, u, b, link: act.activation(
                gh[:, u, 0:CHUNKS[u % 3][1]], src_of(u, b), ACT.Relu, bias=cols[:, cb + u // 3:cb + u // 3 + 1],
                accum_out=gh_sums[:, u:u + 1]),
                weights={0: [n0]}, frees={11: 1})
            nb, nt = first["L2_base"], first["L2_tv"]
            with Stage("tv_in", "mean_ready", "gate_ready", "wide_ready", "rows_ready", "dve_chain") as (
                    block, tv_in, mean_ready, gate_ready, wide_ready, rows_ready, dve_chain):
                g0 = GATE0["L2_gfc2"]

                @block.sync
                def _(sp):
                    for r, nme in enumerate(("L2_ffn_tv_b2", "L2_ffn_tv_ln_g", "L2_ffn_tv_ln_b")):
                        sp.dma_start(tv_rows[:, r, :], I[nme]).then_inc(tv_in, 16)
                    ring.issue(sp, nb + 1 + NE + RING - 1)

                @block.vector
                def _(dve):
                    link = chain(dve, dve_chain)
                    link(dve.tensor_reduce(gh_mean[:], gh_sums[:].rearrange("p (f c) -> p f c", c=3), AX.X, ALU.add))
                    link(dve.tensor_scalar(gh_mean[:], gh_mean[:], 1.0 / N, None, ALU.mult))
                    for k in range(KD):
                        last = dve.tensor_scalar(gh_wide[:, k, :], ones[:, :], gh_mean[:, k:k + 1], None, ALU.mult)
                    last.then_inc(mean_ready, 1)
                    dve.wait_ge(gate_ready, 1)
                    link(dve.tensor_tensor(g_all[:], ps[:, 0, 0:NE], gateb[:, 2, :], ALU.add))
                    link(dve.tensor_tensor(g_col[:], ps[0:NE, 1, 0:1], gfc2_col[:], ALU.add))
                    dve.tensor_scalar(g_wide[:], ones[0:NE, 0:TP], g_col[:, 0:1], None, ALU.mult).then_inc(wide_ready, 1)
                    link(dve.tensor_copy(b1m[:], cols[:, COL0["L2_b1"]:COL0["L2_b1"] + 2]))
                    for e in range(NE):
                        cc = COL0["L2_tv_b1"] + 2 * e
                        link(dve.scalar_tensor_tensor(out=b1m[:], in0=cols[:, cc:cc + 2], scalar=g_all[:, e:e + 1],
                                                      in1=b1m[:], op0=ALU.mult, op1=ALU.add))
                    ring.wait(dve, nb)
                    link(dve.tensor_copy(merged[:], ring.buf[:, nb % RING, :]))
                    dve.sem_inc(ring.freed, 1)
                    for e in range(NE):
                        ring.wait(dve, nt + e)
                        link(dve.scalar_tensor_tensor(out=merged[:], in0=ring.buf[:, (nt + e) % RING, :],
                                                      scalar=g_all[:, e:e + 1], in1=merged[:], op0=ALU.mult, op1=ALU.add))
                        dve.sem_inc(ring.freed, 1)
                    dve.wait_ge(rows_ready, 1)
                    dve.tensor_copy(b2_all[:], bank(2))
                    for dst, a, b in ((lng_all, 3, 4), (lnb_all, 5, 6)):
                        link(dve.tensor_scalar(dst[:], bank(b), 0.03, None, ALU.mult))
                        dve.scalar_tensor_tensor(out=dst[:], in0=bank(a), scalar=1.0 - 0.03 * NE, in1=dst[:],
                                                 op0=ALU.mult, op1=ALU.add)

                @block.tensor
                def _(pe):
                    pe.wait_ge(mean_ready, 1)
                    for k in range(KD):
                        pe.matmul(ps[:, 0, 0:NE], gh_wide[:, k, :], gatew[:, g0 + k, :], start=k == 0, stop=k == KD - 1)
                    for k in range(KD):
                        last = pe.matmul(ps[0:NE, 1, 0:1], gatew[:, g0 + k, :], gh_mean[:, k:k + 1], start=k == 0, stop=k == KD - 1)
                    last.then_inc(gate_ready, 1)
                    pe.wait_ge(wide_ready, 1)
                    pe.wait_ge(tv_in, 48)
                    pe.matmul(bank(2), g_wide[:, :], tv_rows[:, 0, :], start=True, stop=False)
                    pe.matmul(bank(2), pick[:, ROWS.index("L2_b2"), :], rows[:, :], start=False, stop=True)
                    pe.matmul(bank(3), pick[:, ROWS.index("L2_ln_g"), :], rows[:, :], start=True, stop=True)
                    pe.matmul(bank(4), ones[0:NE, 0:TP], tv_rows[:, 1, :], start=True, stop=True)
                    pe.matmul(bank(5), pick[:, ROWS.index("L2_ln_b"), :], rows[:, :], start=True, stop=True)
                    pe.matmul(bank(6), ones[0:NE, 0:TP], tv_rows[:, 2, :], start=True, stop=True).then_inc(rows_ready, 1)
            ring.used += 1 + NE
            w1 = merged[:, 0:2 * D].rearrange("p (k n) -> p k n", k=4)
            w2 = merged[:, 2 * D:4 * D].rearrange("p (k n) -> p k n", k=2)

            def up(pe, u, b):
                f, (lo, w) = u // 3, CHUNKS[u % 3]
                return feat_product(pe, ps[:, b, 0:w], w1, f, xT, lo, w, KD)
            gemm(6, up, lambda act, u, b, link: act.activation(
                hT[:, u // 3, CHUNKS[u % 3][0]:sum(CHUNKS[u % 3])], ps[:, b, 0:CHUNKS[u % 3][1]], ACT.Relu,
                bias=b1m[:, u // 3:u // 3 + 1]))

            def residual(dve, t, b, link):
                link(dve.tensor_tensor(res[:, t, :], bank(b), xn[:, t, :], ALU.add))
                return dve.tensor_tensor(res[:, t, :], res[:, t, :], b2_all[:], ALU.add)
            gemm(NT, lambda pe, t, b: tok_product(pe, bank(b), hT, t, w2, 2), residual, evac_on="vector")
            layernorm(res, res, 1e-5)
            with Stage("dve_chain") as (block, dve_chain):
                @block.vector
                def _(dve):
                    link = chain(dve, dve_chain)
                    for t in range(NT):
                        last = dve.tensor_tensor(res[:, t, :], res[:, t, :], lng_all[:], ALU.mult)
                    link(last)
                    for t in range(NT):
                        last = dve.tensor_tensor(res[:, t, :], res[:, t, :], lnb_all[:], ALU.add)
                    link(last)
                    for t in range(NT):
                        dve.tensor_tensor(x[:, t, :], x[:, t, :], res[:, t, :], ALU.add)

        layernorm(x, xn, 1e-5)
        with ExitStack() as c:
            agg = sbuf(c, "agg", [TP, NT, D])
            aggT = sbuf(c, "agg3T", [128, KD, N])
            with Stage("table_out") as (block, table_out):
                @block.sync
                def _(sp):
                    sp.dma_start(xn_table.rearrange("(t p) d -> p t d", p=TP), xn[:]).then_inc(table_out, 16)
                    sp.wait_ge(table_out, 16)

                @block.gpsimd
                def _(pool):
                    pool.memset(agg[:], 0.0)
            messages(xn_table, F_SRCI, agg, F_W)
            transposes(agg, aggT, KD)
            dense(aggT, first["L3_gnn"], x, row="L3_gnn_b", add=x)

        M = 256
        with ExitStack() as c:
            v = sbuf(c, "v3", [TP, NT, D])
            y = sbuf(c, "y3", [TP, NT, D])
            yT = xT
            kp = sbuf(c, "kp", [TP, NT, M])
            qpT = sbuf(c, "qpT", [128, 2, N])
            hT = sbuf(c, "h3T", [128, KD, N])
            sq = sbuf(c, "sq", [TP, NT])
            sq_out = sbuf(c, "sq_out", [TP, D])
            kv = sbuf(c, "kv3", [128, 2, D])
            ksum = sbuf(c, "ksum", [128, 2])
            den = sbuf(c, "den3", [TP, NT])
            layernorm(xn, y, 1e-3)
            transposes(y, hT, KD, COL0["L3_n1_g"], COL0["L3_n1_b"])
            n0, nw = first["L3_kqv"], first["L3_w"]

            q3 = xn
            sqq = sbuf(c, "sqq", [TP, NT])

            def with_square(dst, acc):
                def evac(act, t, b, link):
                    link(act.activation(dst[:, t, :], bank(b), ACT.Copy))
                    return act.activation(sq_out[:], dst[:, t, :], ACT.Square, accum_out=acc[:, t:t + 1])
                return evac
            for j, (dst, acc, row) in enumerate(((y, sq, "L3_kb"), (q3, sqq, "L3_qb"))):
                gemm(NT, lambda pe, t, b, j=j, row=row: tok_product(pe, bank(b), hT, t, ring.mat(n0 + j), KD, row),
                     with_square(dst, acc), weights={0: [n0 + j]}, frees={NT - 1: 1})
            dense(hT, n0 + 2, v, row="L3_vb")
            with Stage("halved") as (block, halved):
                @block.vector
                def _(dve):
                    dve.tensor_scalar(sq[:], sq[:], -0.5, None, ALU.mult)
                    dve.tensor_scalar(sqq[:], sqq[:], -0.5, None, ALU.mult)

            def random_features(src, acc, dst, free):
                transposes(src, yT, KD)
                w = ring.mat(nw, 0, 2 * D)
                gemm(NT, lambda pe, t, b: tok_product(pe, ps[0:TP, b, 0:M], yT, t, w, KD),
                     lambda act, t, b, link: act.activation(dst[:, t, :], ps[0:TP, b, 0:M], ACT.Exp, bias=acc[:, t:t + 1]),
                     weights={0: [nw]}, frees={NT - 1: 1} if free else None)
            random_features(y, sq, kp, False)
            qp = y[:].rearrange("p t d -> p (t d)")[:, 0:NT * M].rearrange("p (t m) -> p t m", m=M)
            random_features(q3, sqq, qp, True)
            transposes(qp, qpT, 2)
            with Stage("kv_ready", "kv_in", "den_ready", "product_ready", "drained", "dve_chain") as (
                    block, kv_ready, kv_in, den_ready, product_ready, drained, dve_chain):
                @block.tensor
                def _(pe):
                    for m in range(2):
                        for t in range(NT):
                            pe.matmul(ps[:, m, 0:D], kp[:, t, m * 128:(m + 1) * 128], v[:, t, :], start=t == 0, stop=t == NT - 1)
                        for t in range(NT):
                            last = pe.matmul(ps[:, 2 + m, 0:1], kp[:, t, m * 128:(m + 1) * 128], ones[0:TP, 0:1],
                                             start=t == 0, stop=t == NT - 1)
                    last.then_inc(kv_ready, 1)
                    pe.wait_ge(kv_in, 1)
                    for t in range(NT):
                        for m in range(2):
                            last = pe.matmul(ps[0:TP, 4, t:t + 1], qpT[:, m, tile_of(t)], ksum[:, m:m + 1],
                                             start=m == 0, stop=m == 1)
                    last.then_inc(den_ready, 1)
                    for t in range(NT):
                        if t >= 3:
                            pe.wait_ge(drained, t - 2)
                        for m in range(2):
                            last = pe.matmul(bank(5 + t % 3), qpT[:, m, tile_of(t)], kv[:, m, :], start=m == 0, stop=m == 1)
                        last.then_inc(product_ready, 1)

                @block.vector
                def _(dve):
                    link = chain(dve, dve_chain)
                    dve.wait_ge(kv_ready, 1)
                    dve.tensor_copy(kv[:], ps[:, 0:2, :])
                    dve.tensor_copy(ksum[:], ps[:, 2:4, 0]).then_inc(kv_in, 1)
                    dve.wait_ge(den_ready, 1)
                    link(dve.tensor_scalar(den[:], ps[0:TP, 4, 0:NT], 1.0 / M, 1e-8, ALU.mult, ALU.add))
                    link(dve.reciprocal(den[:], den[:]))
                    for t in range(NT):
                        dve.wait_ge(product_ready, t + 1)
                        dve.tensor_scalar(q3[:, t, :], bank(5 + t % 3), 1.0 / M, den[:, t:t + 1], ALU.mult,
                                          ALU.mult).then_inc(drained, 1)
            transposes(q3, yT, KD)
            dense(yT, first["L3_proj"], y, row="L3_proj_b", add=v)
            layernorm(y, v, 1e-3)
            transposes(v, yT, KD, COL0["L3_n2_g"], COL0["L3_n2_b"])
            pr, dst, src_of = feat_units(first["L3_mlp1"], hT, yT, KD)
            cb = COL0["L3_mlp_b1"]
            gemm(12, pr, lambda act, u, b, link: act.activation(dst(u), src_of(u, b), ACT.Gelu,
                                                                bias=cols[:, cb + u // 3:cb + u // 3 + 1]),
                 weights={0: [first["L3_mlp1"]]}, frees={11: 1})
            dense(hT, first["L3_mlp2"], y, row="L3_mlp_b2", add=y)
            with Stage("added") as (block, added):
                @block.vector
                def _(dve):
                    for t in range(NT):
                        dve.tensor_tensor(x[:, t, :], x[:, t, :], y[:, t, :], ALU.add)

        layernorm_T(x, xn, xT)
        with ExitStack() as c:
            comb = sbuf(c, "comb3", [TP, NT, NE])
            with ExitStack() as c2:
                gT = sbuf(c2, "gate_hT", [128, 2, N])
                n = first["L3_gw1"]
                cb = COL0["L3_gb1"]

                def gate_up(pe, u, b):
                    f, (lo, w) = u // 3, CHUNKS[u % 3]
                    return feat_product(pe, ps[:, b, 0:w], ring.mat(n, 0, 2 * D), f, xT, lo, w, KD)
                gemm(6, gate_up, lambda act, u, b, link: act.activation(
                    gT[:, u // 3, CHUNKS[u % 3][0]:sum(CHUNKS[u % 3])], ps[:, b, 0:CHUNKS[u % 3][1]], ACT.Relu,
                    bias=cols[:, cb + u // 3:cb + u // 3 + 1]), weights={0: [n]}, frees={5: 1})
                top_two(c2, "L3_gw2", 1, gT, 2, comb, True)
                add_expert_biases(c2, comb, 1)
            def reload_quarter(sp, e, n, j):
                if j < 2:
                    src = I["L3_ffn_we1"][bass.ds(e, 1), :, j * D:(j + 1) * D]
                else:
                    src = I["L3_ffn_we2"][bass.ds(e, 1), (j - 2) * D:(j - 1) * D, :]
                sp.dma_start(ring.mat(n), src.rearrange("o (k p) n -> p (o k) n", p=128)).then_inc(ring.loaded[n % RING], 16)
            experts(c, first["L3_exp"], comb, ACT.Gelu, COL0["L3_be1"], 8, 4,
                    lambda n, k, f: ring.mat(n + f // 4)[:, k, (f % 4) * 128:(f % 4 + 1) * 128],
                    lambda n, k: ring.mat(n + 2 + k // 4)[:, k % 4, :], reload_quarter)

        def store_x():
            with Stage("x_out",) as (block, x_out):
                @block.sync
                def _(sp):
                    sp.dma_start(out.rearrange("(t p) d -> p t d", p=TP), x[:]).then_inc(x_out, 16)
                    sp.wait_ge(x_out, 16)
        store_x()


def kernel(**inputs):
    import numpy as np
    import concourse.bacc as bacc
    from concourse import mybir as mb
    from concourse.bass_utils import run_bass_kernel_spmd as run

    a = {n: np.asarray(v) for n, v in inputs.items()}
    given = {n: a[n] for n in ("x", "src", "dst", "edge_type_8", "edge_weight1",
                               "L0_gnn_W_self", "L0_gnn_W_neigh", "L0_ffn_experts", "L1_gnn_W1", "L1_gnn_W2",
                               "L1_mix_w_qkv", "L1_mix_w_proj", "L1_ffn_W1", "L1_ffn_W2", "L1_ffn_Ws1", "L1_ffn_Ws2",
                               "L1_ffn_b2", "L2_ffn_tv_b2", "L2_ffn_tv_ln_g", "L2_ffn_tv_ln_b",
                               "L3_mix_kqv_w", "L3_mix_proj_w", "L3_mix_mlp_w1", "L3_mix_mlp_w2",
                               "L3_ffn_gw1", "L3_ffn_we1", "L3_ffn_we2", "L3_ffn_be2")}
    for n in ("L0_mix_Wq", "L0_mix_Wkv", "L2_gnn_W_self", "L2_mix_qkv_w", "L2_mix_out_w", "L2_ffn_gfc1_w",
              "L2_ffn_W1", "L2_ffn_W2", "L3_gnn_W", "L3_mix_w"):
        given[n] = a[n].T
    for n in ("L2_gnn_W_rel", "L2_ffn_tv_W1", "L2_ffn_tv_W2"):
        given[n] = a[n].transpose(0, 2, 1)
    qb, kb = a["L2_mix_qkv_b"], a["L3_mix_kqv_b"]
    row = {"L0_b0": a["L0_gnn_b"][0], "L0_b1": a["L0_gnn_b"][1], "L0_b2": a["L0_gnn_b"][2],
           "L1_gnn_b2": a["L1_gnn_b2"], "L1_mix_b": a["L1_mix_b_proj"], "L1_bs2": a["L1_ffn_bs2"],
           "L2_bias": a["L2_gnn_bias"], "L2_kb": qb[D:2 * D], "L2_vb": qb[2 * D:], "L2_out_b": a["L2_mix_out_b"],
           "L2_b2": a["L2_ffn_b2"], "L2_ln_g": a["L2_ffn_ln_g"], "L2_ln_b": a["L2_ffn_ln_b"],
           "L3_gnn_b": a["L3_gnn_b"], "L3_kb": kb[0:D], "L3_qb": kb[D:2 * D], "L3_vb": kb[2 * D:],
           "L3_proj_b": a["L3_mix_proj_b"], "L3_mlp_b2": a["L3_mix_mlp_b2"]}
    given["rows"] = np.stack([row[n] for n in ROWS])
    col = {"L1_gnn_b1": a["L1_gnn_b1"], "L1_ffn_b1": a["L1_ffn_b1"].reshape(-1), "L1_bs1": a["L1_ffn_bs1"],
           "L2_qb": qb[0:D], "L2_g": a["L2_mix_ln_gamma"], "L2_bt": a["L2_mix_ln_beta"],
           "L2_gfc1_b": a["L2_ffn_gfc1_b"], "L2_b1": a["L2_ffn_b1"], "L2_tv_b1": a["L2_ffn_tv_b1"].reshape(-1),
           "L3_n1_g": a["L3_mix_n1_g"], "L3_n1_b": a["L3_mix_n1_b"], "L3_n2_g": a["L3_mix_n2_g"],
           "L3_n2_b": a["L3_mix_n2_b"], "L3_mlp_b1": a["L3_mix_mlp_b1"], "L3_gb1": a["L3_ffn_gb1"],
           "L3_be1": a["L3_ffn_be1"].reshape(-1)}
    given["cols"] = np.concatenate([col[n] for n in COLS]).reshape(NCOL, 128).T
    gate = {"L0_gate": a["L0_ffn_gate_w"][0], "L1_Wg": a["L1_ffn_Wg"], "L2_gfc2": a["L2_ffn_gfc2_w"].T,
            "L3_gw2": a["L3_ffn_gw2"]}
    given["gatew"] = np.concatenate([gate[n] for n in GATES]).reshape(NGATE, 128, NE).transpose(1, 0, 2)
    given["gateb"] = np.stack([a["L1_ffn_bg"], a["L3_ffn_gb2"], a["L2_ffn_gfc2_b"]])
    given["gfc2_col"] = a["L2_ffn_gfc2_b"].reshape(NE, 1)

    nc = bacc.Bacc("TRN2", target_bir_lowering=False, num_devices=1)
    arrays, ins = {}, {}
    for n, v in given.items():
        v = np.ascontiguousarray(v)
        arrays[f"in_{n}"] = v
        ins[n] = nc.dram_tensor(f"in_{n}", v.shape, mb.dt.from_np(v.dtype), kind="ExternalInput").ap()
    out = nc.dram_tensor("out_x", (N, D), mb.dt.float32, kind="ExternalOutput").ap()
    build(nc, ins, out)
    return run(nc, [arrays], core_ids=[0]).results[0]["out_x"]
```

```python
from contextlib import ExitStack

import concourse.bass as bass
from concourse import mybir

F32 = mybir.dt.float32
BF16 = mybir.dt.bfloat16
F16 = mybir.dt.float16
I32 = mybir.dt.int32
ALU = mybir.AluOpType
ACT = mybir.ActivationFunctionType
AX = mybir.AxisListType.X

N, D = 1250, 512
TP, NT = 125, 10
KD = D // 128
H, HD = 8, 64
NE = 8
E = 40000
EC = E // TP
GJ = 4
NG = (E + NT * (128 * GJ - 1)) // (128 * GJ)
NG += -NG % 4
NC = NG * GJ
AW = 1260
CW = AW // 3
R = 8
F_DST, F_SRC, F_TYPE, F_W, F_RELSRC, F_DSTREL, F_SRCI = range(7)
CHUNKS = ((0, 417), (417, 417), (834, 416))
SLOTS = 2
CAP = NE and N // NE

ROWS = ["L0_b0", "L0_b1", "L0_b2", "L1_gnn_b2", "L1_mix_b", "L1_bs2", "L2_bias", "L2_kb", "L2_vb", "L2_out_b",
        "L2_b2", "L2_ln_g", "L2_ln_b", "L3_gnn_b", "L3_kb", "L3_qb", "L3_vb", "L3_proj_b", "L3_mlp_b2"]
NR = len(ROWS)
COLS = {"L1_gnn_b1": 4, "L1_ffn_b1": 16, "L1_bs1": 2, "L2_qb": 4, "L2_g": 4, "L2_bt": 4, "L2_gfc1_b": 4, "L2_b1": 2,
        "L2_tv_b1": 16, "L3_n1_g": 4, "L3_n1_b": 4, "L3_n2_g": 4, "L3_n2_b": 4, "L3_mlp_b1": 4, "L3_gb1": 2,
        "L3_be1": 64}
COL0 = {}
for _n, _c in COLS.items():
    COL0[_n] = sum(COLS[m] for m in COL0)
NCOL = sum(COLS.values())
GATES = {"L0_gate": 4, "L1_Wg": 4, "L2_gfc2": 4, "L3_gw2": 2}
GATE0 = {}
for _n, _c in GATES.items():
    GATE0[_n] = sum(GATES[m] for m in GATE0)
NGATE = sum(GATES.values())


class Ring:

    def __init__(self, nc, ctx, loads, plain):
        self.plain = plain
        self.raw = ctx.enter_context(nc.sbuf_tensor("weights_in", [128, SLOTS, 4 * D], F32))
        self.buf = ctx.enter_context(nc.sbuf_tensor("weights_split", [128, SLOTS, 2, 4 * D], F16))
        self.loaded = [ctx.enter_context(nc.semaphore(f"weights_loaded{s}")) for s in range(SLOTS)]
        self.high_done = ctx.enter_context(nc.semaphore("weights_high_done"))
        self.split_done = ctx.enter_context(nc.semaphore("weights_split_done"))
        self.freed = [ctx.enter_context(nc.semaphore(f"weights_freed{s}")) for s in range(SLOTS)]
        self.loads = loads
        self.issued = 0
        self.high = 0
        self.low = 0
        self.used = 0
        self.count = []
        per = [0] * SLOTS
        for n, parts in enumerate(loads):
            per[n % SLOTS] += 16 * len(parts)
            self.count.append(per[n % SLOTS])

    def issue(self, sp, upto, over_plain=False):
        for n in range(self.issued, min(upto, len(self.loads))):
            if n - SLOTS in self.plain and not over_plain:
                break
            self.issued = n + 1
            if n >= SLOTS:
                sp.wait_ge(self.split_done, n - SLOTS + 1)
            for lo, hi, k, ap in self.loads[n]:
                dst = self.raw[:, n % SLOTS, lo:hi].rearrange("p (k n) -> p k n", k=k)
                sp.dma_start(dst, ap).then_inc(self.loaded[n % SLOTS], 16)

    def width(self, n):
        return max(hi for lo, hi, k, ap in self.loads[n])

    def split_high(self, act, upto):
        for n in range(self.high, min(upto, len(self.loads))):
            if n in self.plain:
                break
            self.high_of(act, n)
            self.high = n + 1

    def high_of(self, act, n, loads_before=0, in_before=0):
        if n >= SLOTS:
            act.wait_ge(self.freed[n % SLOTS], n // SLOTS + loads_before)
        act.wait_ge(self.loaded[n % SLOTS], self.count[n] + in_before)
        w = self.width(n)
        act.activation(self.buf[:, n % SLOTS, 0, 0:w], self.raw[:, n % SLOTS, 0:w], ACT.Copy).then_inc(self.high_done, 1)

    def split_low(self, dve, upto):
        for n in range(self.low, min(upto, len(self.loads))):
            if n in self.plain:
                break
            self.low_of(dve, n)
            self.low = n + 1

    def low_of(self, dve, n, loads_before=0):
        dve.wait_ge(self.high_done, n + 1 + loads_before)
        w = self.width(n)
        dve.tensor_tensor(self.buf[:, n % SLOTS, 1, 0:w], self.raw[:, n % SLOTS, 0:w], self.buf[:, n % SLOTS, 0, 0:w],
                          ALU.subtract).then_inc(self.split_done, 1)

    def wait(self, eng, n):
        eng.wait_ge(self.split_done, n + 1)

    def mat(self, n, lo=0, hi=4 * D, k=4):
        return self.buf[:, n % SLOTS, :, lo:hi].rearrange("p s (k n) -> p s k n", k=k)


def build(nc, ins, out):
    with ExitStack() as ctx:
        names = {}

        def sbuf(c, name, shape, dt=F32, side="left"):
            names[name] = names.get(name, 0) + 1
            if names[name] > 1:
                name = f"{name}_{names[name]}"
            return c.enter_context(nc.sbuf_tensor(name, shape, dt, side=side))

        def mats(t, order=None):
            w = t.shape[1] // D
            return [[(0, 4 * D, 4, t[:, m * D:(m + 1) * D].rearrange("(k p) n -> p k n", p=128))]
                    for m in (order or range(w))]

        def pairs(a, b):
            return [[(0, 2 * D, 4, a.rearrange("(k p) n -> p k n", p=128)),
                     (2 * D, 4 * D, 2, b.rearrange("(k p) n -> p k n", p=128))]]

        loads, first = [], {}

        def plan(name, items):
            first[name] = len(loads)
            loads.extend(items)

        I = ins
        plan("L0_q", mats(I["L0_mix_Wq"]))
        plan("L0_kv", mats(I["L0_mix_Wkv"]))
        for l in range(3):
            plan(f"L0_self{l}", mats(I["L0_gnn_W_self"][l]))
            plan(f"L0_neigh{l}", mats(I["L0_gnn_W_neigh"][l]))
        plan("L0_exp", [m for e in range(NE) for m in mats(I["L0_ffn_experts"][e])])
        plan("L1_W1", mats(I["L1_gnn_W1"]))
        plan("L1_W2", mats(I["L1_gnn_W2"]))
        plan("L1_qkv", mats(I["L1_mix_w_qkv"]))
        plan("L1_proj", mats(I["L1_mix_w_proj"]))
        plan("L1_exp", [m for e in range(NE) for m in pairs(I["L1_ffn_W1"][e], I["L1_ffn_W2"][e])])
        plan("L1_shared", pairs(I["L1_ffn_Ws1"], I["L1_ffn_Ws2"]))
        plan("L2_self", mats(I["L2_gnn_W_self"]))
        plan("L2_rel", [m for e in range(NE) for m in mats(I["L2_gnn_W_rel"][e])])
        plan("L2_qkv", mats(I["L2_mix_qkv_w"]))
        plan("L2_out", mats(I["L2_mix_out_w"]))
        plan("L2_gfc1", mats(I["L2_ffn_gfc1_w"]))
        plan("L2_base", pairs(I["L2_ffn_W1"], I["L2_ffn_W2"]))
        plan("L2_tv", [m for e in range(NE) for m in pairs(I["L2_ffn_tv_W1"][e], I["L2_ffn_tv_W2"][e])])
        plan("L3_gnn", mats(I["L3_gnn_W"]))
        plan("L3_kqv", mats(I["L3_mix_kqv_w"]))
        plan("L3_w", [[(0, 2 * D, 4, I["L3_mix_w"].rearrange("(k p) n -> p k n", p=128))]])
        plan("L3_proj", mats(I["L3_mix_proj_w"]))
        plan("L3_mlp1", mats(I["L3_mix_mlp_w1"]))
        plan("L3_mlp2", mats(I["L3_mix_mlp_w2"]))
        plan("L3_gw1", [[(0, 2 * D, 4, I["L3_ffn_gw1"].rearrange("(k p) n -> p k n", p=128))]])
        plan("L3_exp", [m for i in range(2 * NE) for m in mats(I["L3_ffn_we1"][i]) + mats(I["L3_ffn_we2"][i])])

        x = sbuf(ctx, "x", [TP, NT, D])
        xn = sbuf(ctx, "xn", [TP, NT, D])
        xT = sbuf(ctx, "xT", [128, 2, KD, N], F16)
        ring = Ring(nc, ctx, loads, range(first["L2_base"], first["L2_tv"] + NE))
        rows = sbuf(ctx, "rows", [NR, 2, D], F16)
        pick = sbuf(ctx, "pick", [NR, NR, TP], F16)
        cols = sbuf(ctx, "cols", [128, NCOL])
        gatew = sbuf(ctx, "gatew", [128, 2, NGATE, NE], F16)
        gateb = sbuf(ctx, "gateb", [128, 3, NE])
        expert_b2 = sbuf(ctx, "expert_b2", [NE, 2, D])
        gfc2_col = sbuf(ctx, "gfc2_col", [NE, 1])
        ident = sbuf(ctx, "ident", [128, 128])
        ones = sbuf(ctx, "ones", [128, 128])
        below = sbuf(ctx, "below", [TP, TP])
        staging = sbuf(ctx, "staging", [128, 4, D])
        stats = sbuf(ctx, "stats", [TP, NT, 6])
        mv = sbuf(ctx, "mv", [TP, NT, 2])
        rstd = sbuf(ctx, "rstd", [TP, NT])
        rdeg = sbuf(ctx, "rdeg", [TP, NT])
        group_tile = sbuf(ctx, "group_tile", [1, NG], I32)
        iota_tile = sbuf(ctx, "iota_tile", [128, TP])
        ps = ctx.enter_context(nc.psum_tensor("ps", [128, 8, 512], F32))

        count_row = sbuf(ctx, "count_row", [128, NC], I32)
        count_weight = sbuf(ctx, "count_weight", [128, NC])

        edge_table = nc.dram_tensor("edge_table", (128 * NC, R), F32, kind="Internal").ap()
        count_table = nc.dram_tensor("count_table", (N * NE, 1), F32, kind="Internal").ap()
        rel_table = nc.dram_tensor("rel_table", (NE * N, D), F32, kind="Internal").ap()
        xn_table = nc.dram_tensor("xn_table", (N, D), F32, kind="Internal").ap()

        class Stage:

            def __init__(self, *names):
                self.names = names

            def __enter__(self):
                self.c = ExitStack()
                sems = [self.c.enter_context(nc.semaphore(n)) for n in self.names]
                self.sems = sems
                self.b = nc.Block()
                block = self.b.__enter__()
                return (block, *sems)

            def __exit__(self, *a):
                self.b.__exit__(*a)
                if a[0] is None:
                    for s in self.sems:
                        nc.sync.sem_clear(s)
                    nc.all_engine_barrier(sem_only=True)
                return self.c.__exit__(*a)

        def chain(eng, sem, before=0):
            n = [0]

            def link(ins):
                n[0] += 1
                ins.then_inc(sem, 1)
                eng.wait_ge(sem, before + n[0])
            return link

        def tile_of(t):
            return slice(t * TP, (t + 1) * TP)

        def bank(b, p=TP, w=D):
            return ps[0:p, b, 0:w]

        PASSES = ((0, 0), (0, 1), (1, 0))

        def tok_product(pe, dst, srcT, t, w, k_blocks, row=None, start=True, stop=True):
            if row is not None:
                for part in range(2):
                    pe.matmul(dst, pick[:, ROWS.index(row), :], rows[:, part, :], start=start and part == 0, stop=False)
                start = False
            for k in range(k_blocks):
                for a, b in PASSES:
                    last = pe.matmul(dst, srcT[:, a, k, tile_of(t)], w[:, b, k, :], start=start, stop=stop and
                                     k == k_blocks - 1 and a == 1)
                    start = False
            return last

        def feat_product(pe, dst, w, f, srcT, lo, n, k_blocks):
            for k in range(k_blocks):
                for a, b in PASSES:
                    last = pe.matmul(dst, w[:, a, k, f * 128:(f + 1) * 128], srcT[:, b, k, lo:lo + n],
                                     start=k == 0 and a + b == 0, stop=k == k_blocks - 1 and a == 1)
            return last

        def split_evac(func, view, out, bias=None):
            def evac(act, u, b, link):
                v = view(u, b)
                g = staging[0:v.shape[0], u % 4, 0:v.shape[1]]
                link(act.activation(g, v, func, **({} if bias is None else {"bias": bias(u)})))
                return act.activation(out(u)[0], g, ACT.Copy)

            def finish(dve, u, b, link):
                high, low = out(u)
                return dve.tensor_tensor(low, staging[0:low.shape[0], u % 4, 0:low.shape[1]], high, ALU.subtract)
            return evac, finish

        def gemm(units, products, evac, finish=None, evac_on="scalar", weights=None, frees=None, extra=None, nb=4,
                 finish_reads_bank=False):
            weights, frees = weights or {}, frees or {}
            total = sum(frees.values())
            with Stage("product_ready", "bank_drained", "evac_chain", "finish_chain", "finished") as (
                    block, product_ready, bank_drained, evac_chain, finish_chain, finished):
                start = ring.used
                need = max([start + total] + [n + 1 for load_numbers in weights.values() for n in load_numbers])

                @block.sync
                def _(sp):
                    ring.issue(sp, start + 2 * SLOTS)

                @block.tensor
                def _(pe):
                    for u in range(units):
                        for n in weights.get(u, ()):
                            ring.wait(pe, n)
                        if u >= nb:
                            pe.wait_ge(finished if finish_reads_bank else bank_drained, u - nb + 1)
                        products(pe, u, u % nb).then_inc(product_ready, 1)

                def split(eng, vector, upto):
                    (ring.split_low if vector else ring.split_high)(eng, upto)

                def drain(eng):
                    link = chain(eng, evac_chain)
                    split(eng, evac_on == "vector", need)
                    for u in range(units):
                        eng.wait_ge(product_ready, u + 1)
                        if finish and u >= 4:
                            eng.wait_ge(finished, u - 3)
                        evac(eng, u, u % nb, link).then_inc(bank_drained, 1)
                        if u == 0:
                            split(eng, evac_on == "vector", start + SLOTS)
                    for n in range(start, start + total):
                        eng.sem_inc(ring.freed[n % SLOTS], 1)

                def complete(eng):
                    link = chain(eng, finish_chain)
                    split(eng, evac_on != "vector", need)
                    for u in range(units if finish else 1):
                        if finish:
                            eng.wait_ge(bank_drained, u + 1)
                            finish(eng, u, u % nb, link).then_inc(finished, 1)
                        if u == 0:
                            split(eng, evac_on != "vector", start + SLOTS)

                if evac_on == "scalar":
                    block.scalar(drain)
                    block.vector(complete)
                else:
                    block.vector(drain)
                    block.scalar(complete)
                if extra:
                    extra(block)
            ring.used += total

        def transposes(src, dstT, blocks, scale=None, bias=None, tokens=None):
            split = len(dstT.shape) == 4

            def products(pe, t, b):
                for k in range(blocks):
                    last = pe.transpose(ps[:, b, k * TP:(k + 1) * TP], src[:, t, k * 128:(k + 1) * 128], ident[0:TP, 0:TP])
                return last

            def view(b):
                return ps[:, b, 0:blocks * TP].rearrange("p (k n) -> p k n", k=blocks)

            def evac(act, t, b, link):
                if tokens is not None:
                    act.activation(tokens[:, 0, t, :], src[:, t, :], ACT.Copy)
                if scale is None:
                    return act.activation(dstT[:, 0, 0:blocks, tile_of(t)] if split else dstT[:, 0:blocks, tile_of(t)],
                                          view(b), ACT.Copy)
                g = staging[:, t % 4, 0:blocks * TP].rearrange("p (k n) -> p k n", k=blocks)
                for k in range(blocks):
                    last = act.activation(g[:, k, :], view(b)[:, k, :], ACT.Identity,
                                          bias=cols[:, bias + k:bias + k + 1], scale=cols[:, scale + k:scale + k + 1])
                link(last)
                return act.activation(dstT[:, 0, 0:blocks, tile_of(t)], g, ACT.Copy)

            def finish(dve, t, b, link):
                if tokens is not None:
                    dve.tensor_tensor(tokens[:, 1, t, :], src[:, t, :], tokens[:, 0, t, :], ALU.subtract)
                full = view(b) if scale is None else staging[:, t % 4, 0:blocks * TP].rearrange("p (k n) -> p k n", k=blocks)
                return dve.tensor_tensor(dstT[:, 1, 0:blocks, tile_of(t)], full, dstT[:, 0, 0:blocks, tile_of(t)],
                                         ALU.subtract)
            gemm(NT, products, evac, finish if split else None, finish_reads_bank=split and scale is None)

        def layernorm(src, dst, eps):
            with Stage("stats_ready", "std_ready", "dve_chain") as (block, stats_ready, std_ready, dve_chain):
                @block.vector
                def _(dve):
                    link = chain(dve, dve_chain)
                    for t in range(NT):
                        last = dve.bn_stats(stats[:, t, :], src[:, t, :])
                    link(last)
                    for t in range(NT):
                        last = dve.bn_aggr(mv[:, t, :], stats[:, t, :])
                    link(last)
                    dve.tensor_scalar(rstd[:], mv[:, :, 1], eps, None, ALU.add).then_inc(stats_ready, 1)
                    dve.wait_ge(std_ready, 1)
                    link(dve.reciprocal(rstd[:], rstd[:]))
                    for t in range(NT):
                        last = dve.tensor_scalar(dst[:, t, :], src[:, t, :], mv[:, t, 0:1], rstd[:, t:t + 1],
                                                 ALU.subtract, ALU.mult)

                @block.scalar
                def _(act):
                    act.wait_ge(stats_ready, 1)
                    act.activation(rstd[:], rstd[:], ACT.Sqrt).then_inc(std_ready, 1)

                @block.sync
                def _(sp):
                    ring.issue(sp, ring.used + SLOTS)

        def layernorm_T(src, dst, dstT, eps=1e-5, scale=None, bias=None, tokens=None):
            layernorm(src, dst, eps)
            transposes(dst, dstT, KD, scale, bias, tokens)

        def add_to_x(dve, t, b, link):
            return dve.tensor_tensor(x[:, t, :], bank(b), x[:, t, :], ALU.add)

        c_in = ExitStack()
        rows_in = sbuf(c_in, "rows_in", [NR, D])
        gatew_in = sbuf(c_in, "gatew_in", [128, NGATE, NE])
        with Stage("consts_in", "pool_step", "x_in", "high_done") as (block, consts_in, pool_step, x_in, high_done):
            @block.sync
            def _(sp):
                sp.dma_start(x[:], I["x"].rearrange("(t p) d -> p t d", p=TP)).then_inc(x_in, 16)
                sp.dma_start(rows_in[:], I["rows"]).then_inc(consts_in, 16)
                sp.dma_start(cols[:], I["cols"]).then_inc(consts_in, 16)
                sp.dma_start(gatew_in[:], I["gatew"]).then_inc(consts_in, 16)
                sp.dma_start(gateb[:], I["gateb"].rearrange("(o g) e -> o g e", o=1).to_broadcast([128, 3, NE])
                             ).then_inc(consts_in, 16)
                sp.dma_start(gfc2_col[:], I["gfc2_col"]).then_inc(consts_in, 16)
                sp.dma_start(expert_b2[:, 0, :], I["L1_ffn_b2"]).then_inc(consts_in, 16)
                sp.dma_start(expert_b2[:, 1, :], I["L3_ffn_be2"]).then_inc(consts_in, 16)
                ring.issue(sp, SLOTS)
                sp.wait_ge(x_in, 16)
                sp.wait_ge(consts_in, 112)

            @block.gpsimd
            def _(pool):
                link = chain(pool, pool_step)
                link(pool.memset(ones[:], 1.0))
                pool.affine_select(out=ident[:], in_=ones[:], compare_op=ALU.is_equal, fill=0.0, base=0,
                                   pattern=[[-1, 128]], channel_multiplier=1)
                pool.affine_select(out=below[:], in_=ones[0:TP, 0:TP], compare_op=ALU.is_gt, fill=0.0, base=0,
                                   pattern=[[1, TP]], channel_multiplier=-1)
                link(pool.memset(pick[:], 1.0))
                link(pool.affine_select(out=pick[:], in_=pick[:], compare_op=ALU.is_equal, fill=0.0, base=0,
                                        pattern=[[-1, NR], [0, TP]], channel_multiplier=1))
                link(pool.iota(iota_tile[:], [[1, TP]], 0, 0, allow_small_or_imprecise_dtypes=True))

            @block.scalar
            def _(act):
                act.wait_ge(consts_in, 112)
                act.activation(rows[:, 0, :], rows_in[:], ACT.Copy)
                act.activation(gatew[:, 0], gatew_in[:], ACT.Copy).then_inc(high_done, 1)

            @block.vector
            def _(dve):
                dve.wait_ge(high_done, 1)
                dve.tensor_tensor(rows[:, 1, :], rows_in[:], rows[:, 0, :], ALU.subtract)
                dve.tensor_tensor(gatew[:, 1], gatew_in[:], gatew[:, 0], ALU.subtract)
        c_in.close()

        c0 = ExitStack()
        records = sbuf(c0, "records", [TP, EC, R])
        slot = sbuf(c0, "slot", [TP, EC], I32)
        with ExitStack() as c:
            esrc = sbuf(c, "esrc", [TP, EC], I32)
            edst = sbuf(c, "edst", [TP, EC], I32)
            etype = sbuf(c, "etype", [TP, EC], I32)
            eweight = sbuf(c, "eweight", [TP, EC])
            dstf = sbuf(c, "dstf", [TP, EC])
            tile_f = sbuf(c, "tile_f", [TP, EC])
            one_row = sbuf(c, "one_row", [TP, EC])
            mask = sbuf(c, "mask", [TP, NT, EC])
            rank = sbuf(c, "rank", [TP, NT, EC])
            pos = sbuf(c, "pos", [TP, EC], I32)
            lane = sbuf(c, "lane", [TP, EC], I32)
            totals = sbuf(c, "totals", [TP, NT])
            ngroups_i = sbuf(c, "ngroups_i", [TP, NT], I32)
            ngroups = sbuf(c, "ngroups", [TP, NT])
            group_end = sbuf(c, "group_end", [TP, NT])
            offset = sbuf(c, "offset", [TP, NT])
            iota_g = sbuf(c, "iota_g", [1, NG])
            tile_acc = sbuf(c, "tile_acc", [1, NG])
            blank = sbuf(c, "blank", [128, NC, R])
            ri = records[:].bitcast(I32)
            with Stage("edges_in", "dve_chain", "pool_step", "totals_ready", "prefix_ready", "table_blank") as (
                    block, edges_in, dve_chain, pool_step, totals_ready, prefix_ready, table_blank):
                @block.sync
                def _(sp):
                    for dst, name in ((esrc, "src"), (edst, "dst"), (etype, "edge_type_8")):
                        sp.dma_start(dst[:], I[name].rearrange("(p c) -> p c", c=EC)).then_inc(edges_in, 16)
                    sp.dma_start(eweight[:], I["edge_weight1"].rearrange("(p c) o -> p (c o)", c=EC)).then_inc(edges_in, 16)
                    sp.wait_ge(pool_step, 2)
                    sp.dma_start(edge_table.rearrange("(p c) r -> p c r", c=NC), blank[:]).then_inc(table_blank, 16)
                    sp.wait_ge(table_blank, 16)

                @block.gpsimd
                def _(pool):
                    link = chain(pool, pool_step)
                    link(pool.memset(blank[:], 0.0))
                    link(pool.memset(blank[:, :, F_DST], -1.0))
                    link(pool.iota(iota_g[:], [[1, NG]], 0, 0, allow_small_or_imprecise_dtypes=True))

                @block.vector
                def _(dve):
                    link = chain(dve, dve_chain)
                    dve.memset(one_row[:], 1.0)
                    dve.memset(records[:], 0.0)
                    link(dve.memset(tile_acc[:], 0.0))
                    dve.wait_ge(edges_in, 64)
                    dve.tensor_copy(dstf[:], edst[:])
                    dve.tensor_copy(records[:, :, F_SRC], esrc[:])
                    dve.tensor_copy(ri[:, :, F_SRCI], esrc[:])
                    dve.tensor_copy(records[:, :, F_W], eweight[:])
                    link(dve.tensor_copy(records[:, :, F_TYPE], etype[:]))
                    dve.scalar_tensor_tensor(out=ri[:, :, F_RELSRC], in0=records[:, :, F_TYPE], scalar=float(N),
                                             in1=records[:, :, F_SRC], op0=ALU.mult, op1=ALU.add)
                    link(dve.scalar_tensor_tensor(out=ri[:, :, F_DSTREL], in0=dstf[:], scalar=float(NE),
                                                  in1=records[:, :, F_TYPE], op0=ALU.mult, op1=ALU.add))
                    link(dve.tensor_scalar(tile_f[:], dstf[:], float(TP), None, ALU.is_ge))
                    for b in range(2, NT):
                        link(dve.scalar_tensor_tensor(out=tile_f[:], in0=dstf[:], scalar=float(TP * b),
                                                      in1=tile_f[:], op0=ALU.is_ge, op1=ALU.add))
                    dve.scalar_tensor_tensor(out=records[:, :, F_DST], in0=tile_f[:], scalar=-float(TP),
                                             in1=dstf[:], op0=ALU.mult, op1=ALU.add)
                    for b in range(NT):
                        last = dve.tensor_scalar(mask[:, b, :], tile_f[:], float(b), None, ALU.is_equal)
                    link(last)
                    for b in range(NT):
                        last = dve.tensor_tensor_scan(out=rank[:, b, :], data0=one_row[:], data1=mask[:, b, :],
                                                      initial=0.0, op0=ALU.mult, op1=ALU.add)
                    link(last)
                    dve.tensor_copy(totals[:], rank[:, :, EC - 1]).then_inc(totals_ready, 1)
                    dve.wait_ge(prefix_ready, 1)
                    link(dve.tensor_scalar(ngroups_i[:], ps[0:TP, 1, 0:NT], float(128 * GJ - 1), None, ALU.add))
                    link(dve.tensor_scalar(ngroups_i[:], ngroups_i[:], 9, None, ALU.arith_shift_right))
                    link(dve.tensor_copy(ngroups[:], ngroups_i[:]))
                    link(dve.tensor_tensor_scan(out=group_end[:], data0=one_row[:, 0:NT], data1=ngroups[:],
                                                initial=0.0, op0=ALU.mult, op1=ALU.add))
                    link(dve.tensor_tensor(offset[:], group_end[:], ngroups[:], ALU.subtract))
                    link(dve.tensor_scalar(offset[:], offset[:], float(128 * GJ), -1.0, ALU.mult, ALU.add))
                    link(dve.tensor_tensor(offset[:], offset[:], ps[0:TP, 0, 0:NT], ALU.add))
                    for b in range(NT):
                        last = dve.scalar_tensor_tensor(out=rank[:, b, :], in0=rank[:, b, :], scalar=offset[:, b:b + 1],
                                                        in1=mask[:, b, :], op0=ALU.add, op1=ALU.mult)
                    link(last)
                    link(dve.tensor_reduce(dstf[:], rank[:].rearrange("p b c -> p c b"), AX.X, ALU.add))
                    link(dve.tensor_copy(pos[:], dstf[:]))
                    dve.tensor_scalar(lane[:], pos[:], 127, None, ALU.bitwise_and)
                    link(dve.tensor_scalar(pos[:], pos[:], 7, None, ALU.arith_shift_right))
                    dve.scalar_tensor_tensor(out=slot[:], in0=lane[:], scalar=float(NC), in1=pos[:],
                                             op0=ALU.mult, op1=ALU.add)
                    dve.wait_ge(pool_step, 3)
                    for b in range(NT - 1):
                        link(dve.scalar_tensor_tensor(out=tile_acc[:], in0=iota_g[:], scalar=group_end[0:1, b:b + 1],
                                                      in1=tile_acc[:], op0=ALU.is_ge, op1=ALU.add))
                    dve.tensor_copy(group_tile[:], tile_acc[:])

                @block.tensor
                def _(pe):
                    pe.wait_ge(totals_ready, 1)
                    pe.matmul(ps[0:TP, 0, 0:NT], below[:], totals[:], start=True, stop=True)
                    pe.matmul(ps[0:TP, 1, 0:NT], ones[0:TP, 0:TP], totals[:], start=True, stop=True).then_inc(prefix_ready, 1)

        layernorm_T(x, xn, xT)

        def elu1(dst, exp_buf, src_of, bias=None):
            def evac(act, u, b, link):
                d = dst(u)
                e = exp_buf[0:d.shape[0], u % 4, 0:d.shape[1]]
                plus = {} if bias is None else {"bias": bias(u)[0]}
                minus = {} if bias is None else {"bias": bias(u)[1]}
                link(act.activation(e, src_of(u, b), ACT.Relu, scale=-1.0, **minus))
                act.activation(e, e, ACT.Exp, scale=-1.0)
                return act.activation(d, src_of(u, b), ACT.Relu, **plus)

            def finish(dve, u, b, link):
                d = dst(u)
                return dve.tensor_tensor(d, exp_buf[0:d.shape[0], u % 4, 0:d.shape[1]], d, ALU.add)
            return evac, finish

        def feat_units(n_load, dstT, srcT, k_blocks):
            def products(pe, u, b):
                f, (lo, n) = u // 3, CHUNKS[u % 3]
                return feat_product(pe, ps[:, b, 0:n], ring.mat(n_load), f, srcT, lo, n, k_blocks)

            def dst(u):
                f, (lo, n) = u // 3, CHUNKS[u % 3]
                return dstT[:, f, lo:lo + n]

            def src_of(u, b):
                return ps[:, b, 0:CHUNKS[u % 3][1]]
            return products, dst, src_of

        def pair_of(dstT):
            def out(u):
                f, (lo, n) = u // 3, CHUNKS[u % 3]
                return dstT[:, 0, f, lo:lo + n], dstT[:, 1, f, lo:lo + n]
            return out

        VW = 129

        def kv_and_apply(c, qT, k, vo, eps, to=None, col_scale=None, den_ones=False, extra=None):
            bd = sbuf(c, "kv_blocks", [128, 4, 130])
            den = sbuf(c, "att_den", [TP, 2, H])
            att = sbuf(c, "att", [TP, 2, D]) if to is None else None
            with Stage("kv_ready", "blocks_ready", "product_ready", "drained", "dve_chain") as (
                    block, kv_ready, blocks_ready, product_ready, drained, dve_chain):
                if extra:
                    extra(block)

                @block.tensor
                def _(pe):
                    for g in range(4):
                        for t in range(NT):
                            last = pe.matmul(ps[:, g, 0:VW], k[:, t, g * 128:(g + 1) * 128], vo[:, t, g, :],
                                             start=t == 0, stop=t == NT - 1)
                    last.then_inc(kv_ready, 1)
                    pe.wait_ge(blocks_ready, 1)
                    for t in range(NT):
                        if t >= 2:
                            pe.wait_ge(drained, t - 1)
                        for g in range(4):
                            last = pe.matmul(ps[0:TP, 4 + 2 * (t % 2) + g // 2, (g % 2) * 130:(g % 2) * 130 + 130],
                                             qT[:, g, tile_of(t)], bd[:, g, :], start=True, stop=True)
                        last.then_inc(product_ready, 1)

                @block.vector
                def _(dve):
                    link = chain(dve, dve_chain)
                    link(dve.memset(bd[:], 0.0))
                    dve.wait_ge(kv_ready, 1)
                    for g in range(4):
                        for h in range(2):
                            pr = slice(64 * h, 64 * h + 64)
                            if col_scale is None:
                                dve.tensor_copy(bd[pr, g, 64 * h:64 * h + 64], ps[pr, g, 64 * h:64 * h + 64])
                            else:
                                dve.tensor_scalar(bd[pr, g, 64 * h:64 * h + 64], ps[pr, g, 64 * h:64 * h + 64],
                                                  col_scale[pr, g:g + 1], None, ALU.mult)
                            if den_ones:
                                last = dve.tensor_copy(bd[pr, g, 128 + h:129 + h], ones[pr, 0:1])
                            else:
                                last = dve.tensor_copy(bd[pr, g, 128 + h:129 + h], ps[pr, g, 128:129])
                    last.then_inc(blocks_ready, 1)
                    for t in range(NT):
                        dve.wait_ge(product_ready, t + 1)
                        v = ps[0:TP, 4 + 2 * (t % 2):6 + 2 * (t % 2), 0:260].rearrange("p b (g w) -> p b g w", g=2)
                        dn = den[:, t % 2, :].rearrange("p (b g h) -> p b g h", b=2, g=2)
                        link(dve.tensor_scalar(dn, v[:, :, :, 128:130], eps, None, ALU.add))
                        link(dve.reciprocal(den[:, t % 2, :], den[:, t % 2, :]))
                        for bb in range(2):
                            a = (att[:, t % 2] if to is None else to[:, t])[:, bb * 256:(bb + 1) * 256].rearrange("p (g h d) -> p g h d", g=2, h=2)
                            vv = v[:, bb, :, 0:128].rearrange("p g (h d) -> p g h d", h=2)
                            dd = dn[:, bb].rearrange("p g (h o) -> p g h o", o=1).to_broadcast([TP, 2, 2, 64])
                            last = dve.tensor_tensor(a, vv, dd, ALU.mult)
                        if to is None:
                            link(last)
                            last = dve.tensor_tensor(x[:, t, :], att[:, t % 2, :], x[:, t, :], ALU.add)
                        last.then_inc(drained, 1)

                @block.sync
                def _(sp):
                    ring.issue(sp, ring.used + SLOTS)

        SC = 8
        slot_stage = sbuf(c0, "slot_stage", [TP, 2, SC], I32)
        record_stage = sbuf(c0, "record_stage", [TP, 2, SC, R])
        records_out = [ctx.enter_context(nc.semaphore(f"records_out{b}")) for b in range(2)]
        record_staged = ctx.enter_context(nc.semaphore("record_staged"))
        loop_turn = ctx.enter_context(nc.semaphore("loop_turn"))

        def scatter_edges(first_set, sets):
            assert sets % 2 == 0 and first_set % 2 == 0

            def put(pool, n, b):
                pool.tensor_copy(slot_stage[:, b, :], slot[:, bass.ds(SC * n, SC)])
                pool.tensor_copy(record_stage[:, b], records[:, bass.ds(SC * n, SC), :]).then_inc(record_staged, 1)
                pool.wait_ge(record_staged, n + 1)
                pool.sem_inc(loop_turn, 1)
                for j in range(SC):
                    pool.indirect_dma_start(edge_table, bass.IndirectOffsetOnAxis(ap=slot_stage[:, b, j:j + 1], axis=0),
                                            record_stage[:, b, j, :], None).then_inc(records_out[b], 16)

            def add(block):
                h = first_set // 2

                @block.gpsimd
                def _(pool):
                    put(pool, first_set, 0)
                    if sets > 2:
                        with pool.Fori(0, sets // 2 - 1) as i:
                            put(pool, 2 * i + (first_set + 1), 1)
                            pool.wait_ge(records_out[0], 16 * SC * i + 16 * SC * (h + 1))
                            pool.sem_inc(loop_turn, 1)
                            put(pool, 2 * i + (first_set + 2), 0)
                            pool.wait_ge(records_out[1], 16 * SC * i + 16 * SC * (h + 1))
                            pool.sem_inc(loop_turn, 1)
                    put(pool, first_set + sets - 1, 1)
                    for b in range(2):
                        pool.wait_ge(records_out[b], 16 * SC * (h + sets // 2))
            return add

        def elu_q(qT, ebuf, srcT, n, bias=None, extra=None):
            pr, dst, src_of = feat_units(n, qT, srcT, KD)
            ev, fi = elu1(dst, ebuf, src_of, bias)
            gemm(12, pr, ev, fi, weights={0: [n]}, frees={11: 1}, extra=extra)

        def elu_k(k, ebuf, srcT, n, row=None, extra=None):
            ev, fi = elu1(lambda u: k[:, u, :], ebuf, lambda u, b: bank(b))
            gemm(NT, lambda pe, u, b: tok_product(pe, bank(b), srcT, u, ring.mat(n), KD, row), ev, fi,
                 weights={0: [n]}, frees={NT - 1: 1}, extra=extra)

        def values(vo, srcT, n, row=None, extra=None):
            def evac(act, u, b, link):
                act.activation(vo[:, u, :, 128], ones[0:TP, 0:4], ACT.Copy)
                return act.activation(vo[:, u, :, 0:128], bank(b).rearrange("p (g w) -> p g w", g=4), ACT.Copy)
            gemm(NT, lambda pe, u, b: tok_product(pe, bank(b), srcT, u, ring.mat(n), KD, row), evac,
                 weights={0: [n]}, frees={NT - 1: 1}, extra=extra)

        def dense(srcT, n, dst, k_blocks=KD, row=None, add=None, scale=None):
            def evac(eng, u, b, link):
                if add is None:
                    return eng.activation(dst[:, u, :], bank(b), ACT.Copy)
                if scale is not None:
                    return eng.scalar_tensor_tensor(out=dst[:, u, :], in0=bank(b), scalar=scale, in1=add[:, u, :],
                                                    op0=ALU.mult, op1=ALU.add)
                return eng.tensor_tensor(dst[:, u, :], bank(b), add[:, u, :], ALU.add)
            w = ring.mat(n) if k_blocks == KD else ring.mat(n, 2 * D, 4 * D, 2)
            gemm(NT, lambda pe, u, b: tok_product(pe, bank(b), srcT, u, w, k_blocks, row), evac,
                 evac_on="scalar" if add is None else "vector", weights={0: [n]}, frees={NT - 1: 1})

        counts_in = [ctx.enter_context(nc.semaphore(f"counts_in{b}")) for b in range(2)]
        count_staged = ctx.enter_context(nc.semaphore("count_staged"))

        def gather_counts(c, first_set, sets):
            assert sets % 2 == 0 and first_set % 2 == 0 and NC % (2 * SC) == 0
            row_stage = sbuf(c, "row_stage", [128, 2, SC], I32)
            count_stage = sbuf(c, "count_stage", [128, 2, SC])

            def ask(pool, n, b):
                pool.tensor_copy(row_stage[:, b, :], count_row[:, bass.ds(SC * n, SC)]).then_inc(count_staged, 1)
                pool.wait_ge(count_staged, n + 1)
                pool.sem_inc(loop_turn, 1)
                for j in range(SC):
                    pool.indirect_dma_start(count_stage[:, b, j:j + 1], None, count_table, bass.IndirectOffsetOnAxis(
                        ap=row_stage[:, b, j:j + 1], axis=0)).then_inc(counts_in[b], 16)

            def take(pool, n, b, count):
                pool.wait_ge(counts_in[b], count)
                pool.sem_inc(loop_turn, 1)
                pool.tensor_copy(count_weight[:, bass.ds(SC * n, SC)], count_stage[:, b, :])

            def add(block):
                h = first_set // 2

                @block.gpsimd
                def _(pool):
                    ask(pool, first_set, 0)
                    with pool.Fori(0, sets // 2 - 1) as i:
                        ask(pool, 2 * i + (first_set + 1), 1)
                        take(pool, 2 * i + first_set, 0, 16 * SC * i + 16 * SC * (h + 1))
                        ask(pool, 2 * i + (first_set + 2), 0)
                        take(pool, 2 * i + (first_set + 1), 1, 16 * SC * i + 16 * SC * (h + 1))
                    ask(pool, first_set + sets - 1, 1)
                    for b in range(2):
                        take(pool, first_set + sets - 2 + b, b, 16 * SC * (h + sets // 2))
            return add

        with ExitStack() as c:
            qT = sbuf(c, "qT", [128, KD, N])
            k = sbuf(c, "k", [TP, NT, D])
            vo = sbuf(c, "vo", [TP, NT, 4, VW])
            ebuf = sbuf(c, "ebuf", [128, 4, D])
            elu_q(qT, ebuf, xT, first["L0_q"], extra=scatter_edges(0, 4))
            elu_k(k, ebuf, xT, first["L0_kv"], extra=scatter_edges(4, 4))
            values(vo, xT, first["L0_kv"] + 1, extra=scatter_edges(8, 4))
            kv_and_apply(c, qT, k, vo, 1e-6, extra=scatter_edges(12, 4))
        with Stage() as (block,):
            scatter_edges(16, EC // SC - 16)(block)
        c0.close()

        with ExitStack() as c_adj:
            degree_all = sbuf(c_adj, "degree_all", [128, N])
            counts = sbuf(c_adj, "counts", [TP, NT, NE])
            degree = sbuf(c_adj, "degree", [TP, NT])
            c_sums = ExitStack()
            sums = sbuf(c_sums, "sums", [TP, NT, AW], side="right")
            with ExitStack() as c:
                edges = sbuf(c, "edges", [128, NC, R])
                iota_src = sbuf(c, "iota_src", [128, N], F16)
                dst_hot = sbuf(c, "dst_hot", [128, 2, GJ, TP], BF16)
                src_hot = sbuf(c, "src_hot", [128, 2, GJ, AW], BF16)
                with Stage("edges_in", "pool_step", "hot_ready", "sums_ready", "banks_free", "dve_chain") as (
                        block, edges_in, pool_step, hot_ready, sums_ready, banks_free, dve_chain):
                    @block.sync
                    def _(sp):
                        sp.dma_start(edges[:], edge_table.rearrange("(p c) r -> p c r", c=NC)).then_inc(edges_in, 16)

                    @block.gpsimd
                    def _(pool):
                        pool.iota(iota_src[:], [[1, N]], 0, 0, allow_small_or_imprecise_dtypes=True)
                        pool.memset(src_hot[:], 0.0)
                        pool.memset(sums[:], 0.0).then_inc(pool_step, 1)

                    def build_hot(dve, n, s):
                        ed = edges[:, bass.ds(GJ * n, GJ), :]
                        dve.tensor_tensor(
                            dst_hot[:, s], iota_tile[:].rearrange("p (o n) -> p o n", o=1).to_broadcast([128, GJ, TP]),
                            ed[:, :, F_DST:F_DST + 1].to_broadcast([128, GJ, TP]), ALU.is_equal)
                        dve.tensor_tensor(
                            src_hot[:, s, :, N:N + NE],
                            iota_tile[:, 0:NE].rearrange("p (o n) -> p o n", o=1).to_broadcast([128, GJ, NE]),
                            ed[:, :, F_TYPE:F_TYPE + 1].to_broadcast([128, GJ, NE]), ALU.is_equal)
                        for j in range(GJ):
                            last = dve.tensor_scalar(
                                src_hot[:, s, j, 0:N], iota_src[:],
                                edges[:, bass.ds(GJ * n + j, 1), F_SRC:F_SRC + 1].rearrange("p a b -> p (a b)"),
                                None, ALU.is_equal)
                        last.then_inc(hot_ready, 1)

                    def add_sums(dve, n, s):
                        dve.wait_ge(sums_ready, n + 1)
                        dve.wait_ge(banks_free, n + 2)
                        tile = dve.value_load(group_tile[0:1, bass.ds(n, 1)], min_val=0, max_val=NT - 1)
                        a = sums[:, bass.ds(tile, 1), :].rearrange("p o (c w) -> p (o c) w", c=3)
                        dve.tensor_tensor(a, ps[0:TP, 3 * s:3 * s + 3, 0:CW], a, ALU.add).then_inc(banks_free, 1)

                    @block.vector
                    def _(dve):
                        dve.wait_ge(edges_in, 16)
                        dve.wait_ge(pool_step, 1)
                        dve.sem_inc(banks_free, 2)
                        dve.tensor_copy(count_row[:], edges[:].bitcast(I32)[:, :, F_DSTREL])
                        build_hot(dve, 0, 0)
                        with dve.Fori(0, NG // 2 - 1) as i:
                            build_hot(dve, 2 * i + 1, 1)
                            add_sums(dve, 2 * i, 0)
                            build_hot(dve, 2 * i + 2, 0)
                            add_sums(dve, 2 * i + 1, 1)
                        build_hot(dve, NG - 1, 1)
                        add_sums(dve, NG - 2, 0)
                        add_sums(dve, NG - 1, 1)

                    @block.tensor
                    def _(pe):
                        with pe.Fori(0, NG // 2) as i:
                            for s in range(2):
                                pe.wait_ge(hot_ready, 2 * i + s + 1)
                                pe.wait_ge(banks_free, 2 * i + s + 1)
                                for w in range(3):
                                    for j in range(GJ):
                                        last = pe.matmul(ps[0:TP, 3 * s + w, 0:CW], dst_hot[:, s, j, :],
                                                         src_hot[:, s, j, w * CW:(w + 1) * CW],
                                                         start=j == 0, stop=j == GJ - 1)
                                last.then_inc(sums_ready, 1)

            c_diag = ExitStack()
            degree_diag = sbuf(c_diag, "degree_diag", [TP, NT, TP])
            with Stage("dve_chain", "counts_ready", "counts_out", "diag_ready", "degree_ready") as (
                    block, dve_chain, counts_ready, counts_out, diag_ready, degree_ready):
                @block.vector
                def _(dve):
                    link = chain(dve, dve_chain)
                    dve.tensor_reduce(degree[:], sums[:, :, N:N + NE], AX.X, ALU.add)
                    link(dve.tensor_scalar(counts[:], sums[:, :, N:N + NE], 1.0, None, ALU.max))
                    dve.reciprocal(counts[:], counts[:]).then_inc(counts_ready, 1)
                    link(dve.tensor_scalar(degree[:], degree[:], 1.0, None, ALU.max))
                    link(dve.reciprocal(rdeg[:], degree[:]))
                    for t in range(NT):
                        last = dve.tensor_scalar(degree_diag[:, t, :], ident[0:TP, 0:TP], rdeg[:, t:t + 1], None, ALU.mult)
                    last.then_inc(diag_ready, 1)
                    dve.wait_ge(degree_ready, 1)
                    for t in range(NT):
                        dve.tensor_copy(degree_all[:, tile_of(t)], ps[:, t // 4, (t % 4) * TP:(t % 4 + 1) * TP])

                @block.tensor
                def _(pe):
                    pe.wait_ge(diag_ready, 1)
                    for t in range(NT):
                        last = pe.matmul(ps[:, t // 4, (t % 4) * TP:(t % 4 + 1) * TP], ones[0:TP, :], degree_diag[:, t, :],
                                         start=True, stop=True)
                    last.then_inc(degree_ready, 1)

                @block.sync
                def _(sp):
                    sp.wait_ge(counts_ready, 1)
                    sp.dma_start(count_table.rearrange("(t p r) o -> p t (r o)", p=TP, r=NE), counts[:]).then_inc(counts_out, 16)
                    sp.wait_ge(counts_out, 16)

            c_diag.close()
            adj = sbuf(c_adj, "adj", [TP, NT, N], F16)
            spans = [(i, j, min(j + 4, NT)) for j in range(0, NT, 4) for i in range(NT)]

            def turn_blocks(pe, u, b):
                i, j0, j1 = spans[u]
                for j in range(j0, j1):
                    last = pe.transpose(ps[0:TP, b, (j - j0) * TP:(j - j0 + 1) * TP], sums[:, i, tile_of(j)],
                                        ident[0:TP, 0:TP])
                return last

            def put_blocks(act, u, b, link):
                i, j0, j1 = spans[u]
                return act.activation(adj[:, j0:j1, tile_of(i)],
                                      ps[0:TP, b, 0:(j1 - j0) * TP].rearrange("p (j n) -> p j n", j=j1 - j0), ACT.Copy)
            gemm(len(spans), turn_blocks, put_blocks)
            c_sums.close()
            xs = sbuf(c_adj, "xs", [TP, 2, NT, D], F16)

            def aggregate(dstT, others, op):
                def products(pe, u, b):
                    f, (lo, n) = u // 3, CHUNKS[u % 3]
                    for t in range(NT):
                        for part in range(2):
                            last = pe.matmul(ps[:, b, 0:n], xs[:, part, t, f * 128:(f + 1) * 128], adj[:, t, lo:lo + n],
                                             start=t + part == 0, stop=t == NT - 1 and part == 1)
                    return last

                def evac(dve, u, b, link):
                    f, (lo, n) = u // 3, CHUNKS[u % 3]
                    g, v = staging[:, u % 4, 0:n], ps[:, b, 0:n]
                    for other in others(f, lo, n):
                        link(dve.tensor_tensor(g, v, other, op))
                        v = g
                    link(dve.tensor_copy(dstT[:, 0, f, lo:lo + n], g))
                    return dve.tensor_tensor(dstT[:, 1, f, lo:lo + n], g, dstT[:, 0, f, lo:lo + n], ALU.subtract)
                gemm(12, products, evac, evac_on="vector")

            transposes(xn, xT, KD, tokens=xs)
            with ExitStack() as c:
                aggT = sbuf(c, "aggT", [128, 2, KD, N], F16)
                squares = sbuf(c, "squares", [TP, 4, D])
                norm = sbuf(c, "norm", [TP, NT])
                for l in range(3):
                    ws, wn = first[f"L0_self{l}"], first[f"L0_neigh{l}"]
                    aggregate(aggT, lambda f, lo, n: [degree_all[:, lo:lo + n]], ALU.mult)

                    def products(pe, t, b):
                        tok_product(pe, bank(b), xT, t, ring.mat(ws), KD, f"L0_b{l}", stop=False)
                        return tok_product(pe, bank(b), aggT, t, ring.mat(wn), KD, start=False)

                    gemm(NT, products, lambda act, t, b, link: act.activation(xn[:, t, :], bank(b), ACT.Relu),
                         lambda dve, t, b, link: dve.tensor_tensor_reduce(
                             out=squares[:, t % 4, :], in0=xn[:, t, :], in1=xn[:, t, :], scale=1.0, scalar=0.0,
                             op0=ALU.mult, op1=ALU.add, accum_out=norm[:, t:t + 1]),
                         weights={0: [ws, wn]}, frees={NT - 1: 2})
                    with Stage("root_ready", "dve_chain") as (block, root_ready, dve_chain):
                        @block.scalar
                        def _(act):
                            act.activation(norm[:], norm[:], ACT.Sqrt).then_inc(root_ready, 1)

                        @block.vector
                        def _(dve):
                            link = chain(dve, dve_chain)
                            dve.wait_ge(root_ready, 1)
                            link(dve.tensor_scalar(norm[:], norm[:], 1e-12, None, ALU.max))
                            link(dve.reciprocal(norm[:], norm[:]))
                            for t in range(NT):
                                if l < 2:
                                    dve.tensor_scalar(xn[:, t, :], xn[:, t, :], norm[:, t:t + 1], None, ALU.mult)
                                else:
                                    dve.scalar_tensor_tensor(out=x[:, t, :], in0=xn[:, t, :], scalar=norm[:, t:t + 1],
                                                             in1=x[:, t, :], op0=ALU.mult, op1=ALU.add)
                    if l < 2:
                        transposes(xn, xT, KD, tokens=xs)

            layernorm_T(x, xn, xT)
            with ExitStack() as c:
                share = sbuf(c, "share", [TP, NT, NE])
                col_sum = sbuf(c, "col_sum", [TP, NE])
                row_sum = sbuf(c, "row_sum", [TP, NT])
                gT = sbuf(c, "gT", [NE, N])
                left = sbuf(c, "left", [NE, N])
                picked = sbuf(c, "picked", [NE, N])
                tied = sbuf(c, "tied", [NE, N])
                order = sbuf(c, "order", [NE, N])
                one_row = sbuf(c, "one_row8", [NE, N])
                top = sbuf(c, "top", [NE, 8])
                above = sbuf(c, "above", [NE, 1])
                n_picks = sbuf(c, "n_picks", [TP, NT])
                sel = sbuf(c, "sel", [TP, NT, 2, NE])
                wt = sbuf(c, "wt", [TP, NT, NE])
                g0 = GATE0["L0_gate"]
                gemm(NT, lambda pe, t, b: tok_product(pe, ps[0:TP, b, 0:NE], xT, t, gatew[:, :, g0:g0 + 4, :], KD),
                     lambda dve, t, b, link: dve.tensor_scalar(share[:, t, :], ps[0:TP, b, 0:NE], 1e-10, None, ALU.max),
                     evac_on="vector")
                with Stage("plan_ready", "sums_ready", "dve_chain") as (block, plan_ready, sums_ready, dve_chain):
                    @block.tensor
                    def _(pe):
                        with pe.Fori(0, 8) as i:
                            pe.wait_ge(plan_ready, i + 1)
                            pe.matmul(ps[0:TP, 0, 0:NT * NE], ones[0:TP, 0:TP], share[:].rearrange("p t e -> p (t e)"),
                                      start=True, stop=True).then_inc(sums_ready, 1)

                    @block.vector
                    def _(dve):
                        dve.sem_inc(plan_ready, 1)
                        with dve.Fori(0, 8) as i:
                            link = chain(dve, dve_chain, 5 * i)
                            dve.wait_ge(sums_ready, i + 1)
                            link(dve.tensor_reduce(col_sum[:], ps[0:TP, 0, 0:NT * NE].rearrange("p (t e) -> p e t", e=NE),
                                                   AX.X, ALU.add))
                            link(dve.reciprocal(col_sum[:], col_sum[:]))
                            link(dve.tensor_tensor(share[:], share[:], col_sum[:].rearrange("p (o e) -> p o e", o=1)
                                                   .to_broadcast([TP, NT, NE]), ALU.mult))
                            link(dve.tensor_reduce(row_sum[:], share[:], AX.X, ALU.add))
                            link(dve.reciprocal(row_sum[:], row_sum[:]))
                            dve.tensor_tensor(share[:], share[:], row_sum[:].rearrange("p (t o) -> p t o", o=1)
                                              .to_broadcast([TP, NT, NE]), ALU.mult).then_inc(plan_ready, 1)

                def plan_T(pe, t, b):
                    return pe.transpose(ps[0:NE, b, 0:TP], share[:, t, :], ident[0:TP, 0:TP])
                gemm(NT, plan_T, lambda act, t, b, link: act.activation(gT[:, tile_of(t)], ps[0:NE, b, 0:TP], ACT.Copy))
                with Stage("dve_chain",) as (block, dve_chain):
                    @block.vector
                    def _(dve):
                        link = chain(dve, dve_chain)
                        dve.memset(one_row[:], 1.0)
                        link(dve.tensor_copy(left[:], gT[:]))
                        for r in range((CAP - 1) // 8):
                            link(dve.max(top[:], left[:]))
                            link(dve.match_replace(left[:], top[:], left[:], -1e30))
                        link(dve.max(top[:], left[:]))
                        limit = top[:, (CAP - 1) % 8:(CAP - 1) % 8 + 1]
                        link(dve.tensor_scalar(picked[:], gT[:], limit, None, ALU.is_gt))
                        dve.tensor_reduce(above[:], picked[:], AX.X, ALU.add)
                        link(dve.tensor_scalar(tied[:], gT[:], limit, None, ALU.is_equal))
                        link(dve.tensor_scalar(above[:], above[:], -1.0, float(CAP), ALU.mult, ALU.add))
                        link(dve.tensor_tensor_scan(out=order[:], data0=one_row[:], data1=tied[:], initial=0.0,
                                                    op0=ALU.mult, op1=ALU.add))
                        link(dve.scalar_tensor_tensor(out=tied[:], in0=order[:], scalar=above[:, 0:1], in1=tied[:],
                                                      op0=ALU.is_le, op1=ALU.mult))
                        link(dve.tensor_tensor(picked[:], picked[:], tied[:], ALU.add))
                        dve.scalar_tensor_tensor(out=order[:], in0=gT[:], scalar=0.5, in1=picked[:],
                                                 op0=ALU.is_gt, op1=ALU.mult)

                def picks_back(pe, t, b):
                    pe.transpose(ps[0:TP, b, 0:NE], picked[:, tile_of(t)], ident[0:NE, 0:NE])
                    return pe.transpose(ps[0:TP, b, NE:2 * NE], order[:, tile_of(t)], ident[0:NE, 0:NE])
                gemm(NT, picks_back, lambda act, t, b, link: act.activation(
                    sel[:, t], ps[0:TP, b, 0:2 * NE].rearrange("p (a e) -> p a e", a=2), ACT.Copy))
                with Stage("dve_chain",) as (block, dve_chain):
                    @block.vector
                    def _(dve):
                        link = chain(dve, dve_chain)
                        link(dve.tensor_reduce(n_picks[:], sel[:, :, 0, :], AX.X, ALU.add))
                        link(dve.tensor_scalar(n_picks[:], n_picks[:], 1.0, None, ALU.add))
                        link(dve.reciprocal(n_picks[:], n_picks[:]))
                        dve.tensor_tensor(wt[:], sel[:, :, 1, :], n_picks[:].rearrange("p (t o) -> p t o", o=1)
                                          .to_broadcast([TP, NT, NE]), ALU.mult)

                def expert_products(n0, W, evac_on, evac, store=None, extra=None):
                    turns, per = NE // SLOTS, NT * SLOTS
                    with Stage("product_ready", "banks_free", "stored0", "stored1", "stored2", "stored3") as (
                            block, product_ready, banks_free, *stored):
                        if extra:
                            extra(block)

                        @block.sync
                        def _(sp):
                            ring.issue(sp, n0 + 2 * SLOTS)
                            with sp.Fori(0, turns - 2) as i:
                                for j in range(SLOTS):
                                    sp.wait_ge(ring.split_done, n0 + SLOTS + j + 1 + SLOTS * i)
                                    sp.dma_start(ring.raw[:, (n0 + j) % SLOTS, :].rearrange("p (k n) -> p k n", k=4),
                                                 W[bass.ds(SLOTS * i + 2 * SLOTS + j, 1)].rearrange(
                                        "o (k p) n -> p (o k) n", p=128)).then_inc(ring.loaded[(n0 + j) % SLOTS], 16)

                        def tensor_turn(pe, i):
                            for j in range(SLOTS):
                                pe.wait_ge(ring.split_done, n0 + j + 1 + SLOTS * i)
                                for t in range(NT):
                                    u = NT * j + t
                                    pe.wait_ge(banks_free, per * i + u + 1)
                                    tok_product(pe, bank(u % 4), xT, t, ring.mat(n0 + j), KD).then_inc(product_ready, 1)

                        @block.tensor
                        def _(pe):
                            with pe.Fori(0, turns) as i:
                                tensor_turn(pe, i)

                        def split_next(eng, vector, j, i):
                            n = n0 + SLOTS + j
                            if vector:
                                ring.low_of(eng, n, SLOTS * i)
                            else:
                                ring.high_of(eng, n, i, 16 * i)

                        def drain_turn(eng, i, more):
                            vector = evac_on == "vector"
                            for j in range(SLOTS):
                                for t in range(NT):
                                    u = NT * j + t
                                    eng.wait_ge(product_ready, per * i + u + 1)
                                    evac(eng, t, u, SLOTS * i + j, i, stored).then_inc(banks_free, 1)
                                    if store:
                                        store(eng, t, u, i, stored, banks_free)
                                    if t == 1 and j >= 1 and more:
                                        split_next(eng, vector, j - 1, i)
                                eng.sem_inc(ring.freed[(n0 + j) % SLOTS], 1)
                            if more:
                                split_next(eng, vector, SLOTS - 1, i)

                        def drain(eng):
                            (ring.split_low if evac_on == "vector" else ring.split_high)(eng, n0 + SLOTS)
                            eng.sem_inc(banks_free, 4)
                            if store:
                                for q in stored:
                                    eng.sem_inc(q, 16)
                            with eng.Fori(0, turns - 1) as i:
                                drain_turn(eng, i, True)
                            drain_turn(eng, turns - 1, False)
                            if store:
                                for q in stored:
                                    eng.wait_ge(q, 16 * (NT * NE // 4 + 1))

                        def other(eng):
                            (ring.split_high if evac_on == "vector" else ring.split_low)(eng, n0 + SLOTS)
                            with eng.Fori(0, turns - 1) as i:
                                for j in range(SLOTS):
                                    split_next(eng, evac_on != "vector", j, i)
                        if evac_on == "vector":
                            block.vector(drain)
                            block.scalar(other)
                        else:
                            block.scalar(drain)
                            block.vector(other)
                    ring.issued = ring.high = ring.low = ring.used = n0 + NE

                def add_expert(dve, t, u, e, i, stored):
                    return dve.scalar_tensor_tensor(
                        out=x[:, t, :], in0=bank(u % 4), scalar=wt[:, t, bass.ds(e, 1)], in1=x[:, t, :],
                        op0=ALU.mult, op1=ALU.add)
                expert_products(first["L0_exp"], I["L0_ffn_experts"], "vector", add_expert,
                                extra=gather_counts(c, 0, NC // SC // 2))

            layernorm_T(x, xn, xT, tokens=xs)
            with ExitStack() as c:
                sT = sbuf(c, "sT", [128, 2, KD, N], F16)
                hT = sbuf(c, "hT", [128, 2, KD, N], F16)
                aggregate(sT, lambda f, lo, n: [xT[:, 0, f, lo:lo + n], xT[:, 1, f, lo:lo + n]], ALU.add)
                n1 = first["L1_W1"]
                pr, dst, src_of = feat_units(n1, hT, sT, KD)
                cb = COL0["L1_gnn_b1"]
                gemm(12, pr, *split_evac(ACT.Relu, src_of, pair_of(hT), lambda u: cols[:, cb + u // 3:cb + u // 3 + 1]),
                     weights={0: [n1]}, frees={11: 1})
                dense(hT, first["L1_W2"], x, row="L1_gnn_b2", add=x)

        with ExitStack() as c:
            qT = sbuf(c, "qT1", [128, KD, N])
            k = sbuf(c, "k1", [TP, NT, D])
            vo = sbuf(c, "vo1", [TP, NT, 4, VW])
            peak = sbuf(c, "peak", [128, KD])
            col_scale = sbuf(c, "col_scale", [128, KD])
            n0 = first["L1_qkv"]
            with ExitStack() as c2:
                q = sbuf(c2, "q1", [TP, NT, D])
                qmax = sbuf(c2, "qmax", [TP, NT, H])

                def q_minus_max(dve, t, b, link):
                    v = bank(b).rearrange("p (h d) -> p h d", h=H)
                    link(dve.tensor_reduce(qmax[:, t, :], v, AX.X, ALU.max))
                    return dve.tensor_tensor(q[:, t, :].rearrange("p (h d) -> p h d", h=H), v,
                                             qmax[:, t, :].rearrange("p (h o) -> p h o", o=1).to_broadcast([TP, H, HD]),
                                             ALU.subtract)
                gemm(NT, lambda pe, t, b: tok_product(pe, bank(b), xT, t, ring.mat(n0), KD), q_minus_max,
                     lambda act, t, b, link: act.activation(q[:, t, :], q[:, t, :], ACT.Exp),
                     evac_on="vector", weights={0: [n0]}, frees={NT - 1: 1})
                transposes(q, qT, KD)
            with ExitStack() as c2:
                kT = sbuf(c2, "kT1", [128, KD, N])
                ebuf = sbuf(c2, "ebuf1", [128, 4, D])
                pr, dst, src_of = feat_units(n0 + 1, kT, xT, KD)
                ev, fi = elu1(dst, ebuf, src_of)
                gemm(12, pr, ev, fi, weights={0: [n0 + 1]}, frees={11: 1})
                with Stage("peak_ready", "exp_ready", "dve_chain") as (block, peak_ready, exp_ready, dve_chain):
                    @block.vector
                    def _(dve):
                        link = chain(dve, dve_chain)
                        link(dve.tensor_reduce(peak[:], kT[:], AX.X, ALU.max))
                        dve.tensor_scalar(peak[:], peak[:], -1.0, None, ALU.mult).then_inc(peak_ready, 1)
                        dve.wait_ge(exp_ready, 1)
                        dve.reciprocal(col_scale[:], col_scale[:])

                    @block.scalar
                    def _(act):
                        act.wait_ge(peak_ready, 1)
                        for f in range(KD):
                            last = act.activation(kT[:, f, :], kT[:, f, :], ACT.Exp, bias=peak[:, f:f + 1],
                                                  accum_out=col_scale[:, f:f + 1])
                        last.then_inc(exp_ready, 1)

                def back(pe, t, b):
                    for f in range(KD):
                        last = pe.transpose(ps[0:TP, b, f * 128:(f + 1) * 128], kT[:, f, tile_of(t)], ident[:, :])
                    return last
                gemm(NT, back, lambda act, t, b, link: act.activation(k[:, t, :], bank(b), ACT.Copy))
            values(vo, xT, n0 + 2)
            kv_and_apply(c, qT, k, vo, 0.0, to=k, col_scale=col_scale, den_ones=True)
            aT = qT[:].rearrange("p k n -> p (k n)").bitcast(F16).rearrange("p (s k n) -> p s k n", s=2, k=KD)
            transposes(k, aT, KD)
            dense(aT, first["L1_proj"], x, row="L1_mix_b", add=x)

        def top_two(c, gate, bias_row, srcT, blocks, comb, softmax_first):
            lg = sbuf(c, "logits", [TP, NT, NE])
            eq = sbuf(c, "tie", [TP, NT, NE])
            pre = sbuf(c, "ties_before", [TP, NT, NE])
            pk = sbuf(c, "picks", [TP, NT, 2, NE])
            m = sbuf(c, "top_values", [TP, 2, NT])
            w = sbuf(c, "pick_weights", [TP, 2, NT])
            g0 = GATE0[gate]
            gemm(NT, lambda pe, t, b: tok_product(pe, ps[0:TP, b, 0:NE], srcT, t, gatew[:, :, g0:g0 + blocks, :], blocks),
                 lambda dve, t, b, link: dve.tensor_tensor(lg[:, t, :], ps[0:TP, b, 0:NE], gateb[0:TP, bias_row, :], ALU.add),
                 evac_on="vector")

            def spread(v):
                return v.rearrange("p (t o) -> p t o", o=1).to_broadcast([TP, NT, NE])

            with Stage("dve_chain", "ready_for_exp", "exp_ready") as (block, dve_chain, ready_for_exp, exp_ready):
                @block.vector
                def _(dve):
                    link = chain(dve, dve_chain)
                    n_exp = 0
                    if softmax_first:
                        link(dve.tensor_reduce(m[:, 0, :], lg[:], AX.X, ALU.max))
                        dve.tensor_tensor(lg[:], lg[:], spread(m[:, 0, :]), ALU.subtract).then_inc(ready_for_exp, 1)
                        n_exp += 1
                        dve.wait_ge(exp_ready, n_exp)
                        link(dve.tensor_reduce(m[:, 0, :], lg[:], AX.X, ALU.add))
                        link(dve.reciprocal(m[:, 0, :], m[:, 0, :]))
                        link(dve.tensor_tensor(lg[:], lg[:], spread(m[:, 0, :]), ALU.mult))
                    for r in range(2):
                        link(dve.tensor_reduce(m[:, r, :], lg[:], AX.X, ALU.max))
                        dve.memset(pre[:], 0.0)
                        link(dve.tensor_tensor(eq[:], lg[:], spread(m[:, r, :]), ALU.is_equal))
                        for e in range(1, NE):
                            link(dve.tensor_tensor(pre[:, :, e], pre[:, :, e - 1], eq[:, :, e - 1], ALU.add))
                        link(dve.scalar_tensor_tensor(out=pk[:, :, r, :], in0=pre[:], scalar=0.0, in1=eq[:],
                                                      op0=ALU.is_equal, op1=ALU.mult))
                        if r == 0:
                            link(dve.scalar_tensor_tensor(out=lg[:], in0=pk[:, :, 0, :], scalar=-1e30, in1=lg[:],
                                                          op0=ALU.mult, op1=ALU.add))
                    dve.tensor_tensor(w[:, 1, :], m[:, 1, :], m[:, 0, :], ALU.subtract).then_inc(ready_for_exp, 1)
                    dve.wait_ge(exp_ready, n_exp + 1)
                    link(dve.tensor_scalar(w[:, 0, :], w[:, 1, :], 1.0, None, ALU.add))
                    link(dve.reciprocal(w[:, 0, :], w[:, 0, :]))
                    link(dve.tensor_tensor(w[:, 1, :], w[:, 1, :], w[:, 0, :], ALU.mult))
                    link(dve.tensor_tensor(comb[:], pk[:, :, 0, :], spread(w[:, 0, :]), ALU.mult))
                    link(dve.tensor_tensor(eq[:], pk[:, :, 1, :], spread(w[:, 1, :]), ALU.mult))
                    dve.tensor_tensor(comb[:], comb[:], eq[:], ALU.add)

                @block.scalar
                def _(act):
                    n_exp = 0
                    if softmax_first:
                        act.wait_ge(ready_for_exp, 1)
                        act.activation(lg[:], lg[:], ACT.Exp).then_inc(exp_ready, 1)
                        n_exp += 1
                    act.wait_ge(ready_for_exp, n_exp + 1)
                    act.activation(w[:, 1, :], w[:, 1, :], ACT.Exp).then_inc(exp_ready, 1)

        def add_expert_biases(c, comb, which):
            combT = sbuf(c, "combT", [NE, N])
            gemm(NT, lambda pe, t, b: pe.transpose(ps[0:NE, b, 0:TP], comb[:, t, :], ident[0:TP, 0:TP]),
                 lambda act, t, b, link: act.activation(combT[:, tile_of(t)], ps[0:NE, b, 0:TP], ACT.Copy))
            gemm(NT, lambda pe, t, b: pe.matmul(bank(b), combT[:, tile_of(t)], expert_b2[:, which, :], start=True, stop=True),
                 add_to_x, evac_on="vector")

        def experts(c, n0, items, comb, expert_of, func, col, fb, per, up, down, reload, extra=None):
            turn = SLOTS // per
            turns = items // turn
            units = 3 * fb
            order = [(f, ch) for ch in range(3) for f in range(fb)]
            last_unit = [fb * (1 + sum(lo + n <= TP * t + TP - 1 for lo, n in CHUNKS)) for t in range(NT)]
            n_dma = len(ring.loads[n0])
            hT = sbuf(c, "hidden", [128, 2, fb, N], F16)
            bias_now = sbuf(c, "bias_now", [128, turn, fb])
            with Stage("feat_ready", "feat_drained", "hidden_ready", "out_ready", "out_free", "bias_ready",
                       "act_chain") as (block, feat_ready, feat_drained, hidden_ready, out_ready, out_free, bias_ready,
                                           act_chain):
                if extra:
                    extra(block)

                @block.sync
                def _(sp):
                    ring.issue(sp, n0 + 2 * SLOTS)
                    with sp.Fori(0, turns - 2) as i:
                        for s in range(turn):
                            for j in range(per):
                                n = n0 + per * s + j
                                sp.wait_ge(ring.split_done, n + SLOTS + 1 + SLOTS * i)
                                reload(sp, turn * i + 2 * turn + s, n, j)

                @block.tensor
                def _(pe):
                    with pe.Fori(0, turns) as i:
                        for s in range(turn):
                            n = n0 + per * s
                            pe.wait_ge(ring.split_done, n + 1 + SLOTS * i)
                            for q, (f, ch) in enumerate(order):
                                lo, w = CHUNKS[ch]
                                v = units * s + q
                                pe.wait_ge(feat_drained, units * turn * i + v + 1)
                                feat_product(pe, ps[:, v % 4, 0:w], up(n), f, xT, lo, w, KD).then_inc(feat_ready, 1)
                            if per > 1:
                                pe.wait_ge(ring.split_done, n + 2 + SLOTS * i)
                            for t in range(NT):
                                v = NT * s + t
                                pe.wait_ge(hidden_ready, units * (turn * i + s) + min(last_unit[t], units) + 4)
                                pe.wait_ge(out_free, NT * turn * i + v + 1)
                                tok_product(pe, bank(4 + v % 4), hT, t, down(n), fb).then_inc(out_ready, 1)

                def act_turn(act, i, more):
                    for s in range(turn):
                        act.activation(bias_now[:, s, :], cols[:, bass.ds(fb * turn * i + (col + fb * s), fb)],
                                       ACT.Copy).then_inc(bias_ready, 1)
                        act.wait_ge(bias_ready, turn * i + s + 1)
                        link = chain(act, act_chain, units * (turn * i + s))
                        for q, (f, ch) in enumerate(order):
                            lo, w = CHUNKS[ch]
                            v = units * s + q
                            act.wait_ge(feat_ready, units * turn * i + v + 1)
                            act.wait_ge(hidden_ready, units * turn * i + v + 1)
                            link(act.activation(staging[:, v % 4, 0:w], ps[:, v % 4, 0:w], func, bias=bias_now[:, s, f:f + 1]))
                            act.activation(hT[:, 0, f, lo:lo + w], staging[:, v % 4, 0:w], ACT.Copy).then_inc(feat_drained, 1)
                        if per > 1:
                            act.sem_inc(ring.freed[n0 % SLOTS], 1)
                        if more:
                            for j in range(per):
                                n = n0 + per * s + j
                                ring.high_of(act, n + SLOTS, i, 16 * n_dma * i)

                def dve_turn(dve, i, more):
                    for s in range(turn):
                        for q, (f, ch) in enumerate(order):
                            lo, w = CHUNKS[ch]
                            v = units * s + q
                            dve.wait_ge(feat_drained, units * turn * i + v + 1 + 4)
                            dve.tensor_tensor(hT[:, 1, f, lo:lo + w], staging[:, v % 4, 0:w], hT[:, 0, f, lo:lo + w],
                                              ALU.subtract).then_inc(hidden_ready, 1)
                        for t in range(NT):
                            v = NT * s + t
                            dve.wait_ge(out_ready, NT * turn * i + v + 1)
                            dve.scalar_tensor_tensor(out=x[:, t, :], in0=bank(4 + v % 4),
                                                     scalar=comb[:, t, bass.ds(expert_of(turn * i + s), 1)], in1=x[:, t, :],
                                                     op0=ALU.mult, op1=ALU.add).then_inc(out_free, 1)
                            if t == 2 and per > 1 and more:
                                ring.low_of(dve, n0 + SLOTS, SLOTS * i)
                        dve.sem_inc(ring.freed[(n0 + per * s + per - 1) % SLOTS], 1)
                        if more:
                            ring.low_of(dve, n0 + per * s + per - 1 + SLOTS, SLOTS * i)

                @block.scalar
                def _(act):
                    ring.split_high(act, n0 + SLOTS)
                    act.sem_inc(feat_drained, 4)
                    with act.Fori(0, turns - 1) as i:
                        act_turn(act, i, True)
                    act_turn(act, turns - 1, False)

                @block.vector
                def _(dve):
                    ring.split_low(dve, n0 + SLOTS)
                    dve.sem_inc(hidden_ready, 4)
                    dve.sem_inc(out_free, 4)
                    with dve.Fori(0, turns - 1) as i:
                        dve_turn(dve, i, True)
                    dve_turn(dve, turns - 1, False)
            ring.issued = ring.high = ring.low = ring.used = n0 + items * per

        layernorm_T(x, xn, xT)
        with ExitStack() as c:
            comb = sbuf(c, "comb1", [TP, NT, NE])
            top_two(c, "L1_Wg", 0, xT, 4, comb, False)
            add_expert_biases(c, comb, 0)

            def reload_pair(sp, e, n, j):
                for lo, hi, k, W in ((0, 2 * D, 4, I["L1_ffn_W1"]), (2 * D, 4 * D, 2, I["L1_ffn_W2"])):
                    sp.dma_start(ring.raw[:, n % SLOTS, lo:hi].rearrange("p (k n) -> p k n", k=k),
                                 W[bass.ds(e, 1)].rearrange("o (k p) n -> p (o k) n", p=128)
                                 ).then_inc(ring.loaded[n % SLOTS], 16)
            experts(c, first["L1_exp"], NE, comb, lambda e: e, ACT.Relu, COL0["L1_ffn_b1"], 2, 1,
                    lambda n: ring.mat(n, 0, 2 * D), lambda n: ring.mat(n, 2 * D, 4 * D, 2), reload_pair,
                    extra=gather_counts(c, NC // SC // 2, NC // SC // 2))
        def chunk_view(u, b):
            return ps[:, b, 0:CHUNKS[u % 3][1]]

        with ExitStack() as c:
            hT = sbuf(c, "shared_h", [128, 2, 2, N], F16)
            n = first["L1_shared"]
            cb = COL0["L1_bs1"]

            def shared_up(pe, u, b):
                f, (lo, w) = u // 3, CHUNKS[u % 3]
                return feat_product(pe, ps[:, b, 0:w], ring.mat(n, 0, 2 * D), f, xT, lo, w, KD)
            gemm(6, shared_up, *split_evac(ACT.Relu, chunk_view, pair_of(hT), lambda u: cols[:, cb + u // 3:cb + u // 3 + 1]),
                 weights={0: [n]})
            dense(hT, n, x, k_blocks=2, row="L1_bs2", add=x, scale=0.5)

        MB = 4

        def messages(table, word, dest, weight_word, layer):
            assert NG % MB == 0
            with ExitStack() as c:
                edges = sbuf(c, "edges_m", [128, NC, R])
                index = sbuf(c, "index_stage", [128, MB, GJ], I32)
                got = sbuf(c, "gathered", [128, MB, GJ, D])
                hot = sbuf(c, "weighted_hot", [128, MB, GJ, TP])
                ei = edges[:].bitcast(I32)
                rows_in = [ctx.enter_context(nc.semaphore(f"{layer}_rows_in{s}")) for s in range(MB)]
                with Stage("edges_in", "index_ready", "hot_ready", "sums_ready", "banks_free", "dve_chain") as (
                        block, edges_in, index_ready, hot_ready, sums_ready, banks_free, dve_chain):
                    @block.sync
                    def _(sp):
                        sp.dma_start(edges[:], edge_table.rearrange("(p c) r -> p c r", c=NC)).then_inc(edges_in, 16)
                        ring.issue(sp, ring.used + SLOTS)

                    @block.gpsimd
                    def _(pool):
                        with pool.Fori(0, NG // MB) as i:
                            for s in range(MB):
                                pool.wait_ge(index_ready, MB * i + s + 1)
                                pool.sem_inc(loop_turn, 1)
                                for j in range(GJ):
                                    pool.indirect_dma_start(
                                        got[:, s, j, :], None, table,
                                        bass.IndirectOffsetOnAxis(ap=index[:, s, j:j + 1], axis=0)).then_inc(rows_in[s], 16)

                    def prepare(dve, n, s):
                        link = chain(dve, dve_chain, n)
                        dve.wait_ge(sums_ready, n + 1)
                        ed = edges[:, bass.ds(GJ * n, GJ), :]
                        dve.tensor_copy(index[:, s, :], ei[:, bass.ds(GJ * n, GJ), word]).then_inc(index_ready, 1)
                        link(dve.tensor_tensor(
                            hot[:, s], iota_tile[:].rearrange("p (o n) -> p o n", o=1).to_broadcast([128, GJ, TP]),
                            ed[:, :, F_DST:F_DST + 1].to_broadcast([128, GJ, TP]), ALU.is_equal))
                        if weight_word is None:
                            w = count_weight[:, bass.ds(GJ * n, GJ)].rearrange("p (j o) -> p j o", o=1)
                        else:
                            w = ed[:, :, weight_word:weight_word + 1]
                        dve.tensor_tensor(hot[:, s], hot[:, s], w.to_broadcast([128, GJ, TP]), ALU.mult).then_inc(hot_ready, 1)

                    def add_sums(dve, n, s):
                        dve.wait_ge(sums_ready, n + MB + 1)
                        dve.wait_ge(banks_free, n + MB)
                        tile = dve.value_load(group_tile[0:1, bass.ds(n, 1)], min_val=0, max_val=NT - 1)
                        a = dest[:, bass.ds(tile, 1), :].rearrange("p o d -> p (o d)")
                        dve.tensor_tensor(a, bank(s), a, ALU.add).then_inc(banks_free, 1)

                    @block.vector
                    def _(dve):
                        dve.wait_ge(edges_in, 16)
                        dve.sem_inc(banks_free, MB)
                        for n in range(MB - 1):
                            prepare(dve, n, n)
                        with dve.Fori(0, NG // MB - 1) as i:
                            for s in range(MB):
                                prepare(dve, MB * i + s + (MB - 1), (s + MB - 1) % MB)
                                add_sums(dve, MB * i + s, s)
                        prepare(dve, NG - 1, MB - 1)
                        for s in range(MB):
                            add_sums(dve, NG - MB + s, s)

                    @block.tensor
                    def _(pe):
                        pe.sem_inc(sums_ready, MB)
                        with pe.Fori(0, NG // MB) as i:
                            for s in range(MB):
                                pe.wait_ge(hot_ready, MB * i + s + 1)
                                pe.wait_ge(banks_free, MB * i + s + 1)
                                pe.wait_ge(rows_in[s], 16 * GJ * i + 16 * GJ)
                                for j in range(GJ):
                                    last = pe.matmul(bank(s), hot[:, s, j, :], got[:, s, j, :], start=j == 0, stop=j == GJ - 1)
                                last.then_inc(sums_ready, 1)

        layernorm_T(x, xn, xT)
        dense(xT, first["L2_self"], x, row="L2_bias", add=x)
        with ExitStack() as c:
            rel_out = sbuf(c, "rel_out", [TP, 4, D])

            def stage_rows(act, t, u, e, i, stored):
                act.wait_ge(stored[u % 4], 16 * (NT * SLOTS // 4 * i + u // 4) + 16)
                return act.activation(rel_out[:, u % 4, :], bank(u % 4), ACT.Copy)

            def store_rows(act, t, u, i, stored, banks_free):
                act.wait_ge(banks_free, NT * SLOTS * i + u + 5)
                act.dma_start(rel_table[bass.ds(N * SLOTS * i + u * TP, TP), :], rel_out[:, u % 4, :]).then_inc(stored[u % 4], 16)
            expert_products(first["L2_rel"], I["L2_gnn_W_rel"], "scalar", stage_rows, store_rows)
        messages(rel_table, F_RELSRC, x, None, "L2")

        with ExitStack() as c:
            y = sbuf(c, "y", [TP, NT, D])
            yT = sbuf(c, "yT", [128, 2, KD, N], F16)
            layernorm_T(xn, y, yT, scale=COL0["L2_g"], bias=COL0["L2_bt"])
            qT = sbuf(c, "qT2", [128, KD, N])
            vo = sbuf(c, "vo2", [TP, NT, 4, VW])
            neg_qb = sbuf(c, "neg_qb", [128, KD])
            ebuf = sbuf(c, "ebuf2", [128, 4, D])
            cb = COL0["L2_qb"]
            with Stage("negated") as (block, negated):
                @block.vector
                def _(dve):
                    dve.tensor_scalar(neg_qb[:], cols[:, cb:cb + KD], -1.0, None, ALU.mult)
            n0 = first["L2_qkv"]
            elu_q(qT, ebuf, yT, n0, lambda u: (cols[:, cb + u // 3:cb + u // 3 + 1], neg_qb[:, u // 3:u // 3 + 1]))
            elu_k(y, ebuf, yT, n0 + 1, "L2_kb")
            values(vo, yT, n0 + 2, "L2_vb")
            kv_and_apply(c, qT, y, vo, 1e-8, to=y)
            transposes(y, yT, KD)
            dense(yT, first["L2_out"], x, row="L2_out_b", add=x)
            with Stage("added") as (block, added):
                @block.vector
                def _(dve):
                    for t in range(NT):
                        dve.tensor_tensor(x[:, t, :], x[:, t, :], xn[:, t, :], ALU.add)

        layernorm_T(x, xn, xT)
        with ExitStack() as c:
            gh = sbuf(c, "gh", [128, 12, CHUNKS[0][1]])
            gh_sums = sbuf(c, "gh_sums", [128, 12])
            gh_mean = sbuf(c, "gh_mean", [128, KD])
            gh_wide = sbuf(c, "gh_wide", [128, KD, 128])
            g_all = sbuf(c, "g_all", [128, NE])
            gate_full = sbuf(c, "gate_full", [128, KD, NE])
            g_col = sbuf(c, "g_col", [NE, 1])
            g_wide = sbuf(c, "g_wide", [NE, TP])
            b1m = sbuf(c, "b1m", [128, 2])
            merged = sbuf(c, "merged", [128, 4 * D])
            tv_rows = sbuf(c, "tv_rows", [NE, 3, D])
            b2_all = sbuf(c, "b2_all", [TP, D])
            lng_all = sbuf(c, "lng_all", [TP, D])
            lnb_all = sbuf(c, "lnb_all", [TP, D])
            hT = sbuf(c, "h2T", [128, 2, 2, N], F16)
            merged_split = sbuf(c, "merged_split", [128, 2, 4 * D], F16)
            res = sbuf(c, "res", [TP, NT, D])
            n0 = first["L2_gfc1"]
            cb = COL0["L2_gfc1_b"]
            pr, _dst, src_of = feat_units(n0, None, xT, KD)
            gemm(12, pr, lambda act, u, b, link: act.activation(
                gh[:, u, 0:CHUNKS[u % 3][1]], src_of(u, b), ACT.Relu, bias=cols[:, cb + u // 3:cb + u // 3 + 1],
                accum_out=gh_sums[:, u:u + 1]),
                weights={0: [n0]}, frees={11: 1})
            nb, nt = first["L2_base"], first["L2_tv"]

            def skip_split(dve, n):
                dve.sem_inc(ring.high_done, 1)
                dve.sem_inc(ring.split_done, 1)
                dve.sem_inc(ring.freed[n % SLOTS], 1)

            with Stage("tv_in", "mean_ready", "gate_ready", "wide_ready", "rows_ready", "dve_chain", "merged_ready",
                       "merged_high", "gate_in") as (block, tv_in, mean_ready, gate_ready, wide_ready, rows_ready, dve_chain,
                                          merged_ready, merged_high, gate_in):
                @block.scalar
                def _(act):
                    act.wait_ge(merged_ready, 1)
                    act.activation(merged_split[:, 0, :], merged[:], ACT.Copy).then_inc(merged_high, 1)

                g0 = GATE0["L2_gfc2"]

                @block.sync
                def _(sp):
                    sp.dma_start(gate_full[:], I["gatew"][:, g0:g0 + KD, :]).then_inc(gate_in, 16)
                    for r, nme in enumerate(("L2_ffn_tv_b2", "L2_ffn_tv_ln_g", "L2_ffn_tv_ln_b")):
                        sp.dma_start(tv_rows[:, r, :], I[nme]).then_inc(tv_in, 16)
                    ring.issue(sp, nb + 1 + NE + SLOTS, over_plain=True)

                @block.vector
                def _(dve):
                    link = chain(dve, dve_chain)
                    link(dve.tensor_reduce(gh_mean[:], gh_sums[:].rearrange("p (f c) -> p f c", c=3), AX.X, ALU.add))
                    link(dve.tensor_scalar(gh_mean[:], gh_mean[:], 1.0 / N, None, ALU.mult))
                    for k in range(KD):
                        last = dve.tensor_scalar(gh_wide[:, k, :], ones[:, :], gh_mean[:, k:k + 1], None, ALU.mult)
                    last.then_inc(mean_ready, 1)
                    dve.wait_ge(gate_ready, 1)
                    link(dve.tensor_tensor(g_all[:], ps[:, 0, 0:NE], gateb[:, 2, :], ALU.add))
                    link(dve.tensor_tensor(g_col[:], ps[0:NE, 1, 0:1], gfc2_col[:], ALU.add))
                    dve.tensor_scalar(g_wide[:], ones[0:NE, 0:TP], g_col[:, 0:1], None, ALU.mult).then_inc(wide_ready, 1)
                    link(dve.tensor_copy(b1m[:], cols[:, COL0["L2_b1"]:COL0["L2_b1"] + 2]))
                    for e in range(NE):
                        cc = COL0["L2_tv_b1"] + 2 * e
                        link(dve.scalar_tensor_tensor(out=b1m[:], in0=cols[:, cc:cc + 2], scalar=g_all[:, e:e + 1],
                                                      in1=b1m[:], op0=ALU.mult, op1=ALU.add))
                    dve.wait_ge(ring.loaded[nb % SLOTS], ring.count[nb])
                    link(dve.tensor_copy(merged[:], ring.raw[:, nb % SLOTS, :]))
                    skip_split(dve, nb)
                    for e in range(NE):
                        dve.wait_ge(ring.loaded[(nt + e) % SLOTS], ring.count[nt + e])
                        link(dve.scalar_tensor_tensor(out=merged[:], in0=ring.raw[:, (nt + e) % SLOTS, :],
                                                      scalar=g_all[:, e:e + 1], in1=merged[:], op0=ALU.mult, op1=ALU.add))
                        skip_split(dve, nt + e)
                    dve.sem_inc(merged_ready, 1)
                    dve.wait_ge(merged_high, 1)
                    dve.tensor_tensor(merged_split[:, 1, :], merged[:], merged_split[:, 0, :], ALU.subtract)
                    dve.wait_ge(rows_ready, 1)
                    dve.tensor_copy(b2_all[:], bank(2))
                    for dst, a, b in ((lng_all, 3, 4), (lnb_all, 5, 6)):
                        link(dve.tensor_scalar(dst[:], bank(b), 0.03, None, ALU.mult))
                        dve.scalar_tensor_tensor(out=dst[:], in0=bank(a), scalar=1.0 - 0.03 * NE, in1=dst[:],
                                                 op0=ALU.mult, op1=ALU.add)

                @block.tensor
                def _(pe):
                    pe.wait_ge(mean_ready, 1)
                    pe.wait_ge(gate_in, 16)
                    for k in range(KD):
                        pe.matmul(ps[:, 0, 0:NE], gh_wide[:, k, :], gate_full[:, k, :], start=k == 0, stop=k == KD - 1)
                    for k in range(KD):
                        last = pe.matmul(ps[0:NE, 1, 0:1], gate_full[:, k, :], gh_mean[:, k:k + 1], start=k == 0, stop=k == KD - 1)
                    last.then_inc(gate_ready, 1)
                    pe.wait_ge(wide_ready, 1)
                    pe.wait_ge(tv_in, 48)
                    pe.matmul(bank(2), g_wide[:, :], tv_rows[:, 0, :], start=True, stop=False)
                    for bk, name in ((2, "L2_b2"), (3, "L2_ln_g"), (5, "L2_ln_b")):
                        for part in range(2):
                            pe.matmul(bank(bk), pick[:, ROWS.index(name), :], rows[:, part, :],
                                      start=bk != 2 and part == 0, stop=part == 1)
                    pe.matmul(bank(4), ones[0:NE, 0:TP], tv_rows[:, 1, :], start=True, stop=True)
                    pe.matmul(bank(6), ones[0:NE, 0:TP], tv_rows[:, 2, :], start=True, stop=True).then_inc(rows_ready, 1)
            ring.used += 1 + NE
            ring.high = ring.low = ring.used
            w1 = merged_split[:, :, 0:2 * D].rearrange("p s (k n) -> p s k n", k=4)
            w2 = merged_split[:, :, 2 * D:4 * D].rearrange("p s (k n) -> p s k n", k=2)

            def up(pe, u, b):
                f, (lo, w) = u // 3, CHUNKS[u % 3]
                return feat_product(pe, ps[:, b, 0:w], w1, f, xT, lo, w, KD)
            gemm(6, up, *split_evac(ACT.Relu, chunk_view, pair_of(hT), lambda u: b1m[:, u // 3:u // 3 + 1]))

            def residual(dve, t, b, link):
                link(dve.tensor_tensor(res[:, t, :], bank(b), xn[:, t, :], ALU.add))
                return dve.tensor_tensor(res[:, t, :], res[:, t, :], b2_all[:], ALU.add)
            gemm(NT, lambda pe, t, b: tok_product(pe, bank(b), hT, t, w2, 2), residual, evac_on="vector")
            layernorm(res, res, 1e-5)
            with Stage("dve_chain") as (block, dve_chain):
                @block.vector
                def _(dve):
                    link = chain(dve, dve_chain)
                    for t in range(NT):
                        last = dve.tensor_tensor(res[:, t, :], res[:, t, :], lng_all[:], ALU.mult)
                    link(last)
                    for t in range(NT):
                        last = dve.tensor_tensor(res[:, t, :], res[:, t, :], lnb_all[:], ALU.add)
                    link(last)
                    for t in range(NT):
                        dve.tensor_tensor(x[:, t, :], x[:, t, :], res[:, t, :], ALU.add)

        layernorm(x, xn, 1e-5)
        with ExitStack() as c:
            agg = sbuf(c, "agg", [TP, NT, D])
            aggT = sbuf(c, "agg3T", [128, 2, KD, N], F16)
            with Stage("table_out") as (block, table_out):
                @block.sync
                def _(sp):
                    sp.dma_start(xn_table.rearrange("(t p) d -> p t d", p=TP), xn[:]).then_inc(table_out, 16)
                    sp.wait_ge(table_out, 16)

                @block.gpsimd
                def _(pool):
                    pool.memset(agg[:], 0.0)
            messages(xn_table, F_SRCI, agg, F_W, "L3")
            transposes(agg, aggT, KD)
            dense(aggT, first["L3_gnn"], x, row="L3_gnn_b", add=x)

        M = 256
        with ExitStack() as c:
            v = sbuf(c, "v3", [TP, NT, D])
            y = sbuf(c, "y3", [TP, NT, D])
            yT = xT
            kp = sbuf(c, "kp", [TP, NT, M])
            qpT = sbuf(c, "qpT", [128, 2, N])
            hT = sbuf(c, "h3T", [128, 2, KD, N], F16)
            sq = sbuf(c, "sq", [TP, NT])
            sq_out = sbuf(c, "sq_out", [TP, D])
            kv = sbuf(c, "kv3", [128, 2, D])
            ksum = sbuf(c, "ksum", [128, 2])
            den = sbuf(c, "den3", [TP, NT])
            layernorm(xn, y, 1e-3)
            transposes(y, hT, KD, COL0["L3_n1_g"], COL0["L3_n1_b"])
            n0, nw = first["L3_kqv"], first["L3_w"]

            q3 = xn
            sqq = sbuf(c, "sqq", [TP, NT])

            def with_square(dst, acc):
                def evac(act, t, b, link):
                    link(act.activation(dst[:, t, :], bank(b), ACT.Copy))
                    return act.activation(sq_out[:], dst[:, t, :], ACT.Square, accum_out=acc[:, t:t + 1])
                return evac
            for j, (dst, acc, row) in enumerate(((y, sq, "L3_kb"), (q3, sqq, "L3_qb"))):
                gemm(NT, lambda pe, t, b, j=j, row=row: tok_product(pe, bank(b), hT, t, ring.mat(n0 + j), KD, row),
                     with_square(dst, acc), weights={0: [n0 + j]}, frees={NT - 1: 1})
            dense(hT, n0 + 2, v, row="L3_vb")
            with Stage("halved") as (block, halved):
                @block.vector
                def _(dve):
                    dve.tensor_scalar(sq[:], sq[:], -0.5, None, ALU.mult)
                    dve.tensor_scalar(sqq[:], sqq[:], -0.5, None, ALU.mult)

            def random_features(src, acc, dst, free):
                transposes(src, yT, KD)
                w = ring.mat(nw, 0, 2 * D)
                gemm(NT, lambda pe, t, b: tok_product(pe, ps[0:TP, b, 0:M], yT, t, w, KD),
                     lambda act, t, b, link: act.activation(dst[:, t, :], ps[0:TP, b, 0:M], ACT.Exp, bias=acc[:, t:t + 1]),
                     weights={0: [nw]}, frees={NT - 1: 1} if free else None)
            random_features(y, sq, kp, False)
            qp = y[:].rearrange("p t d -> p (t d)")[:, 0:NT * M].rearrange("p (t m) -> p t m", m=M)
            random_features(q3, sqq, qp, True)
            transposes(qp, qpT, 2)
            with Stage("kv_ready", "kv_in", "den_ready", "product_ready", "drained", "dve_chain") as (
                    block, kv_ready, kv_in, den_ready, product_ready, drained, dve_chain):
                @block.tensor
                def _(pe):
                    for m in range(2):
                        for t in range(NT):
                            pe.matmul(ps[:, m, 0:D], kp[:, t, m * 128:(m + 1) * 128], v[:, t, :], start=t == 0, stop=t == NT - 1)
                        for t in range(NT):
                            last = pe.matmul(ps[:, 2 + m, 0:1], kp[:, t, m * 128:(m + 1) * 128], ones[0:TP, 0:1],
                                             start=t == 0, stop=t == NT - 1)
                    last.then_inc(kv_ready, 1)
                    pe.wait_ge(kv_in, 1)
                    for t in range(NT):
                        for m in range(2):
                            last = pe.matmul(ps[0:TP, 4, t:t + 1], qpT[:, m, tile_of(t)], ksum[:, m:m + 1],
                                             start=m == 0, stop=m == 1)
                    last.then_inc(den_ready, 1)
                    for t in range(NT):
                        if t >= 3:
                            pe.wait_ge(drained, t - 2)
                        for m in range(2):
                            last = pe.matmul(bank(5 + t % 3), qpT[:, m, tile_of(t)], kv[:, m, :], start=m == 0, stop=m == 1)
                        last.then_inc(product_ready, 1)

                @block.vector
                def _(dve):
                    link = chain(dve, dve_chain)
                    dve.wait_ge(kv_ready, 1)
                    dve.tensor_copy(kv[:], ps[:, 0:2, :])
                    dve.tensor_copy(ksum[:], ps[:, 2:4, 0]).then_inc(kv_in, 1)
                    dve.wait_ge(den_ready, 1)
                    link(dve.tensor_scalar(den[:], ps[0:TP, 4, 0:NT], 1.0 / M, 1e-8, ALU.mult, ALU.add))
                    link(dve.reciprocal(den[:], den[:]))
                    for t in range(NT):
                        dve.wait_ge(product_ready, t + 1)
                        dve.tensor_scalar(q3[:, t, :], bank(5 + t % 3), 1.0 / M, den[:, t:t + 1], ALU.mult,
                                          ALU.mult).then_inc(drained, 1)
            transposes(q3, yT, KD)
            dense(yT, first["L3_proj"], y, row="L3_proj_b", add=v)
            layernorm(y, v, 1e-3)
            transposes(v, yT, KD, COL0["L3_n2_g"], COL0["L3_n2_b"])
            pr, dst, src_of = feat_units(first["L3_mlp1"], hT, yT, KD)
            cb = COL0["L3_mlp_b1"]
            gemm(12, pr, *split_evac(ACT.Gelu, src_of, pair_of(hT), lambda u: cols[:, cb + u // 3:cb + u // 3 + 1]),
                 weights={0: [first["L3_mlp1"]]}, frees={11: 1})
            dense(hT, first["L3_mlp2"], y, row="L3_mlp_b2", add=y)
            with Stage("added") as (block, added):
                @block.vector
                def _(dve):
                    for t in range(NT):
                        dve.tensor_tensor(x[:, t, :], x[:, t, :], y[:, t, :], ALU.add)

        layernorm_T(x, xn, xT)
        with ExitStack() as c:
            comb = sbuf(c, "comb3", [TP, NT, NE])
            comb2 = sbuf(c, "comb_halves", [TP, NT, 2 * NE])
            with ExitStack() as c2:
                gT = sbuf(c2, "gate_hT", [128, 2, 2, N], F16)
                n = first["L3_gw1"]
                cb = COL0["L3_gb1"]

                def gate_up(pe, u, b):
                    f, (lo, w) = u // 3, CHUNKS[u % 3]
                    return feat_product(pe, ps[:, b, 0:w], ring.mat(n, 0, 2 * D), f, xT, lo, w, KD)
                gemm(6, gate_up, *split_evac(ACT.Relu, chunk_view, pair_of(gT), lambda u: cols[:, cb + u // 3:cb + u // 3 + 1]),
                     weights={0: [n]}, frees={5: 1})
                top_two(c2, "L3_gw2", 1, gT, 2, comb, True)
                add_expert_biases(c2, comb, 1)
            with Stage("doubled") as (block, doubled):
                @block.vector
                def _(dve):
                    for h in range(2):
                        dve.tensor_copy(comb2[:].rearrange("p t (e h) -> p t e h", h=2)[:, :, :, h], comb[:])
            def reload_half(sp, item, n, j):
                src = (I["L3_ffn_we1"], I["L3_ffn_we2"])[j][bass.ds(item, 1)]
                sp.dma_start(ring.raw[:, n % SLOTS, :].rearrange("p (k n) -> p k n", k=4),
                             src.rearrange("o (k p) n -> p (o k) n", p=128)).then_inc(ring.loaded[n % SLOTS], 16)
            experts(c, first["L3_exp"], 2 * NE, comb2, lambda i: i, ACT.Gelu, COL0["L3_be1"], 4, 2,
                    lambda n: ring.mat(n), lambda n: ring.mat(n + 1), reload_half)

        def store_x():
            with Stage("x_out",) as (block, x_out):
                @block.sync
                def _(sp):
                    sp.dma_start(out.rearrange("(t p) d -> p t d", p=TP), x[:]).then_inc(x_out, 16)
                    sp.wait_ge(x_out, 16)
        store_x()


def kernel(**inputs):
    import numpy as np
    import concourse.bacc as bacc
    from concourse import mybir as mb
    from concourse.bass_utils import run_bass_kernel_spmd as run

    a = {n: np.asarray(v) for n, v in inputs.items()}
    given = {n: a[n] for n in ("x", "src", "dst", "edge_type_8", "edge_weight1",
                               "L0_gnn_W_self", "L0_gnn_W_neigh", "L0_ffn_experts", "L1_gnn_W1", "L1_gnn_W2",
                               "L1_mix_w_qkv", "L1_mix_w_proj", "L1_ffn_W1", "L1_ffn_W2", "L1_ffn_Ws1", "L1_ffn_Ws2",
                               "L1_ffn_b2", "L2_ffn_tv_b2", "L2_ffn_tv_ln_g", "L2_ffn_tv_ln_b",
                               "L3_mix_kqv_w", "L3_mix_proj_w", "L3_mix_mlp_w1", "L3_mix_mlp_w2",
                               "L3_ffn_gw1", "L3_ffn_be2")}
    given["L3_ffn_we1"] = a["L3_ffn_we1"].reshape(NE, D, 2, D).transpose(0, 2, 1, 3).reshape(2 * NE, D, D)
    given["L3_ffn_we2"] = a["L3_ffn_we2"].reshape(2 * NE, D, D)
    for n in ("L0_mix_Wq", "L0_mix_Wkv", "L2_gnn_W_self", "L2_mix_qkv_w", "L2_mix_out_w", "L2_ffn_gfc1_w",
              "L2_ffn_W1", "L2_ffn_W2", "L3_gnn_W", "L3_mix_w"):
        given[n] = a[n].T
    for n in ("L2_gnn_W_rel", "L2_ffn_tv_W1", "L2_ffn_tv_W2"):
        given[n] = a[n].transpose(0, 2, 1)
    qb, kb = a["L2_mix_qkv_b"], a["L3_mix_kqv_b"]
    row = {"L0_b0": a["L0_gnn_b"][0], "L0_b1": a["L0_gnn_b"][1], "L0_b2": a["L0_gnn_b"][2],
           "L1_gnn_b2": a["L1_gnn_b2"], "L1_mix_b": a["L1_mix_b_proj"], "L1_bs2": a["L1_ffn_bs2"],
           "L2_bias": a["L2_gnn_bias"], "L2_kb": qb[D:2 * D], "L2_vb": qb[2 * D:], "L2_out_b": a["L2_mix_out_b"],
           "L2_b2": a["L2_ffn_b2"], "L2_ln_g": a["L2_ffn_ln_g"], "L2_ln_b": a["L2_ffn_ln_b"],
           "L3_gnn_b": a["L3_gnn_b"], "L3_kb": kb[0:D], "L3_qb": kb[D:2 * D], "L3_vb": kb[2 * D:],
           "L3_proj_b": a["L3_mix_proj_b"], "L3_mlp_b2": a["L3_mix_mlp_b2"]}
    given["rows"] = np.stack([row[n] for n in ROWS])
    col = {"L1_gnn_b1": a["L1_gnn_b1"], "L1_ffn_b1": a["L1_ffn_b1"].reshape(-1), "L1_bs1": a["L1_ffn_bs1"],
           "L2_qb": qb[0:D], "L2_g": a["L2_mix_ln_gamma"], "L2_bt": a["L2_mix_ln_beta"],
           "L2_gfc1_b": a["L2_ffn_gfc1_b"], "L2_b1": a["L2_ffn_b1"], "L2_tv_b1": a["L2_ffn_tv_b1"].reshape(-1),
           "L3_n1_g": a["L3_mix_n1_g"], "L3_n1_b": a["L3_mix_n1_b"], "L3_n2_g": a["L3_mix_n2_g"],
           "L3_n2_b": a["L3_mix_n2_b"], "L3_mlp_b1": a["L3_mix_mlp_b1"], "L3_gb1": a["L3_ffn_gb1"],
           "L3_be1": a["L3_ffn_be1"].reshape(-1)}
    given["cols"] = np.concatenate([col[n] for n in COLS]).reshape(NCOL, 128).T
    gate = {"L0_gate": a["L0_ffn_gate_w"][0], "L1_Wg": a["L1_ffn_Wg"], "L2_gfc2": a["L2_ffn_gfc2_w"].T,
            "L3_gw2": a["L3_ffn_gw2"]}
    given["gatew"] = np.concatenate([gate[n] for n in GATES]).reshape(NGATE, 128, NE).transpose(1, 0, 2)
    given["gateb"] = np.stack([a["L1_ffn_bg"], a["L3_ffn_gb2"], a["L2_ffn_gfc2_b"]])
    given["gfc2_col"] = a["L2_ffn_gfc2_b"].reshape(NE, 1)

    nc = bacc.Bacc("TRN2", target_bir_lowering=False, num_devices=1)
    arrays, ins = {}, {}
    for n, v in given.items():
        v = np.ascontiguousarray(v)
        arrays[f"in_{n}"] = v
        ins[n] = nc.dram_tensor(f"in_{n}", v.shape, mb.dt.from_np(v.dtype), kind="ExternalInput").ap()
    out = nc.dram_tensor("out_x", (N, D), mb.dt.float32, kind="ExternalOutput").ap()
    build(nc, ins, out)
    return run(nc, [arrays], core_ids=[0]).results[0]["out_x"]
```

```python
from contextlib import ExitStack

import concourse.bass as bass
from concourse import mybir

F32 = mybir.dt.float32
BF16 = mybir.dt.bfloat16
F16 = mybir.dt.float16
I32 = mybir.dt.int32
ALU = mybir.AluOpType
ACT = mybir.ActivationFunctionType
AX = mybir.AxisListType.X

N, D = 1250, 512
TP, NT = 125, 10
assert TP * NT == N
KD = D // 128
H, HD = 8, 64
NE = 8
E = 40000
EC = E // TP
GJ = 4
NG = (E + NT * (128 * GJ - 1)) // (128 * GJ)
NG += -NG % 4
NC = NG * GJ
AW = 1260
CW = AW // 3
R = 8
F_DST, F_SRC, F_TYPE, F_W, F_RELSRC, F_DSTREL, F_SRCI = range(7)
CHUNKS = ((0, 417), (417, 417), (834, 416))
SLOTS = 2
GT = 3
GR = 128 * GT
PG = (2 * N + NE * (GR - 1)) // GR
PG += PG % 2
CAP = N // NE

ROWS = ["L0_b0", "L0_b1", "L0_b2", "L1_gnn_b2", "L1_mix_b", "L1_bs2", "L2_bias", "L2_kb", "L2_vb", "L2_out_b",
        "L2_b2", "L2_ln_g", "L2_ln_b", "L3_gnn_b", "L3_kb", "L3_qb", "L3_vb", "L3_proj_b", "L3_mlp_b2"]
NR = len(ROWS)
COLS = {"L1_gnn_b1": 4, "L1_ffn_b1": 16, "L1_bs1": 2, "L2_qb": 4, "L2_g": 4, "L2_bt": 4, "L2_gfc1_b": 4, "L2_b1": 2,
        "L2_tv_b1": 16, "L3_n1_g": 4, "L3_n1_b": 4, "L3_n2_g": 4, "L3_n2_b": 4, "L3_mlp_b1": 4, "L3_gb1": 2,
        "L3_be1": 64}
COL0 = {}
for _n, _c in COLS.items():
    COL0[_n] = sum(COLS[m] for m in COL0)
NCOL = sum(COLS.values())
GATES = {"L0_gate": 4, "L1_Wg": 4, "L2_gfc2": 4, "L3_gw2": 2}
GATE0 = {}
for _n, _c in GATES.items():
    GATE0[_n] = sum(GATES[m] for m in GATE0)
NGATE = sum(GATES.values())


class Ring:

    def __init__(self, nc, ctx, loads, plain):
        self.plain = plain
        self.raw = ctx.enter_context(nc.sbuf_tensor("weights_in", [128, SLOTS, 4 * D], F32))
        self.buf = ctx.enter_context(nc.sbuf_tensor("weights_split", [128, SLOTS, 2, 4 * D], F16))
        self.loaded = [ctx.enter_context(nc.semaphore(f"weights_loaded{s}")) for s in range(SLOTS)]
        self.high_done = ctx.enter_context(nc.semaphore("weights_high_done"))
        self.split_done = ctx.enter_context(nc.semaphore("weights_split_done"))
        self.freed = [ctx.enter_context(nc.semaphore(f"weights_freed{s}")) for s in range(SLOTS)]
        self.loads = loads
        self.issued = 0
        self.high = 0
        self.low = 0
        self.used = 0
        self.count = []
        per = [0] * SLOTS
        for n, parts in enumerate(loads):
            per[n % SLOTS] += 16 * len(parts)
            self.count.append(per[n % SLOTS])

    def issue(self, sp, upto, over_plain=False):
        for n in range(self.issued, min(upto, len(self.loads))):
            if n - SLOTS in self.plain and not over_plain:
                break
            self.issued = n + 1
            if n >= SLOTS:
                sp.wait_ge(self.split_done, n - SLOTS + 1)
            for lo, hi, k, ap in self.loads[n]:
                dst = self.raw[:, n % SLOTS, lo:hi].rearrange("p (k n) -> p k n", k=k)
                sp.dma_start(dst, ap).then_inc(self.loaded[n % SLOTS], 16)

    def width(self, n):
        return max(hi for lo, hi, k, ap in self.loads[n])

    def split_high(self, act, upto):
        for n in range(self.high, min(upto, len(self.loads))):
            if n in self.plain:
                break
            self.high_of(act, n)
            self.high = n + 1

    def high_of(self, act, n, loads_before=0, in_before=0):
        if n >= SLOTS:
            act.wait_ge(self.freed[n % SLOTS], n // SLOTS + loads_before)
        act.wait_ge(self.loaded[n % SLOTS], self.count[n] + in_before)
        w = self.width(n)
        act.activation(self.buf[:, n % SLOTS, 0, 0:w], self.raw[:, n % SLOTS, 0:w], ACT.Copy).then_inc(self.high_done, 1)

    def split_low(self, dve, upto):
        for n in range(self.low, min(upto, len(self.loads))):
            if n in self.plain:
                break
            self.low_of(dve, n)
            self.low = n + 1

    def low_of(self, dve, n, loads_before=0):
        dve.wait_ge(self.high_done, n + 1 + loads_before)
        w = self.width(n)
        dve.tensor_tensor(self.buf[:, n % SLOTS, 1, 0:w], self.raw[:, n % SLOTS, 0:w], self.buf[:, n % SLOTS, 0, 0:w],
                          ALU.subtract).then_inc(self.split_done, 1)

    def wait(self, eng, n):
        eng.wait_ge(self.split_done, n + 1)

    def mat(self, n, lo=0, hi=4 * D, k=4):
        return self.buf[:, n % SLOTS, :, lo:hi].rearrange("p s (k n) -> p s k n", k=k)


def build(nc, ins, out):
    with ExitStack() as ctx:
        names = {}

        def sbuf(c, name, shape, dt=F32, side="left"):
            names[name] = names.get(name, 0) + 1
            if names[name] > 1:
                name = f"{name}_{names[name]}"
            return c.enter_context(nc.sbuf_tensor(name, shape, dt, side=side))

        def mats(t, order=None):
            w = t.shape[1] // D
            return [[(0, 4 * D, 4, t[:, m * D:(m + 1) * D].rearrange("(k p) n -> p k n", p=128))]
                    for m in (order or range(w))]

        def pairs(a, b):
            return [[(0, 2 * D, 4, a.rearrange("(k p) n -> p k n", p=128)),
                     (2 * D, 4 * D, 2, b.rearrange("(k p) n -> p k n", p=128))]]

        loads, first = [], {}

        def plan(name, items):
            first[name] = len(loads)
            loads.extend(items)

        I = ins
        plan("L0_q", mats(I["L0_mix_Wq"]))
        plan("L0_kv", mats(I["L0_mix_Wkv"]))
        for l in range(3):
            plan(f"L0_self{l}", mats(I["L0_gnn_W_self"][l]))
            plan(f"L0_neigh{l}", mats(I["L0_gnn_W_neigh"][l]))
        plan("L0_exp", [m for e in range(NE) for m in mats(I["L0_ffn_experts"][e])])
        plan("L1_W1", mats(I["L1_gnn_W1"]))
        plan("L1_W2", mats(I["L1_gnn_W2"]))
        plan("L1_qkv", mats(I["L1_mix_w_qkv"]))
        plan("L1_proj", mats(I["L1_mix_w_proj"]))
        plan("L1_exp", [m for e in range(NE) for m in pairs(I["L1_ffn_W1"][e], I["L1_ffn_W2"][e])])
        plan("L1_shared", pairs(I["L1_ffn_Ws1"], I["L1_ffn_Ws2"]))
        plan("L2_self", mats(I["L2_gnn_W_self"]))
        plan("L2_rel", [m for e in range(NE) for m in mats(I["L2_gnn_W_rel"][e])])
        plan("L2_qkv", mats(I["L2_mix_qkv_w"]))
        plan("L2_out", mats(I["L2_mix_out_w"]))
        plan("L2_gfc1", mats(I["L2_ffn_gfc1_w"]))
        plan("L2_base", pairs(I["L2_ffn_W1"], I["L2_ffn_W2"]))
        plan("L2_tv", [m for e in range(NE) for m in pairs(I["L2_ffn_tv_W1"][e], I["L2_ffn_tv_W2"][e])])
        plan("L3_gnn", mats(I["L3_gnn_W"]))
        plan("L3_kqv", mats(I["L3_mix_kqv_w"]))
        plan("L3_w", [[(0, 2 * D, 4, I["L3_mix_w"].rearrange("(k p) n -> p k n", p=128))]])
        plan("L3_proj", mats(I["L3_mix_proj_w"]))
        plan("L3_mlp1", mats(I["L3_mix_mlp_w1"]))
        plan("L3_mlp2", mats(I["L3_mix_mlp_w2"]))
        plan("L3_gw1", [[(0, 2 * D, 4, I["L3_ffn_gw1"].rearrange("(k p) n -> p k n", p=128))]])

        x = sbuf(ctx, "x", [TP, NT, D])
        xn = sbuf(ctx, "xn", [TP, NT, D])
        xT = sbuf(ctx, "xT", [128, 2, KD, N], F16)
        ring = Ring(nc, ctx, loads, range(first["L2_base"], first["L2_tv"] + NE))
        rows = sbuf(ctx, "rows", [64, D], F16)
        pick = sbuf(ctx, "pick", [64, NR, TP], F16)
        cols = sbuf(ctx, "cols", [128, NCOL])
        gatew = sbuf(ctx, "gatew", [128, 2, NGATE, NE], F16)
        gateb = sbuf(ctx, "gateb", [128, 3, NE])
        expert_b2 = sbuf(ctx, "expert_b2", [NE, 2, D])
        gfc2_col = sbuf(ctx, "gfc2_col", [NE, 1])
        ident = sbuf(ctx, "ident", [128, 128])
        ones = sbuf(ctx, "ones", [128, 128])
        below = sbuf(ctx, "below", [TP, TP])
        staging = sbuf(ctx, "staging", [128, 4, D])
        stats = sbuf(ctx, "stats", [TP, NT, 6])
        mv = sbuf(ctx, "mv", [TP, NT, 2])
        rstd = sbuf(ctx, "rstd", [TP, NT])
        rdeg = sbuf(ctx, "rdeg", [TP, NT])
        group_tile = sbuf(ctx, "group_tile", [1, NG], I32)
        iota_tile = sbuf(ctx, "iota_tile", [128, TP])
        ps = ctx.enter_context(nc.psum_tensor("ps", [128, 8, 512], F32))

        count_row = sbuf(ctx, "count_row", [128, NC], I32)
        count_weight = sbuf(ctx, "count_weight", [128, NC])

        edge_table = nc.dram_tensor("edge_table", (128 * NC, R), F32, kind="Internal").ap()
        count_table = nc.dram_tensor("count_table", (N * NE, 1), F32, kind="Internal").ap()
        rel_table = nc.dram_tensor("rel_table", (NE * N, D), F32, kind="Internal").ap()
        pick_table = nc.dram_tensor("pick_table", (PG * GR, D), F32, kind="Internal").ap()
        xn_table = nc.dram_tensor("xn_table", (N, D), F32, kind="Internal").ap()

        class Stage:

            def __init__(self, *names):
                self.names = names

            def __enter__(self):
                self.c = ExitStack()
                sems = [self.c.enter_context(nc.semaphore(n)) for n in self.names]
                self.sems = sems
                self.b = nc.Block()
                block = self.b.__enter__()
                return (block, *sems)

            def __exit__(self, *a):
                self.b.__exit__(*a)
                if a[0] is None:
                    for s in self.sems:
                        nc.sync.sem_clear(s)
                    nc.all_engine_barrier(sem_only=True)
                return self.c.__exit__(*a)

        def chain(eng, sem, before=0):
            n = [0]

            def link(ins):
                n[0] += 1
                ins.then_inc(sem, 1)
                eng.wait_ge(sem, before + n[0])
            return link

        def tile_of(t):
            return slice(t * TP, (t + 1) * TP)

        def bank(b, p=TP, w=D):
            return ps[0:p, b, 0:w]

        PASSES = ((0, 0), (0, 1), (1, 0))

        def tok_product(pe, dst, srcT, t, w, k_blocks, row=None, start=True, stop=True):
            if row is not None:
                pe.matmul(dst, pick[:, ROWS.index(row), :], rows[:], start=start, stop=False)
                start = False
            for k in range(k_blocks):
                for a, b in PASSES:
                    last = pe.matmul(dst, srcT[:, a, k, tile_of(t)], w[:, b, k, :], start=start, stop=stop and
                                     k == k_blocks - 1 and a == 1)
                    start = False
            return last

        def feat_product(pe, dst, w, f, srcT, lo, n, k_blocks):
            for k in range(k_blocks):
                for a, b in PASSES:
                    last = pe.matmul(dst, w[:, a, k, f * 128:(f + 1) * 128], srcT[:, b, k, lo:lo + n],
                                     start=k == 0 and a + b == 0, stop=k == k_blocks - 1 and a == 1)
            return last

        def split_evac(func, view, out, bias=None):
            def evac(act, u, b, link):
                v = view(u, b)
                g = staging[0:v.shape[0], u % 4, 0:v.shape[1]]
                link(act.activation(g, v, func, **({} if bias is None else {"bias": bias(u)})))
                return act.activation(out(u)[0], g, ACT.Copy)

            def finish(dve, u, b, link):
                high, low = out(u)
                return dve.tensor_tensor(low, staging[0:low.shape[0], u % 4, 0:low.shape[1]], high, ALU.subtract)
            return evac, finish

        def gemm(units, products, evac, finish=None, evac_on="scalar", weights=None, frees=None, extra=None, nb=4,
                 finish_reads_bank=False):
            weights, frees = weights or {}, frees or {}
            total = sum(frees.values())
            with Stage("product_ready", "bank_drained", "evac_chain", "finish_chain", "finished") as (
                    block, product_ready, bank_drained, evac_chain, finish_chain, finished):
                start = ring.used
                need = max([start + total] + [n + 1 for load_numbers in weights.values() for n in load_numbers])

                @block.sync
                def _(sp):
                    ring.issue(sp, start + 2 * SLOTS)

                @block.tensor
                def _(pe):
                    for u in range(units):
                        for n in weights.get(u, ()):
                            ring.wait(pe, n)
                        if u >= nb:
                            pe.wait_ge(finished if finish_reads_bank else bank_drained, u - nb + 1)
                        products(pe, u, u % nb).then_inc(product_ready, 1)

                def split(eng, vector, upto):
                    (ring.split_low if vector else ring.split_high)(eng, upto)

                def drain(eng):
                    link = chain(eng, evac_chain)
                    split(eng, evac_on == "vector", need)
                    for u in range(units):
                        eng.wait_ge(product_ready, u + 1)
                        if finish and u >= 4:
                            eng.wait_ge(finished, u - 3)
                        evac(eng, u, u % nb, link).then_inc(bank_drained, 1)
                        if u == 0:
                            split(eng, evac_on == "vector", start + SLOTS)
                    for n in range(start, start + total):
                        eng.sem_inc(ring.freed[n % SLOTS], 1)

                def complete(eng):
                    link = chain(eng, finish_chain)
                    split(eng, evac_on != "vector", need)
                    for u in range(units if finish else 1):
                        if finish:
                            eng.wait_ge(bank_drained, u + 1)
                            finish(eng, u, u % nb, link).then_inc(finished, 1)
                        if u == 0:
                            split(eng, evac_on != "vector", start + SLOTS)

                if evac_on == "scalar":
                    block.scalar(drain)
                    block.vector(complete)
                else:
                    block.vector(drain)
                    block.scalar(complete)
                if extra:
                    extra(block)
            ring.used += total

        def transposes(src, dstT, blocks, scale=None, bias=None, tokens=None, extra=None):
            split = len(dstT.shape) == 4

            def products(pe, t, b):
                for k in range(blocks):
                    last = pe.transpose(ps[:, b, k * TP:(k + 1) * TP], src[:, t, k * 128:(k + 1) * 128], ident[0:TP, 0:TP])
                return last

            def view(b):
                return ps[:, b, 0:blocks * TP].rearrange("p (k n) -> p k n", k=blocks)

            def evac(act, t, b, link):
                if tokens is not None:
                    act.activation(tokens[:, 0, t, :], src[:, t, :], ACT.Copy)
                if scale is None:
                    return act.activation(dstT[:, 0, 0:blocks, tile_of(t)] if split else dstT[:, 0:blocks, tile_of(t)],
                                          view(b), ACT.Copy)
                g = staging[:, t % 4, 0:blocks * TP].rearrange("p (k n) -> p k n", k=blocks)
                for k in range(blocks):
                    last = act.activation(g[:, k, :], view(b)[:, k, :], ACT.Identity,
                                          bias=cols[:, bias + k:bias + k + 1], scale=cols[:, scale + k:scale + k + 1])
                link(last)
                return act.activation(dstT[:, 0, 0:blocks, tile_of(t)], g, ACT.Copy)

            def finish(dve, t, b, link):
                if tokens is not None:
                    dve.tensor_tensor(tokens[:, 1, t, :], src[:, t, :], tokens[:, 0, t, :], ALU.subtract)
                full = view(b) if scale is None else staging[:, t % 4, 0:blocks * TP].rearrange("p (k n) -> p k n", k=blocks)
                return dve.tensor_tensor(dstT[:, 1, 0:blocks, tile_of(t)], full, dstT[:, 0, 0:blocks, tile_of(t)],
                                         ALU.subtract)
            gemm(NT, products, evac, finish if split else None, finish_reads_bank=split and scale is None, extra=extra)

        def layernorm_to_table(src, dst, table, eps, extra):
            with Stage("stats_ready", "std_ready", "half_ready", "table_out", "dve_chain") as (
                    block, stats_ready, std_ready, half_ready, table_out, dve_chain):
                extra(block)

                @block.vector
                def _(dve):
                    link = chain(dve, dve_chain)
                    for t in range(NT):
                        last = dve.bn_stats(stats[:, t, :], src[:, t, :])
                    link(last)
                    for t in range(NT):
                        last = dve.bn_aggr(mv[:, t, :], stats[:, t, :])
                    link(last)
                    dve.tensor_scalar(rstd[:], mv[:, :, 1], eps, None, ALU.add).then_inc(stats_ready, 1)
                    dve.wait_ge(std_ready, 1)
                    link(dve.reciprocal(rstd[:], rstd[:]))
                    for h in range(2):
                        for t in range(h * NT // 2, (h + 1) * NT // 2):
                            last = dve.tensor_scalar(dst[:, t, :], src[:, t, :], mv[:, t, 0:1], rstd[:, t:t + 1],
                                                     ALU.subtract, ALU.mult)
                        last.then_inc(half_ready, 1)

                @block.scalar
                def _(act):
                    act.wait_ge(stats_ready, 1)
                    act.activation(rstd[:], rstd[:], ACT.Sqrt).then_inc(std_ready, 1)

                @block.sync
                def _(sp):
                    ring.issue(sp, ring.used + SLOTS)
                    for h in range(2):
                        tiles = slice(h * NT // 2, (h + 1) * NT // 2)
                        sp.wait_ge(half_ready, h + 1)
                        sp.dma_start(table.rearrange("(t p) d -> p t d", p=TP)[:, tiles, :], dst[:, tiles, :]
                                     ).then_inc(table_out, 16)
                    sp.wait_ge(table_out, 32)

        def layernorm_T(src, dst, dstT, eps=1e-5, scale=None, bias=None, tokens=None, extra=None, row_squares=None):
            root = rstd if row_squares is None else row_squares
            with Stage("stats_ready", "std_ready", "norm_ready", "turned", "high_ready", "low_ready", "dve_chain",
                       "act_chain") as (block, stats_ready, std_ready, norm_ready, turned, high_ready, low_ready, dve_chain,
                                        act_chain):
                start = ring.used
                if extra:
                    extra(block)

                def view(b):
                    return ps[:, b, 0:KD * TP].rearrange("p (k n) -> p k n", k=KD)

                def staged(b):
                    return staging[:, b, 0:KD * TP].rearrange("p (k n) -> p k n", k=KD)

                @block.sync
                def _(sp):
                    ring.issue(sp, start + 2 * SLOTS)

                @block.tensor
                def _(pe):
                    for t in range(NT):
                        pe.wait_ge(norm_ready, t + 1)
                        if t >= 4:
                            pe.wait_ge(low_ready, t - 3)
                        for k in range(KD):
                            last = pe.transpose(ps[:, t % 4, k * TP:(k + 1) * TP], dst[:, t, k * 128:(k + 1) * 128],
                                                ident[0:TP, 0:TP])
                        last.then_inc(turned, 1)

                @block.scalar
                def _(act):
                    link = chain(act, act_chain)
                    act.wait_ge(stats_ready, 1)
                    act.activation(root[:], root[:], ACT.Sqrt).then_inc(std_ready, 1)
                    ring.split_high(act, start + SLOTS)
                    for t in range(NT):
                        if tokens is not None:
                            act.wait_ge(norm_ready, t + 1)
                            act.activation(tokens[:, 0, t, :], dst[:, t, :], ACT.Copy)
                        act.wait_ge(turned, t + 1)
                        if scale is None:
                            full = view(t % 4)
                        else:
                            if t >= 4:
                                act.wait_ge(low_ready, t - 3)
                            full = staged(t % 4)
                            for k in range(KD):
                                last = act.activation(full[:, k, :], view(t % 4)[:, k, :], ACT.Identity,
                                                      bias=cols[:, bias + k:bias + k + 1], scale=cols[:, scale + k:scale + k + 1])
                            link(last)
                        act.activation(dstT[:, 0, 0:KD, tile_of(t)], full, ACT.Copy).then_inc(high_ready, 1)

                @block.vector
                def _(dve):
                    link = chain(dve, dve_chain)
                    if row_squares is None:
                        for t in range(NT):
                            last = dve.bn_stats(stats[:, t, :], src[:, t, :])
                        link(last)
                        for t in range(NT):
                            last = dve.bn_aggr(mv[:, t, :], stats[:, t, :])
                        link(last)
                        dve.tensor_scalar(rstd[:], mv[:, :, 1], eps, None, ALU.add).then_inc(stats_ready, 1)
                        dve.wait_ge(std_ready, 1)
                    else:
                        dve.sem_inc(stats_ready, 1)
                        dve.wait_ge(std_ready, 1)
                        link(dve.tensor_scalar(root[:], root[:], 1e-12, None, ALU.max))
                    link(dve.reciprocal(root[:], root[:]))

                    def low(t):
                        dve.wait_ge(high_ready, t + 1)
                        if tokens is not None:
                            dve.tensor_tensor(tokens[:, 1, t, :], dst[:, t, :], tokens[:, 0, t, :], ALU.subtract)
                        dve.tensor_tensor(dstT[:, 1, 0:KD, tile_of(t)], view(t % 4) if scale is None else staged(t % 4),
                                          dstT[:, 0, 0:KD, tile_of(t)], ALU.subtract).then_inc(low_ready, 1)
                    for t in range(NT):
                        if row_squares is None:
                            last = dve.tensor_scalar(dst[:, t, :], src[:, t, :], mv[:, t, 0:1], rstd[:, t:t + 1],
                                                     ALU.subtract, ALU.mult)
                        else:
                            last = dve.tensor_scalar(dst[:, t, :], src[:, t, :], root[:, t:t + 1], None, ALU.mult)
                        last.then_inc(norm_ready, 1)
                        if t >= 3:
                            low(t - 3)
                        if t == 4:
                            ring.split_low(dve, start + SLOTS)
                    for t in range(NT - 3, NT):
                        low(t)

        def add_to_x(dve, t, b, link):
            return dve.tensor_tensor(x[:, t, :], bank(b), x[:, t, :], ALU.add)


        c_in = ExitStack()
        rows_in = sbuf(c_in, "rows_in", [64, D], side="right")
        rows_high = sbuf(c_in, "rows_high", [64, D], F16, side="right")
        gatew_in = sbuf(c_in, "gatew_in", [128, NGATE, NE], side="right")
        edges_in, x_in, consts_in = (ctx.enter_context(nc.semaphore(n)) for n in ("edge_words_in", "x_in", "consts_in"))
        c0 = ExitStack()
        records = sbuf(c0, "records", [TP, EC, R])
        slot = sbuf(c0, "slot", [TP, EC], I32)
        with ExitStack() as c:
            esrc = sbuf(c, "esrc", [TP, EC], I32)
            edst = sbuf(c, "edst", [TP, EC], I32)
            etype = sbuf(c, "etype", [TP, EC], I32)
            eweight = sbuf(c, "eweight", [TP, EC])
            dstf = sbuf(c, "dstf", [TP, EC])
            tile_f = sbuf(c, "tile_f", [TP, EC])
            one_row = sbuf(c, "one_row", [TP, EC])
            mask = sbuf(c, "mask", [TP, NT, EC])
            rank = sbuf(c, "rank", [TP, NT, EC])
            pos = sbuf(c, "pos", [TP, EC], I32)
            lane = sbuf(c, "lane", [TP, EC], I32)
            totals = sbuf(c, "totals", [TP, NT])
            ngroups_i = sbuf(c, "ngroups_i", [TP, NT], I32)
            ngroups = sbuf(c, "ngroups", [TP, NT])
            group_end = sbuf(c, "group_end", [TP, NT])
            offset = sbuf(c, "offset", [TP, NT])
            iota_g = sbuf(c, "iota_g", [1, NG])
            tile_acc = sbuf(c, "tile_acc", [1, NG])
            blank = sbuf(c, "blank", [128, NC, R])
            ri = records[:].bitcast(I32)
            with Stage("pool_step", "rows_blank") as (block, pool_step, rows_blank):
                @block.sync
                def _(sp):
                    for dst, name in ((esrc, "src"), (edst, "dst"), (etype, "edge_type_8")):
                        sp.dma_start(dst[:], I[name].rearrange("(p c) -> p c", c=EC)).then_inc(edges_in, 16)
                    sp.dma_start(eweight[:], I["edge_weight1"].rearrange("(p c) o -> p (c o)", c=EC)).then_inc(edges_in, 16)
                    sp.dma_start(x[:], I["x"].rearrange("(t p) d -> p t d", p=TP)).then_inc(x_in, 16)
                    sp.wait_ge(rows_blank, 1)
                    for part in range(2):
                        sp.dma_start(rows_in[32 * part:32 * part + NR], I["rows"]).then_inc(consts_in, 16)
                    sp.dma_start(cols[:], I["cols"]).then_inc(consts_in, 16)
                    sp.dma_start(gatew_in[:], I["gatew"]).then_inc(consts_in, 16)
                    sp.dma_start(gateb[:], I["gateb"].rearrange("(o g) e -> o g e", o=1).to_broadcast([128, 3, NE])
                                 ).then_inc(consts_in, 16)
                    sp.dma_start(gfc2_col[:], I["gfc2_col"]).then_inc(consts_in, 16)
                    sp.dma_start(expert_b2[:, 0, :], I["L1_ffn_b2"]).then_inc(consts_in, 16)
                    sp.dma_start(expert_b2[:, 1, :], I["L3_ffn_be2"]).then_inc(consts_in, 16)
                    ring.issue(sp, SLOTS)

                @block.gpsimd
                def _(pool):
                    link = chain(pool, pool_step)
                    link(pool.memset(ones[:], 1.0))
                    pool.affine_select(out=ident[:], in_=ones[:], compare_op=ALU.is_equal, fill=0.0, base=0,
                                       pattern=[[-1, 128]], channel_multiplier=1)
                    pool.affine_select(out=below[:], in_=ones[0:TP, 0:TP], compare_op=ALU.is_gt, fill=0.0, base=0,
                                       pattern=[[1, TP]], channel_multiplier=-1)
                    pool.memset(records[:], 0.0)
                    link(pool.iota(iota_tile[:], [[1, TP]], 0, 0, allow_small_or_imprecise_dtypes=True))

                @block.vector
                def _(dve):
                    dve.memset(rows_in[:], 0.0).then_inc(rows_blank, 1)

            with Stage("high_done", "dve_chain", "pool_step", "totals_ready", "prefix_ready", "table_blank") as (
                    block, high_done, dve_chain, pool_step, totals_ready, prefix_ready, table_blank):
                @block.scalar
                def _(act):
                    act.wait_ge(consts_in, 128)
                    act.activation(rows_high[:], rows_in[:], ACT.Copy)
                    act.activation(rows[0:32], rows_in[0:32], ACT.Copy)
                    act.activation(gatew[:, 0], gatew_in[:], ACT.Copy).then_inc(high_done, 1)

                @block.sync
                def _(sp):
                    sp.wait_ge(x_in, 16)
                    sp.wait_ge(consts_in, 128)
                    sp.wait_ge(pool_step, 2)
                    sp.dma_start(edge_table.rearrange("(p c) r -> p c r", c=NC), blank[:]).then_inc(table_blank, 16)
                    sp.wait_ge(table_blank, 16)

                @block.gpsimd
                def _(pool):
                    link = chain(pool, pool_step)
                    link(pool.memset(blank[:], 0.0))
                    link(pool.memset(blank[:, :, F_DST], -1.0))
                    link(pool.iota(iota_g[:], [[1, NG]], 0, 0, allow_small_or_imprecise_dtypes=True))
                    link(pool.memset(pick[:], 1.0))
                    for part in range(2):
                        link(pool.affine_select(out=pick[32 * part:32 * part + 32], in_=pick[32 * part:32 * part + 32],
                                                compare_op=ALU.is_equal, fill=0.0, base=0, pattern=[[-1, NR], [0, TP]],
                                                channel_multiplier=1))

                @block.vector
                def _(dve):
                    link = chain(dve, dve_chain)
                    dve.memset(one_row[:], 1.0)
                    link(dve.memset(tile_acc[:], 0.0))
                    dve.wait_ge(edges_in, 64)
                    dve.tensor_copy(dstf[:], edst[:])
                    dve.tensor_copy(records[:, :, F_SRC], esrc[:])
                    dve.tensor_copy(ri[:, :, F_SRCI], esrc[:])
                    dve.tensor_copy(records[:, :, F_W], eweight[:])
                    link(dve.tensor_copy(records[:, :, F_TYPE], etype[:]))
                    dve.scalar_tensor_tensor(out=ri[:, :, F_RELSRC], in0=records[:, :, F_TYPE], scalar=float(N),
                                             in1=records[:, :, F_SRC], op0=ALU.mult, op1=ALU.add)
                    link(dve.scalar_tensor_tensor(out=ri[:, :, F_DSTREL], in0=dstf[:], scalar=float(NE),
                                                  in1=records[:, :, F_TYPE], op0=ALU.mult, op1=ALU.add))
                    link(dve.tensor_scalar(tile_f[:], dstf[:], float(TP), None, ALU.is_ge))
                    for b in range(2, NT):
                        link(dve.scalar_tensor_tensor(out=tile_f[:], in0=dstf[:], scalar=float(TP * b),
                                                      in1=tile_f[:], op0=ALU.is_ge, op1=ALU.add))
                    dve.scalar_tensor_tensor(out=records[:, :, F_DST], in0=tile_f[:], scalar=-float(TP),
                                             in1=dstf[:], op0=ALU.mult, op1=ALU.add)
                    for b in range(NT):
                        last = dve.tensor_scalar(mask[:, b, :], tile_f[:], float(b), None, ALU.is_equal)
                    link(last)
                    for b in range(NT):
                        last = dve.tensor_tensor_scan(out=rank[:, b, :], data0=one_row[:], data1=mask[:, b, :],
                                                      initial=0.0, op0=ALU.mult, op1=ALU.add)
                    link(last)
                    dve.tensor_copy(totals[:], rank[:, :, EC - 1]).then_inc(totals_ready, 1)
                    dve.wait_ge(prefix_ready, 1)
                    link(dve.tensor_scalar(ngroups_i[:], ps[0:TP, 1, 0:NT], float(128 * GJ - 1), None, ALU.add))
                    link(dve.tensor_scalar(ngroups_i[:], ngroups_i[:], 9, None, ALU.arith_shift_right))
                    link(dve.tensor_copy(ngroups[:], ngroups_i[:]))
                    link(dve.tensor_tensor_scan(out=group_end[:], data0=one_row[:, 0:NT], data1=ngroups[:],
                                                initial=0.0, op0=ALU.mult, op1=ALU.add))
                    link(dve.tensor_tensor(offset[:], group_end[:], ngroups[:], ALU.subtract))
                    link(dve.tensor_scalar(offset[:], offset[:], float(128 * GJ), -1.0, ALU.mult, ALU.add))
                    link(dve.tensor_tensor(offset[:], offset[:], ps[0:TP, 0, 0:NT], ALU.add))
                    for b in range(NT):
                        last = dve.scalar_tensor_tensor(out=rank[:, b, :], in0=rank[:, b, :], scalar=offset[:, b:b + 1],
                                                        in1=mask[:, b, :], op0=ALU.add, op1=ALU.mult)
                    link(last)
                    link(dve.tensor_reduce(dstf[:], rank[:].rearrange("p b c -> p c b"), AX.X, ALU.add))
                    link(dve.tensor_copy(pos[:], dstf[:]))
                    dve.tensor_scalar(lane[:], pos[:], 127, None, ALU.bitwise_and)
                    link(dve.tensor_scalar(pos[:], pos[:], 7, None, ALU.arith_shift_right))
                    dve.scalar_tensor_tensor(out=slot[:], in0=lane[:], scalar=float(NC), in1=pos[:],
                                             op0=ALU.mult, op1=ALU.add)
                    dve.wait_ge(pool_step, 3)
                    for b in range(NT - 1):
                        link(dve.scalar_tensor_tensor(out=tile_acc[:], in0=iota_g[:], scalar=group_end[0:1, b:b + 1],
                                                      in1=tile_acc[:], op0=ALU.is_ge, op1=ALU.add))
                    dve.tensor_copy(group_tile[:], tile_acc[:])
                    dve.wait_ge(high_done, 1)
                    dve.tensor_tensor(rows[32:64], rows_in[32:64], rows_high[32:64], ALU.subtract)
                    dve.tensor_tensor(gatew[:, 1], gatew_in[:], gatew[:, 0], ALU.subtract)

                @block.tensor
                def _(pe):
                    pe.wait_ge(totals_ready, 1)
                    pe.matmul(ps[0:TP, 0, 0:NT], below[:], totals[:], start=True, stop=True)
                    pe.matmul(ps[0:TP, 1, 0:NT], ones[0:TP, 0:TP], totals[:], start=True, stop=True).then_inc(prefix_ready, 1)

        c_in.close()
        SC = 8
        slot_stage = sbuf(c0, "slot_stage", [TP, 2, SC], I32)
        record_stage = sbuf(c0, "record_stage", [TP, 2, SC, R])
        records_out = [ctx.enter_context(nc.semaphore(f"records_out{b}")) for b in range(2)]
        record_staged = ctx.enter_context(nc.semaphore("record_staged"))
        loop_turn = ctx.enter_context(nc.semaphore("loop_turn"))

        def scatter_edges(first_set, sets):
            assert sets % 2 == 0 and first_set % 2 == 0

            def put(pool, n, b):
                pool.tensor_copy(slot_stage[:, b, :], slot[:, bass.ds(SC * n, SC)])
                pool.tensor_copy(record_stage[:, b], records[:, bass.ds(SC * n, SC), :]).then_inc(record_staged, 1)
                pool.wait_ge(record_staged, n + 1)
                pool.sem_inc(loop_turn, 1)
                for j in range(SC):
                    pool.indirect_dma_start(edge_table, bass.IndirectOffsetOnAxis(ap=slot_stage[:, b, j:j + 1], axis=0),
                                            record_stage[:, b, j, :], None).then_inc(records_out[b], 16)

            def add(block):
                h = first_set // 2

                @block.gpsimd
                def _(pool):
                    put(pool, first_set, 0)
                    if sets > 2:
                        with pool.Fori(0, sets // 2 - 1) as i:
                            put(pool, 2 * i + (first_set + 1), 1)
                            pool.wait_ge(records_out[0], 16 * SC * i + 16 * SC * (h + 1))
                            pool.sem_inc(loop_turn, 1)
                            put(pool, 2 * i + (first_set + 2), 0)
                            pool.wait_ge(records_out[1], 16 * SC * i + 16 * SC * (h + 1))
                            pool.sem_inc(loop_turn, 1)
                    put(pool, first_set + sets - 1, 1)
                    for b in range(2):
                        pool.wait_ge(records_out[b], 16 * SC * (h + sets // 2))
            return add

        layernorm_T(x, xn, xT, extra=scatter_edges(0, 4))

        def elu1(dst, exp_buf, src_of, bias=None):
            def evac(act, u, b, link):
                d = dst(u)
                e = exp_buf[0:d.shape[0], u % 4, 0:d.shape[1]]
                plus = {} if bias is None else {"bias": bias(u)[0]}
                minus = {} if bias is None else {"bias": bias(u)[1]}
                link(act.activation(e, src_of(u, b), ACT.Relu, scale=-1.0, **minus))
                act.activation(e, e, ACT.Exp, scale=-1.0)
                return act.activation(d, src_of(u, b), ACT.Relu, **plus)

            def finish(dve, u, b, link):
                d = dst(u)
                return dve.tensor_tensor(d, exp_buf[0:d.shape[0], u % 4, 0:d.shape[1]], d, ALU.add)
            return evac, finish

        def feat_units(n_load, dstT, srcT, k_blocks):
            def products(pe, u, b):
                f, (lo, n) = u // 3, CHUNKS[u % 3]
                return feat_product(pe, ps[:, b, 0:n], ring.mat(n_load), f, srcT, lo, n, k_blocks)

            def dst(u):
                f, (lo, n) = u // 3, CHUNKS[u % 3]
                return dstT[:, f, lo:lo + n]

            def src_of(u, b):
                return ps[:, b, 0:CHUNKS[u % 3][1]]
            return products, dst, src_of

        def pair_of(dstT):
            def out(u):
                f, (lo, n) = u // 3, CHUNKS[u % 3]
                return dstT[:, 0, f, lo:lo + n], dstT[:, 1, f, lo:lo + n]
            return out

        VW = 129

        def kv_and_apply(c, qT, k, vo, eps, to=None, col_scale=None, den_ones=False, extra=None):
            bd = sbuf(c, "kv_blocks", [128, 4, 130])
            den = sbuf(c, "att_den", [TP, 2, H])
            att = sbuf(c, "att", [TP, 2, D]) if to is None else None
            with Stage("kv_ready", "blocks_ready", "product_ready", "drained", "dve_chain") as (
                    block, kv_ready, blocks_ready, product_ready, drained, dve_chain):
                if extra:
                    extra(block)

                @block.tensor
                def _(pe):
                    for g in range(4):
                        for t in range(NT):
                            last = pe.matmul(ps[:, g, 0:VW], k[:, t, g * 128:(g + 1) * 128], vo[:, t, g, :],
                                             start=t == 0, stop=t == NT - 1)
                    last.then_inc(kv_ready, 1)
                    pe.wait_ge(blocks_ready, 1)
                    for t in range(NT):
                        if t >= 2:
                            pe.wait_ge(drained, t - 1)
                        for g in range(4):
                            last = pe.matmul(ps[0:TP, 4 + 2 * (t % 2) + g // 2, (g % 2) * 130:(g % 2) * 130 + 130],
                                             qT[:, g, tile_of(t)], bd[:, g, :], start=True, stop=True)
                        last.then_inc(product_ready, 1)

                @block.vector
                def _(dve):
                    link = chain(dve, dve_chain)
                    link(dve.memset(bd[:], 0.0))
                    dve.wait_ge(kv_ready, 1)
                    for g in range(4):
                        for h in range(2):
                            pr = slice(64 * h, 64 * h + 64)
                            if col_scale is None:
                                dve.tensor_copy(bd[pr, g, 64 * h:64 * h + 64], ps[pr, g, 64 * h:64 * h + 64])
                            else:
                                dve.tensor_scalar(bd[pr, g, 64 * h:64 * h + 64], ps[pr, g, 64 * h:64 * h + 64],
                                                  col_scale[pr, g:g + 1], None, ALU.mult)
                            if den_ones:
                                last = dve.tensor_copy(bd[pr, g, 128 + h:129 + h], ones[pr, 0:1])
                            else:
                                last = dve.tensor_copy(bd[pr, g, 128 + h:129 + h], ps[pr, g, 128:129])
                    last.then_inc(blocks_ready, 1)
                    for t in range(NT):
                        dve.wait_ge(product_ready, t + 1)
                        v = ps[0:TP, 4 + 2 * (t % 2):6 + 2 * (t % 2), 0:260].rearrange("p b (g w) -> p b g w", g=2)
                        dn = den[:, t % 2, :].rearrange("p (b g h) -> p b g h", b=2, g=2)
                        link(dve.tensor_scalar(dn, v[:, :, :, 128:130], eps, None, ALU.add))
                        link(dve.reciprocal(den[:, t % 2, :], den[:, t % 2, :]))
                        for bb in range(2):
                            a = (att[:, t % 2] if to is None else to[:, t])[:, bb * 256:(bb + 1) * 256].rearrange("p (g h d) -> p g h d", g=2, h=2)
                            vv = v[:, bb, :, 0:128].rearrange("p g (h d) -> p g h d", h=2)
                            dd = dn[:, bb].rearrange("p g (h o) -> p g h o", o=1).to_broadcast([TP, 2, 2, 64])
                            last = dve.tensor_tensor(a, vv, dd, ALU.mult)
                        if to is None:
                            link(last)
                            last = dve.tensor_tensor(x[:, t, :], att[:, t % 2, :], x[:, t, :], ALU.add)
                        last.then_inc(drained, 1)

                @block.sync
                def _(sp):
                    ring.issue(sp, ring.used + SLOTS)

        def elu_q(qT, ebuf, srcT, n, bias=None, extra=None):
            pr, dst, src_of = feat_units(n, qT, srcT, KD)
            ev, fi = elu1(dst, ebuf, src_of, bias)
            gemm(12, pr, ev, fi, weights={0: [n]}, frees={11: 1}, extra=extra)

        def elu_k(k, ebuf, srcT, n, row=None, extra=None):
            ev, fi = elu1(lambda u: k[:, u, :], ebuf, lambda u, b: bank(b))
            gemm(NT, lambda pe, u, b: tok_product(pe, bank(b), srcT, u, ring.mat(n), KD, row), ev, fi,
                 weights={0: [n]}, frees={NT - 1: 1}, extra=extra)

        def values(vo, srcT, n, row=None, extra=None):
            def evac(act, u, b, link):
                act.activation(vo[:, u, :, 128], ones[0:TP, 0:4], ACT.Copy)
                return act.activation(vo[:, u, :, 0:128], bank(b).rearrange("p (g w) -> p g w", g=4), ACT.Copy)
            gemm(NT, lambda pe, u, b: tok_product(pe, bank(b), srcT, u, ring.mat(n), KD, row), evac,
                 weights={0: [n]}, frees={NT - 1: 1}, extra=extra)

        def dense(srcT, n, dst, k_blocks=KD, row=None, add=None, scale=None, add2=None):
            def evac(eng, u, b, link):
                if add is None:
                    return eng.activation(dst[:, u, :], bank(b), ACT.Copy)
                if scale is not None:
                    return eng.scalar_tensor_tensor(out=dst[:, u, :], in0=bank(b), scalar=scale, in1=add[:, u, :],
                                                    op0=ALU.mult, op1=ALU.add)
                if add2 is not None:
                    link(eng.tensor_tensor(dst[:, u, :], bank(b), add[:, u, :], ALU.add))
                    return eng.tensor_tensor(dst[:, u, :], dst[:, u, :], add2[:, u, :], ALU.add)
                return eng.tensor_tensor(dst[:, u, :], bank(b), add[:, u, :], ALU.add)
            w = ring.mat(n) if k_blocks == KD else ring.mat(n, 2 * D, 4 * D, 2)
            gemm(NT, lambda pe, u, b: tok_product(pe, bank(b), srcT, u, w, k_blocks, row), evac,
                 evac_on="scalar" if add is None else "vector", weights={0: [n]}, frees={NT - 1: 1})

        counts_in = [ctx.enter_context(nc.semaphore(f"counts_in{b}")) for b in range(2)]
        count_staged = ctx.enter_context(nc.semaphore("count_staged"))

        def gather_counts(c, first_set, sets):
            assert sets % 2 == 0 and first_set % 2 == 0 and NC % (2 * SC) == 0
            row_stage = sbuf(c, "row_stage", [128, 2, SC], I32)
            count_stage = sbuf(c, "count_stage", [128, 2, SC])

            def ask(pool, n, b):
                pool.tensor_copy(row_stage[:, b, :], count_row[:, bass.ds(SC * n, SC)]).then_inc(count_staged, 1)
                pool.wait_ge(count_staged, n + 1)
                pool.sem_inc(loop_turn, 1)
                for j in range(SC):
                    pool.indirect_dma_start(count_stage[:, b, j:j + 1], None, count_table, bass.IndirectOffsetOnAxis(
                        ap=row_stage[:, b, j:j + 1], axis=0)).then_inc(counts_in[b], 16)

            def take(pool, n, b, count):
                pool.wait_ge(counts_in[b], count)
                pool.sem_inc(loop_turn, 1)
                pool.tensor_copy(count_weight[:, bass.ds(SC * n, SC)], count_stage[:, b, :])

            def add(block):
                h = first_set // 2

                @block.gpsimd
                def _(pool):
                    ask(pool, first_set, 0)
                    with pool.Fori(0, sets // 2 - 1) as i:
                        ask(pool, 2 * i + (first_set + 1), 1)
                        take(pool, 2 * i + first_set, 0, 16 * SC * i + 16 * SC * (h + 1))
                        ask(pool, 2 * i + (first_set + 2), 0)
                        take(pool, 2 * i + (first_set + 1), 1, 16 * SC * i + 16 * SC * (h + 1))
                    ask(pool, first_set + sets - 1, 1)
                    for b in range(2):
                        take(pool, first_set + sets - 2 + b, b, 16 * SC * (h + sets // 2))
            return add

        with ExitStack() as c:
            qT = sbuf(c, "qT", [128, KD, N])
            k = sbuf(c, "k", [TP, NT, D])
            vo = sbuf(c, "vo", [TP, NT, 4, VW])
            ebuf = sbuf(c, "ebuf", [128, 4, D])
            elu_q(qT, ebuf, xT, first["L0_q"], extra=scatter_edges(4, 4))
            elu_k(k, ebuf, xT, first["L0_kv"], extra=scatter_edges(8, 4))
            values(vo, xT, first["L0_kv"] + 1, extra=scatter_edges(12, 4))
            kv_and_apply(c, qT, k, vo, 1e-6, extra=scatter_edges(16, 4))
        with Stage() as (block,):
            scatter_edges(20, EC // SC - 20)(block)
        c0.close()

        with ExitStack() as c_adj:
            degree_all = sbuf(c_adj, "degree_all", [128, N])
            counts = sbuf(c_adj, "counts", [TP, NT, NE])
            degree = sbuf(c_adj, "degree", [TP, NT])
            c_sums = ExitStack()
            sums = sbuf(c_sums, "sums", [TP, NT, AW], side="right")
            with ExitStack() as c:
                edges = sbuf(c, "edges", [128, NC, R])
                iota_src = sbuf(c, "iota_src", [128, N], F16)
                dst_hot = sbuf(c, "dst_hot", [128, 2, GJ, TP], BF16)
                src_hot = sbuf(c, "src_hot", [128, 2, GJ, AW], BF16)
                minus_src = sbuf(c, "minus_src", [128, NG])
                minus_now = sbuf(c, "minus_now", [128, 2])
                distance = staging[:].rearrange("p a b -> p (a b)").bitcast(F16)[:, 0:N]
                square = [staging[:, 2 + b, 0:GJ * TP].rearrange("p (j n) -> p j n", j=GJ) for b in range(2)]
                with Stage("edges_in", "pool_step", "hot_ready", "act_hot_ready", "square_ready", "square_chain", "minus_ready", "sums_ready",
                           "banks_free", "act_chain") as (block, edges_in, pool_step, hot_ready, act_hot_ready,
                                                          square_ready, square_chain, minus_ready, sums_ready, banks_free, act_chain):
                    @block.sync
                    def _(sp):
                        sp.dma_start(edges[:], edge_table.rearrange("(p c) r -> p c r", c=NC)).then_inc(edges_in, 16)

                    @block.gpsimd
                    def _(pool):
                        pool.iota(iota_src[:], [[1, N]], 0, 0, allow_small_or_imprecise_dtypes=True)
                        pool.memset(src_hot[:], 0.0)
                        pool.memset(sums[:], 0.0).then_inc(pool_step, 1)
                        pool.wait_ge(edges_in, 16)
                        with pool.Fori(0, NG // 2) as i:
                            for s in range(2):
                                n = 2 * i + s
                                link = chain(pool, square_chain, n)
                                pool.wait_ge(act_hot_ready, n + 1)
                                pool.sem_inc(loop_turn, 1)
                                ed = edges[:, bass.ds(GJ * n, GJ), :]
                                link(pool.tensor_tensor(
                                    square[s], iota_tile[:].rearrange("p (o n) -> p o n", o=1).to_broadcast([128, GJ, TP]),
                                    ed[:, :, F_DST:F_DST + 1].to_broadcast([128, GJ, TP]), ALU.subtract))
                                pool.tensor_tensor(square[s], square[s], square[s], ALU.mult).then_inc(square_ready, 1)

                    def build_hot(dve, n, s):
                        ed = edges[:, bass.ds(GJ * n, GJ), :]
                        dve.tensor_tensor(
                            src_hot[:, s, :, N:N + NE],
                            iota_tile[:, 0:NE].rearrange("p (o n) -> p o n", o=1).to_broadcast([128, GJ, NE]),
                            ed[:, :, F_TYPE:F_TYPE + 1].to_broadcast([128, GJ, NE]), ALU.is_equal)
                        for j in range(GJ - 1):
                            last = dve.tensor_scalar(
                                src_hot[:, s, j, 0:N], iota_src[:],
                                edges[:, bass.ds(GJ * n + j, 1), F_SRC:F_SRC + 1].rearrange("p a b -> p (a b)"),
                                None, ALU.is_equal)
                        last.then_inc(hot_ready, 1)

                    @block.scalar
                    def _(act):
                        act.wait_ge(minus_ready, 1)
                        act.sem_inc(act_hot_ready, 2)
                        with act.Fori(0, NG // 2) as i:
                            act.activation(minus_now[:], minus_src[:, bass.ds(2 * i, 2)], ACT.Copy).then_inc(act_chain, 1)
                            act.wait_ge(act_chain, 3 * i + 1)
                            for s in range(2):
                                n = 2 * i + s
                                act.wait_ge(act_hot_ready, n + 2)
                                act.activation(distance, iota_src[:], ACT.Abs, bias=minus_now[:, s:s + 1]).then_inc(act_chain, 1)
                                act.wait_ge(sums_ready, n + 1)
                                act.wait_ge(square_ready, n + 1)
                                act.activation(dst_hot[:, s], square[s], ACT.Relu, scale=-1.0, bias=ones[:, 0:1])
                                act.wait_ge(act_chain, 3 * i + s + 2)
                                act.activation(src_hot[:, s, GJ - 1, 0:N], distance, ACT.Relu, scale=-1.0,
                                               bias=ones[:, 0:1]).then_inc(act_hot_ready, 1)

                    def add_sums(dve, n, s):
                        dve.wait_ge(sums_ready, n + 3)
                        dve.wait_ge(banks_free, n + 2)
                        tile = dve.value_load(group_tile[0:1, bass.ds(n, 1)], min_val=0, max_val=NT - 1)
                        a = sums[:, bass.ds(tile, 1), :].rearrange("p o (c w) -> p (o c) w", c=3)
                        dve.tensor_tensor(a, ps[0:TP, 3 * s:3 * s + 3, 0:CW], a, ALU.add).then_inc(banks_free, 1)

                    @block.vector
                    def _(dve):
                        dve.wait_ge(edges_in, 16)
                        dve.wait_ge(pool_step, 1)
                        dve.sem_inc(banks_free, 2)
                        dve.tensor_copy(count_row[:], edges[:].bitcast(I32)[:, :, F_DSTREL])
                        dve.tensor_scalar(minus_src[:], edges[:, :, F_SRC].rearrange("p (g j) -> p g j", j=GJ)[:, :, GJ - 1],
                                          -1.0, None, ALU.mult).then_inc(minus_ready, 1)
                        build_hot(dve, 0, 0)
                        with dve.Fori(0, NG // 2 - 1) as i:
                            build_hot(dve, 2 * i + 1, 1)
                            add_sums(dve, 2 * i, 0)
                            build_hot(dve, 2 * i + 2, 0)
                            add_sums(dve, 2 * i + 1, 1)
                        build_hot(dve, NG - 1, 1)
                        add_sums(dve, NG - 2, 0)
                        add_sums(dve, NG - 1, 1)

                    @block.tensor
                    def _(pe):
                        pe.sem_inc(sums_ready, 2)
                        with pe.Fori(0, NG // 2) as i:
                            for s in range(2):
                                pe.wait_ge(hot_ready, 2 * i + s + 1)
                                pe.wait_ge(act_hot_ready, 2 * i + s + 3)
                                pe.wait_ge(banks_free, 2 * i + s + 1)
                                for w in range(3):
                                    for j in range(GJ):
                                        last = pe.matmul(ps[0:TP, 3 * s + w, 0:CW], dst_hot[:, s, j, :],
                                                         src_hot[:, s, j, w * CW:(w + 1) * CW],
                                                         start=j == 0, stop=j == GJ - 1)
                                last.then_inc(sums_ready, 1)

            c_diag = ExitStack()
            degree_diag = sbuf(c_diag, "degree_diag", [TP, NT, TP])
            with Stage("dve_chain", "counts_ready", "counts_out", "diag_ready", "degree_ready") as (
                    block, dve_chain, counts_ready, counts_out, diag_ready, degree_ready):
                @block.vector
                def _(dve):
                    link = chain(dve, dve_chain)
                    dve.tensor_reduce(degree[:], sums[:, :, N:N + NE], AX.X, ALU.add)
                    link(dve.tensor_scalar(counts[:], sums[:, :, N:N + NE], 1.0, None, ALU.max))
                    dve.reciprocal(counts[:], counts[:]).then_inc(counts_ready, 1)
                    link(dve.tensor_scalar(degree[:], degree[:], 1.0, None, ALU.max))
                    link(dve.reciprocal(rdeg[:], degree[:]))
                    for t in range(NT):
                        last = dve.tensor_scalar(degree_diag[:, t, :], ident[0:TP, 0:TP], rdeg[:, t:t + 1], None, ALU.mult)
                    last.then_inc(diag_ready, 1)
                    dve.wait_ge(degree_ready, 1)
                    for t in range(NT):
                        dve.tensor_copy(degree_all[:, tile_of(t)], ps[:, t // 4, (t % 4) * TP:(t % 4 + 1) * TP])

                @block.tensor
                def _(pe):
                    pe.wait_ge(diag_ready, 1)
                    for t in range(NT):
                        last = pe.matmul(ps[:, t // 4, (t % 4) * TP:(t % 4 + 1) * TP], ones[0:TP, :], degree_diag[:, t, :],
                                         start=True, stop=True)
                    last.then_inc(degree_ready, 1)

                @block.sync
                def _(sp):
                    sp.wait_ge(counts_ready, 1)
                    sp.dma_start(count_table.rearrange("(t p r) o -> p t (r o)", p=TP, r=NE), counts[:]).then_inc(counts_out, 16)
                    sp.wait_ge(counts_out, 16)

            c_diag.close()
            adj = sbuf(c_adj, "adj", [TP, NT, N], F16)
            spans = [(i, j, min(j + 4, NT)) for j in range(0, NT, 4) for i in range(NT)]

            def turn_blocks(pe, u, b):
                i, j0, j1 = spans[u]
                for j in range(j0, j1):
                    last = pe.transpose(ps[0:TP, b, (j - j0) * TP:(j - j0 + 1) * TP], sums[:, i, tile_of(j)],
                                        ident[0:TP, 0:TP])
                return last

            def put_blocks(act, u, b, link):
                i, j0, j1 = spans[u]
                return act.activation(adj[:, j0:j1, tile_of(i)],
                                      ps[0:TP, b, 0:(j1 - j0) * TP].rearrange("p (j n) -> p j n", j=j1 - j0), ACT.Copy)
            gemm(len(spans), turn_blocks, put_blocks)
            c_sums.close()
            xs = sbuf(c_adj, "xs", [TP, 2, NT, D], F16)

            def aggregate(dstT, others, op):
                def products(pe, u, b):
                    f, (lo, n) = u // 3, CHUNKS[u % 3]
                    for t in range(NT):
                        for part in range(2):
                            last = pe.matmul(ps[:, b, 0:n], xs[:, part, t, f * 128:(f + 1) * 128], adj[:, t, lo:lo + n],
                                             start=t + part == 0, stop=t == NT - 1 and part == 1)
                    return last

                def evac(dve, u, b, link):
                    f, (lo, n) = u // 3, CHUNKS[u % 3]
                    g, v = staging[:, u % 4, 0:n], ps[:, b, 0:n]
                    for other in others(f, lo, n):
                        link(dve.tensor_tensor(g, v, other, op))
                        v = g
                    link(dve.tensor_copy(dstT[:, 0, f, lo:lo + n], g))
                    return dve.tensor_tensor(dstT[:, 1, f, lo:lo + n], g, dstT[:, 0, f, lo:lo + n], ALU.subtract)
                gemm(12, products, evac, evac_on="vector")

            transposes(xn, xT, KD, tokens=xs)
            with ExitStack() as c:
                aggT = sbuf(c, "aggT", [128, 2, KD, N], F16)
                squares = sbuf(c, "squares", [TP, 4, D])
                norm = sbuf(c, "norm", [TP, NT])
                for l in range(3):
                    ws, wn = first[f"L0_self{l}"], first[f"L0_neigh{l}"]
                    aggregate(aggT, lambda f, lo, n: [degree_all[:, lo:lo + n]], ALU.mult)

                    def products(pe, t, b):
                        tok_product(pe, bank(b), xT, t, ring.mat(ws), KD, f"L0_b{l}", stop=False)
                        return tok_product(pe, bank(b), aggT, t, ring.mat(wn), KD, start=False)

                    gemm(NT, products, lambda act, t, b, link: act.activation(xn[:, t, :], bank(b), ACT.Relu),
                         lambda dve, t, b, link: dve.tensor_tensor_reduce(
                             out=squares[:, t % 4, :], in0=xn[:, t, :], in1=xn[:, t, :], scale=1.0, scalar=0.0,
                             op0=ALU.mult, op1=ALU.add, accum_out=norm[:, t:t + 1]),
                         weights={0: [ws, wn]}, frees={NT - 1: 2})
                    if l < 2:
                        layernorm_T(xn, xn, xT, tokens=xs, row_squares=norm)
                        continue
                    with Stage("root_ready", "dve_chain") as (block, root_ready, dve_chain):
                        @block.scalar
                        def _(act):
                            act.activation(norm[:], norm[:], ACT.Sqrt).then_inc(root_ready, 1)

                        @block.vector
                        def _(dve):
                            link = chain(dve, dve_chain)
                            dve.wait_ge(root_ready, 1)
                            link(dve.tensor_scalar(norm[:], norm[:], 1e-12, None, ALU.max))
                            link(dve.reciprocal(norm[:], norm[:]))
                            for t in range(NT):
                                dve.scalar_tensor_tensor(out=x[:, t, :], in0=xn[:, t, :], scalar=norm[:, t:t + 1],
                                                         in1=x[:, t, :], op0=ALU.mult, op1=ALU.add)

            layernorm_T(x, xn, xT)
            with ExitStack() as c:
                share = sbuf(c, "share", [TP, NT, NE])
                col_sum = sbuf(c, "col_sum", [TP, NE])
                row_sum = sbuf(c, "row_sum", [TP, NT])
                gT = sbuf(c, "gT", [NE, N])
                left = sbuf(c, "left", [NE, N])
                picked = sbuf(c, "picked", [NE, N])
                tied = sbuf(c, "tied", [NE, N])
                order = sbuf(c, "order", [NE, N])
                one_row = sbuf(c, "one_row8", [NE, N])
                top = sbuf(c, "top", [NE, 8])
                above = sbuf(c, "above", [NE, 1])
                n_picks = sbuf(c, "n_picks", [TP, NT])
                sel = sbuf(c, "sel", [TP, NT, 2, NE])
                wt = sbuf(c, "wt", [TP, NT, NE])
                g0 = GATE0["L0_gate"]
                gemm(NT, lambda pe, t, b: tok_product(pe, ps[0:TP, b, 0:NE], xT, t, gatew[:, :, g0:g0 + 4, :], KD),
                     lambda dve, t, b, link: dve.tensor_scalar(share[:, t, :], ps[0:TP, b, 0:NE], 1e-10, None, ALU.max),
                     evac_on="vector")
                with Stage("plan_ready", "sums_ready", "dve_chain") as (block, plan_ready, sums_ready, dve_chain):
                    @block.tensor
                    def _(pe):
                        with pe.Fori(0, 8) as i:
                            pe.wait_ge(plan_ready, i + 1)
                            pe.matmul(ps[0:TP, 0, 0:NT * NE], ones[0:TP, 0:TP], share[:].rearrange("p t e -> p (t e)"),
                                      start=True, stop=True).then_inc(sums_ready, 1)

                    @block.vector
                    def _(dve):
                        dve.sem_inc(plan_ready, 1)
                        with dve.Fori(0, 8) as i:
                            link = chain(dve, dve_chain, 5 * i)
                            dve.wait_ge(sums_ready, i + 1)
                            link(dve.tensor_reduce(col_sum[:], ps[0:TP, 0, 0:NT * NE].rearrange("p (t e) -> p e t", e=NE),
                                                   AX.X, ALU.add))
                            link(dve.reciprocal(col_sum[:], col_sum[:]))
                            link(dve.tensor_tensor(share[:], share[:], col_sum[:].rearrange("p (o e) -> p o e", o=1)
                                                   .to_broadcast([TP, NT, NE]), ALU.mult))
                            link(dve.tensor_reduce(row_sum[:], share[:], AX.X, ALU.add))
                            link(dve.reciprocal(row_sum[:], row_sum[:]))
                            dve.tensor_tensor(share[:], share[:], row_sum[:].rearrange("p (t o) -> p t o", o=1)
                                              .to_broadcast([TP, NT, NE]), ALU.mult).then_inc(plan_ready, 1)

                def plan_T(pe, t, b):
                    return pe.transpose(ps[0:NE, b, 0:TP], share[:, t, :], ident[0:TP, 0:TP])
                gemm(NT, plan_T, lambda act, t, b, link: act.activation(gT[:, tile_of(t)], ps[0:NE, b, 0:TP], ACT.Copy))
                with Stage("dve_chain",) as (block, dve_chain):
                    @block.vector
                    def _(dve):
                        link = chain(dve, dve_chain)
                        dve.memset(one_row[:], 1.0)
                        link(dve.tensor_copy(left[:], gT[:]))
                        for r in range((CAP - 1) // 8):
                            link(dve.max(top[:], left[:]))
                            link(dve.match_replace(left[:], top[:], left[:], -1e30))
                        link(dve.max(top[:], left[:]))
                        limit = top[:, (CAP - 1) % 8:(CAP - 1) % 8 + 1]
                        link(dve.tensor_scalar(picked[:], gT[:], limit, None, ALU.is_gt))
                        dve.tensor_reduce(above[:], picked[:], AX.X, ALU.add)
                        link(dve.tensor_scalar(tied[:], gT[:], limit, None, ALU.is_equal))
                        link(dve.tensor_scalar(above[:], above[:], -1.0, float(CAP), ALU.mult, ALU.add))
                        link(dve.tensor_tensor_scan(out=order[:], data0=one_row[:], data1=tied[:], initial=0.0,
                                                    op0=ALU.mult, op1=ALU.add))
                        link(dve.scalar_tensor_tensor(out=tied[:], in0=order[:], scalar=above[:, 0:1], in1=tied[:],
                                                      op0=ALU.is_le, op1=ALU.mult))
                        link(dve.tensor_tensor(picked[:], picked[:], tied[:], ALU.add))
                        dve.scalar_tensor_tensor(out=order[:], in0=gT[:], scalar=0.5, in1=picked[:],
                                                 op0=ALU.is_gt, op1=ALU.mult)

                def picks_back(pe, t, b):
                    pe.transpose(ps[0:TP, b, 0:NE], picked[:, tile_of(t)], ident[0:NE, 0:NE])
                    return pe.transpose(ps[0:TP, b, NE:2 * NE], order[:, tile_of(t)], ident[0:NE, 0:NE])
                gemm(NT, picks_back, lambda act, t, b, link: act.activation(
                    sel[:, t], ps[0:TP, b, 0:2 * NE].rearrange("p (a e) -> p a e", a=2), ACT.Copy))
                with Stage("dve_chain",) as (block, dve_chain):
                    @block.vector
                    def _(dve):
                        link = chain(dve, dve_chain)
                        link(dve.tensor_reduce(n_picks[:], sel[:, :, 0, :], AX.X, ALU.add))
                        link(dve.tensor_scalar(n_picks[:], n_picks[:], 1.0, None, ALU.add))
                        link(dve.reciprocal(n_picks[:], n_picks[:]))
                        dve.tensor_tensor(wt[:], sel[:, :, 1, :], n_picks[:].rearrange("p (t o) -> p t o", o=1)
                                          .to_broadcast([TP, NT, NE]), ALU.mult)

                def expert_products(n0, W, evac_on, evac, store=None, extra=None):
                    turns, per = NE // SLOTS, NT * SLOTS
                    with Stage("product_ready", "banks_free", "stored0", "stored1", "stored2", "stored3") as (
                            block, product_ready, banks_free, *stored):
                        if extra:
                            extra(block)

                        @block.sync
                        def _(sp):
                            ring.issue(sp, n0 + 2 * SLOTS)
                            with sp.Fori(0, turns - 2) as i:
                                for j in range(SLOTS):
                                    sp.wait_ge(ring.split_done, n0 + SLOTS + j + 1 + SLOTS * i)
                                    sp.dma_start(ring.raw[:, (n0 + j) % SLOTS, :].rearrange("p (k n) -> p k n", k=4),
                                                 W[bass.ds(SLOTS * i + 2 * SLOTS + j, 1)].rearrange(
                                        "o (k p) n -> p (o k) n", p=128)).then_inc(ring.loaded[(n0 + j) % SLOTS], 16)

                        def tensor_turn(pe, i):
                            for j in range(SLOTS):
                                pe.wait_ge(ring.split_done, n0 + j + 1 + SLOTS * i)
                                for t in range(NT):
                                    u = NT * j + t
                                    pe.wait_ge(banks_free, per * i + u + 1)
                                    tok_product(pe, bank(u % 4), xT, t, ring.mat(n0 + j), KD).then_inc(product_ready, 1)

                        @block.tensor
                        def _(pe):
                            with pe.Fori(0, turns) as i:
                                tensor_turn(pe, i)

                        def split_next(eng, vector, j, i):
                            n = n0 + SLOTS + j
                            if vector:
                                ring.low_of(eng, n, SLOTS * i)
                            else:
                                ring.high_of(eng, n, i, 16 * i)

                        def drain_turn(eng, i, more):
                            vector = evac_on == "vector"
                            for j in range(SLOTS):
                                for t in range(NT):
                                    u = NT * j + t
                                    eng.wait_ge(product_ready, per * i + u + 1)
                                    evac(eng, t, u, SLOTS * i + j, i, stored).then_inc(banks_free, 1)
                                    if store:
                                        store(eng, t, u, i, stored, banks_free)
                                    if t == 1 and j >= 1 and more:
                                        split_next(eng, vector, j - 1, i)
                                eng.sem_inc(ring.freed[(n0 + j) % SLOTS], 1)
                            if more:
                                split_next(eng, vector, SLOTS - 1, i)

                        def drain(eng):
                            (ring.split_low if evac_on == "vector" else ring.split_high)(eng, n0 + SLOTS)
                            eng.sem_inc(banks_free, 4)
                            if store:
                                for q in stored:
                                    eng.sem_inc(q, 16)
                            with eng.Fori(0, turns - 1) as i:
                                drain_turn(eng, i, True)
                            drain_turn(eng, turns - 1, False)
                            if store:
                                for q in stored:
                                    eng.wait_ge(q, 16 * (NT * NE // 4 + 1))

                        def other(eng):
                            (ring.split_high if evac_on == "vector" else ring.split_low)(eng, n0 + SLOTS)
                            with eng.Fori(0, turns - 1) as i:
                                for j in range(SLOTS):
                                    split_next(eng, evac_on != "vector", j, i)
                        if evac_on == "vector":
                            block.vector(drain)
                            block.scalar(other)
                        else:
                            block.scalar(drain)
                            block.vector(other)
                    ring.issued = ring.high = ring.low = ring.used = n0 + NE

                def add_expert(dve, t, u, e, i, stored):
                    return dve.scalar_tensor_tensor(
                        out=x[:, t, :], in0=bank(u % 4), scalar=wt[:, t, bass.ds(e, 1)], in1=x[:, t, :],
                        op0=ALU.mult, op1=ALU.add)
                expert_products(first["L0_exp"], I["L0_ffn_experts"], "vector", add_expert,
                                extra=gather_counts(c, 0, NC // SC // 2))

            layernorm_T(x, xn, xT, tokens=xs)
            with ExitStack() as c:
                sT = sbuf(c, "sT", [128, 2, KD, N], F16)
                hT = sbuf(c, "hT", [128, 2, KD, N], F16)
                aggregate(sT, lambda f, lo, n: [xT[:, 0, f, lo:lo + n], xT[:, 1, f, lo:lo + n]], ALU.add)
                n1 = first["L1_W1"]
                pr, dst, src_of = feat_units(n1, hT, sT, KD)
                cb = COL0["L1_gnn_b1"]
                gemm(12, pr, *split_evac(ACT.Relu, src_of, pair_of(hT), lambda u: cols[:, cb + u // 3:cb + u // 3 + 1]),
                     weights={0: [n1]}, frees={11: 1})
                dense(hT, first["L1_W2"], x, row="L1_gnn_b2", add=x)

        with ExitStack() as c:
            qT = sbuf(c, "qT1", [128, KD, N])
            k = sbuf(c, "k1", [TP, NT, D])
            vo = sbuf(c, "vo1", [TP, NT, 4, VW])
            peak = sbuf(c, "peak", [128, KD])
            col_scale = sbuf(c, "col_scale", [128, KD])
            n0 = first["L1_qkv"]
            with ExitStack() as c2:
                q = sbuf(c2, "q1", [TP, NT, D])
                qmax = sbuf(c2, "qmax", [TP, NT, H])

                def q_minus_max(dve, t, b, link):
                    v = bank(b).rearrange("p (h d) -> p h d", h=H)
                    link(dve.tensor_reduce(qmax[:, t, :], v, AX.X, ALU.max))
                    return dve.tensor_tensor(q[:, t, :].rearrange("p (h d) -> p h d", h=H), v,
                                             qmax[:, t, :].rearrange("p (h o) -> p h o", o=1).to_broadcast([TP, H, HD]),
                                             ALU.subtract)
                gemm(NT, lambda pe, t, b: tok_product(pe, bank(b), xT, t, ring.mat(n0), KD), q_minus_max,
                     lambda act, t, b, link: act.activation(q[:, t, :], q[:, t, :], ACT.Exp),
                     evac_on="vector", weights={0: [n0]}, frees={NT - 1: 1})
                transposes(q, qT, KD)
            with ExitStack() as c2:
                kT = sbuf(c2, "kT1", [128, KD, N])
                ebuf = sbuf(c2, "ebuf1", [128, 4, D])
                pr, dst, src_of = feat_units(n0 + 1, kT, xT, KD)
                ev, fi = elu1(dst, ebuf, src_of)
                gemm(12, pr, ev, fi, weights={0: [n0 + 1]}, frees={11: 1})
                with Stage("peak_ready", "exp_ready", "dve_chain") as (block, peak_ready, exp_ready, dve_chain):
                    @block.vector
                    def _(dve):
                        link = chain(dve, dve_chain)
                        link(dve.tensor_reduce(peak[:], kT[:], AX.X, ALU.max))
                        dve.tensor_scalar(peak[:], peak[:], -1.0, None, ALU.mult).then_inc(peak_ready, 1)
                        dve.wait_ge(exp_ready, 1)
                        dve.reciprocal(col_scale[:], col_scale[:])

                    @block.scalar
                    def _(act):
                        act.wait_ge(peak_ready, 1)
                        for f in range(KD):
                            last = act.activation(kT[:, f, :], kT[:, f, :], ACT.Exp, bias=peak[:, f:f + 1],
                                                  accum_out=col_scale[:, f:f + 1])
                        last.then_inc(exp_ready, 1)

                def back(pe, t, b):
                    for f in range(KD):
                        last = pe.transpose(ps[0:TP, b, f * 128:(f + 1) * 128], kT[:, f, tile_of(t)], ident[:, :])
                    return last
                gemm(NT, back, lambda act, t, b, link: act.activation(k[:, t, :], bank(b), ACT.Copy))
            values(vo, xT, n0 + 2)
            kv_and_apply(c, qT, k, vo, 0.0, to=k, col_scale=col_scale, den_ones=True)
            aT = qT[:].rearrange("p k n -> p (k n)").bitcast(F16).rearrange("p (s k n) -> p s k n", s=2, k=KD)
            transposes(k, aT, KD)
            dense(aT, first["L1_proj"], x, row="L1_mix_b", add=x)

        def top_two(c, gate, bias_row, srcT, blocks, comb, softmax_first, pk=None, w=None):
            lg = sbuf(c, "logits", [TP, NT, NE])
            eq = sbuf(c, "tie", [TP, NT, NE])
            pre = sbuf(c, "ties_before", [TP, NT, NE])
            pk = sbuf(c, "picks", [TP, NT, 2, NE]) if pk is None else pk
            m = sbuf(c, "top_values", [TP, 2, NT])
            w = sbuf(c, "pick_weights", [TP, 2, NT]) if w is None else w
            g0 = GATE0[gate]
            gemm(NT, lambda pe, t, b: tok_product(pe, ps[0:TP, b, 0:NE], srcT, t, gatew[:, :, g0:g0 + blocks, :], blocks),
                 lambda dve, t, b, link: dve.tensor_tensor(lg[:, t, :], ps[0:TP, b, 0:NE], gateb[0:TP, bias_row, :], ALU.add),
                 evac_on="vector")

            def spread(v):
                return v.rearrange("p (t o) -> p t o", o=1).to_broadcast([TP, NT, NE])

            with Stage("dve_chain", "ready_for_exp", "exp_ready") as (block, dve_chain, ready_for_exp, exp_ready):
                @block.vector
                def _(dve):
                    link = chain(dve, dve_chain)
                    n_exp = 0
                    if softmax_first:
                        link(dve.tensor_reduce(m[:, 0, :], lg[:], AX.X, ALU.max))
                        dve.tensor_tensor(lg[:], lg[:], spread(m[:, 0, :]), ALU.subtract).then_inc(ready_for_exp, 1)
                        n_exp += 1
                        dve.wait_ge(exp_ready, n_exp)
                        link(dve.tensor_reduce(m[:, 0, :], lg[:], AX.X, ALU.add))
                        link(dve.reciprocal(m[:, 0, :], m[:, 0, :]))
                        link(dve.tensor_tensor(lg[:], lg[:], spread(m[:, 0, :]), ALU.mult))
                    for r in range(2):
                        link(dve.tensor_reduce(m[:, r, :], lg[:], AX.X, ALU.max))
                        dve.memset(pre[:], 0.0)
                        link(dve.tensor_tensor(eq[:], lg[:], spread(m[:, r, :]), ALU.is_equal))
                        for e in range(1, NE):
                            link(dve.tensor_tensor(pre[:, :, e], pre[:, :, e - 1], eq[:, :, e - 1], ALU.add))
                        link(dve.scalar_tensor_tensor(out=pk[:, :, r, :], in0=pre[:], scalar=0.0, in1=eq[:],
                                                      op0=ALU.is_equal, op1=ALU.mult))
                        if r == 0:
                            link(dve.scalar_tensor_tensor(out=lg[:], in0=pk[:, :, 0, :], scalar=-1e30, in1=lg[:],
                                                          op0=ALU.mult, op1=ALU.add))
                    dve.tensor_tensor(w[:, 1, :], m[:, 1, :], m[:, 0, :], ALU.subtract).then_inc(ready_for_exp, 1)
                    dve.wait_ge(exp_ready, n_exp + 1)
                    link(dve.tensor_scalar(w[:, 0, :], w[:, 1, :], 1.0, None, ALU.add))
                    link(dve.reciprocal(w[:, 0, :], w[:, 0, :]))
                    link(dve.tensor_tensor(w[:, 1, :], w[:, 1, :], w[:, 0, :], ALU.mult))
                    link(dve.tensor_tensor(comb[:], pk[:, :, 0, :], spread(w[:, 0, :]), ALU.mult))
                    link(dve.tensor_tensor(eq[:], pk[:, :, 1, :], spread(w[:, 1, :]), ALU.mult))
                    dve.tensor_tensor(comb[:], comb[:], eq[:], ALU.add)

                @block.scalar
                def _(act):
                    n_exp = 0
                    if softmax_first:
                        act.wait_ge(ready_for_exp, 1)
                        act.activation(lg[:], lg[:], ACT.Exp).then_inc(exp_ready, 1)
                        n_exp += 1
                    act.wait_ge(ready_for_exp, n_exp + 1)
                    act.activation(w[:, 1, :], w[:, 1, :], ACT.Exp).then_inc(exp_ready, 1)

        def add_expert_biases(c, comb, which, extra=None):
            combT = sbuf(c, "combT", [NE, N])
            gemm(NT, lambda pe, t, b: pe.transpose(ps[0:NE, b, 0:TP], comb[:, t, :], ident[0:TP, 0:TP]),
                 lambda act, t, b, link: act.activation(combT[:, tile_of(t)], ps[0:NE, b, 0:TP], ACT.Copy))
            gemm(NT, lambda pe, t, b: pe.matmul(bank(b), combT[:, tile_of(t)], expert_b2[:, which, :], start=True, stop=True),
                 add_to_x, evac_on="vector", extra=extra)

        def experts(c, n0, comb, func, col, fb, up, down, reload, extra=None):
            turn = SLOTS
            turns = NE // turn
            units = 3 * fb
            order = [(f, ch) for ch in range(3) for f in range(fb)]
            last_unit = [fb * (1 + sum(lo + n <= TP * t + TP - 1 for lo, n in CHUNKS)) for t in range(NT)]
            n_dma = len(ring.loads[n0])
            hT = sbuf(c, "hidden", [128, 2, fb, N], F16)
            bias_now = sbuf(c, "bias_now", [128, turn, fb])
            with Stage("feat_ready", "feat_drained", "hidden_ready", "out_ready", "out_free", "bias_ready",
                       "act_chain") as (block, feat_ready, feat_drained, hidden_ready, out_ready, out_free, bias_ready,
                                           act_chain):
                if extra:
                    extra(block)

                @block.sync
                def _(sp):
                    ring.issue(sp, n0 + 2 * SLOTS)
                    with sp.Fori(0, turns - 2) as i:
                        for s in range(turn):
                            sp.wait_ge(ring.split_done, n0 + s + SLOTS + 1 + SLOTS * i)
                            reload(sp, turn * i + 2 * turn + s, n0 + s)

                @block.tensor
                def _(pe):
                    with pe.Fori(0, turns) as i:
                        for s in range(turn):
                            n = n0 + s
                            pe.wait_ge(ring.split_done, n + 1 + SLOTS * i)
                            for q, (f, ch) in enumerate(order):
                                lo, w = CHUNKS[ch]
                                v = units * s + q
                                pe.wait_ge(feat_drained, units * turn * i + v + 1)
                                feat_product(pe, ps[:, v % 4, 0:w], up(n), f, xT, lo, w, KD).then_inc(feat_ready, 1)
                            for t in range(NT):
                                v = NT * s + t
                                pe.wait_ge(hidden_ready, units * (turn * i + s) + min(last_unit[t], units) + 4)
                                pe.wait_ge(out_free, NT * turn * i + v + 1)
                                tok_product(pe, bank(4 + v % 4), hT, t, down(n), fb).then_inc(out_ready, 1)

                def act_turn(act, i, more):
                    for s in range(turn):
                        act.activation(bias_now[:, s, :], cols[:, bass.ds(fb * turn * i + (col + fb * s), fb)],
                                       ACT.Copy).then_inc(bias_ready, 1)
                        act.wait_ge(bias_ready, turn * i + s + 1)
                        link = chain(act, act_chain, units * (turn * i + s))
                        for q, (f, ch) in enumerate(order):
                            lo, w = CHUNKS[ch]
                            v = units * s + q
                            act.wait_ge(feat_ready, units * turn * i + v + 1)
                            act.wait_ge(hidden_ready, units * turn * i + v + 1)
                            link(act.activation(staging[:, v % 4, 0:w], ps[:, v % 4, 0:w], func, bias=bias_now[:, s, f:f + 1]))
                            act.activation(hT[:, 0, f, lo:lo + w], staging[:, v % 4, 0:w], ACT.Copy).then_inc(feat_drained, 1)
                        if more:
                            ring.high_of(act, n0 + s + SLOTS, i, 16 * n_dma * i)

                def dve_turn(dve, i, more):
                    for s in range(turn):
                        for q, (f, ch) in enumerate(order):
                            lo, w = CHUNKS[ch]
                            v = units * s + q
                            dve.wait_ge(feat_drained, units * turn * i + v + 1 + 4)
                            dve.tensor_tensor(hT[:, 1, f, lo:lo + w], staging[:, v % 4, 0:w], hT[:, 0, f, lo:lo + w],
                                              ALU.subtract).then_inc(hidden_ready, 1)
                        for t in range(NT):
                            v = NT * s + t
                            dve.wait_ge(out_ready, NT * turn * i + v + 1)
                            dve.scalar_tensor_tensor(out=x[:, t, :], in0=bank(4 + v % 4),
                                                     scalar=comb[:, t, bass.ds(turn * i + s, 1)], in1=x[:, t, :],
                                                     op0=ALU.mult, op1=ALU.add).then_inc(out_free, 1)
                        dve.sem_inc(ring.freed[(n0 + s) % SLOTS], 1)
                        if more:
                            ring.low_of(dve, n0 + s + SLOTS, SLOTS * i)

                @block.scalar
                def _(act):
                    ring.split_high(act, n0 + SLOTS)
                    act.sem_inc(feat_drained, 4)
                    with act.Fori(0, turns - 1) as i:
                        act_turn(act, i, True)
                    act_turn(act, turns - 1, False)

                @block.vector
                def _(dve):
                    ring.split_low(dve, n0 + SLOTS)
                    dve.sem_inc(hidden_ready, 4)
                    dve.sem_inc(out_free, 4)
                    with dve.Fori(0, turns - 1) as i:
                        dve_turn(dve, i, True)
                    dve_turn(dve, turns - 1, False)
            ring.issued = ring.high = ring.low = ring.used = n0 + NE

        layernorm_T(x, xn, xT)
        with ExitStack() as c:
            comb = sbuf(c, "comb1", [TP, NT, NE])
            top_two(c, "L1_Wg", 0, xT, 4, comb, False)
            add_expert_biases(c, comb, 0)

            def reload_pair(sp, e, n):
                for lo, hi, k, W in ((0, 2 * D, 4, I["L1_ffn_W1"]), (2 * D, 4 * D, 2, I["L1_ffn_W2"])):
                    sp.dma_start(ring.raw[:, n % SLOTS, lo:hi].rearrange("p (k n) -> p k n", k=k),
                                 W[bass.ds(e, 1)].rearrange("o (k p) n -> p (o k) n", p=128)
                                 ).then_inc(ring.loaded[n % SLOTS], 16)
            experts(c, first["L1_exp"], comb, ACT.Relu, COL0["L1_ffn_b1"], 2,
                    lambda n: ring.mat(n, 0, 2 * D), lambda n: ring.mat(n, 2 * D, 4 * D, 2), reload_pair,
                    extra=gather_counts(c, NC // SC // 2, NC // SC // 2))
        def chunk_view(u, b):
            return ps[:, b, 0:CHUNKS[u % 3][1]]

        with ExitStack() as c:
            hT = sbuf(c, "shared_h", [128, 2, 2, N], F16)
            n = first["L1_shared"]
            cb = COL0["L1_bs1"]

            def shared_up(pe, u, b):
                f, (lo, w) = u // 3, CHUNKS[u % 3]
                return feat_product(pe, ps[:, b, 0:w], ring.mat(n, 0, 2 * D), f, xT, lo, w, KD)
            gemm(6, shared_up, *split_evac(ACT.Relu, chunk_view, pair_of(hT), lambda u: cols[:, cb + u // 3:cb + u // 3 + 1]),
                 weights={0: [n]})
            dense(hT, n, x, k_blocks=2, row="L1_bs2", add=x, scale=0.5)

        MB = 4

        def messages(table, word, dest, weight_word, layer):
            assert NG % MB == 0
            with ExitStack() as c:
                edges = sbuf(c, "edges_m", [128, NC, R])
                index = sbuf(c, "index_stage", [128, MB, GJ], I32)
                got = sbuf(c, "gathered", [128, MB, GJ, D])
                hot = sbuf(c, "weighted_hot", [128, MB, GJ, TP])
                ei = edges[:].bitcast(I32)
                rows_in = [ctx.enter_context(nc.semaphore(f"{layer}_rows_in{s}")) for s in range(MB)]
                with Stage("edges_in", "index_ready", "hot_ready", "sums_ready", "banks_free", "dve_chain") as (
                        block, edges_in, index_ready, hot_ready, sums_ready, banks_free, dve_chain):
                    @block.sync
                    def _(sp):
                        sp.dma_start(edges[:], edge_table.rearrange("(p c) r -> p c r", c=NC)).then_inc(edges_in, 16)
                        ring.issue(sp, ring.used + SLOTS)

                    @block.gpsimd
                    def _(pool):
                        with pool.Fori(0, NG // MB) as i:
                            for s in range(MB):
                                pool.wait_ge(index_ready, MB * i + s + 1)
                                pool.sem_inc(loop_turn, 1)
                                for j in range(GJ):
                                    pool.indirect_dma_start(
                                        got[:, s, j, :], None, table,
                                        bass.IndirectOffsetOnAxis(ap=index[:, s, j:j + 1], axis=0)).then_inc(rows_in[s], 16)

                    def prepare(dve, n, s):
                        link = chain(dve, dve_chain, n)
                        dve.wait_ge(sums_ready, n + 1)
                        ed = edges[:, bass.ds(GJ * n, GJ), :]
                        dve.tensor_copy(index[:, s, :], ei[:, bass.ds(GJ * n, GJ), word]).then_inc(index_ready, 1)
                        link(dve.tensor_tensor(
                            hot[:, s], iota_tile[:].rearrange("p (o n) -> p o n", o=1).to_broadcast([128, GJ, TP]),
                            ed[:, :, F_DST:F_DST + 1].to_broadcast([128, GJ, TP]), ALU.is_equal))
                        if weight_word is None:
                            w = count_weight[:, bass.ds(GJ * n, GJ)].rearrange("p (j o) -> p j o", o=1)
                        else:
                            w = ed[:, :, weight_word:weight_word + 1]
                        dve.tensor_tensor(hot[:, s], hot[:, s], w.to_broadcast([128, GJ, TP]), ALU.mult).then_inc(hot_ready, 1)

                    def add_sums(dve, n, s):
                        dve.wait_ge(sums_ready, n + MB + 1)
                        dve.wait_ge(banks_free, n + MB)
                        tile = dve.value_load(group_tile[0:1, bass.ds(n, 1)], min_val=0, max_val=NT - 1)
                        a = dest[:, bass.ds(tile, 1), :].rearrange("p o d -> p (o d)")
                        dve.tensor_tensor(a, bank(s), a, ALU.add).then_inc(banks_free, 1)

                    @block.vector
                    def _(dve):
                        dve.wait_ge(edges_in, 16)
                        dve.sem_inc(banks_free, MB)
                        for n in range(MB - 1):
                            prepare(dve, n, n)
                        with dve.Fori(0, NG // MB - 1) as i:
                            for s in range(MB):
                                prepare(dve, MB * i + s + (MB - 1), (s + MB - 1) % MB)
                                add_sums(dve, MB * i + s, s)
                        prepare(dve, NG - 1, MB - 1)
                        for s in range(MB):
                            add_sums(dve, NG - MB + s, s)

                    @block.tensor
                    def _(pe):
                        pe.sem_inc(sums_ready, MB)
                        with pe.Fori(0, NG // MB) as i:
                            for s in range(MB):
                                pe.wait_ge(hot_ready, MB * i + s + 1)
                                pe.wait_ge(banks_free, MB * i + s + 1)
                                pe.wait_ge(rows_in[s], 16 * GJ * i + 16 * GJ)
                                for j in range(GJ):
                                    last = pe.matmul(bank(s), hot[:, s, j, :], got[:, s, j, :], start=j == 0, stop=j == GJ - 1)
                                last.then_inc(sums_ready, 1)

        layernorm_T(x, xn, xT)
        dense(xT, first["L2_self"], x, row="L2_bias", add=x)
        with ExitStack() as c:
            rel_out = sbuf(c, "rel_out", [TP, 4, D])

            def stage_rows(act, t, u, e, i, stored):
                act.wait_ge(stored[u % 4], 16 * (NT * SLOTS // 4 * i + u // 4) + 16)
                return act.activation(rel_out[:, u % 4, :], bank(u % 4), ACT.Copy)

            def store_rows(act, t, u, i, stored, banks_free):
                act.wait_ge(banks_free, NT * SLOTS * i + u + 5)
                act.dma_start(rel_table[bass.ds(N * SLOTS * i + u * TP, TP), :], rel_out[:, u % 4, :]).then_inc(stored[u % 4], 16)
            expert_products(first["L2_rel"], I["L2_gnn_W_rel"], "scalar", stage_rows, store_rows)
        messages(rel_table, F_RELSRC, x, None, "L2")

        with ExitStack() as c:
            y = sbuf(c, "y", [TP, NT, D])
            yT = sbuf(c, "yT", [128, 2, KD, N], F16)
            layernorm_T(xn, y, yT, scale=COL0["L2_g"], bias=COL0["L2_bt"])
            qT = sbuf(c, "qT2", [128, KD, N])
            vo = sbuf(c, "vo2", [TP, NT, 4, VW])
            neg_qb = sbuf(c, "neg_qb", [128, KD])
            ebuf = sbuf(c, "ebuf2", [128, 4, D])
            cb = COL0["L2_qb"]
            with Stage("negated") as (block, negated):
                @block.vector
                def _(dve):
                    dve.tensor_scalar(neg_qb[:], cols[:, cb:cb + KD], -1.0, None, ALU.mult)
            n0 = first["L2_qkv"]
            elu_q(qT, ebuf, yT, n0, lambda u: (cols[:, cb + u // 3:cb + u // 3 + 1], neg_qb[:, u // 3:u // 3 + 1]))
            elu_k(y, ebuf, yT, n0 + 1, "L2_kb")
            values(vo, yT, n0 + 2, "L2_vb")
            kv_and_apply(c, qT, y, vo, 1e-8, to=y)
            transposes(y, yT, KD)
            dense(yT, first["L2_out"], x, row="L2_out_b", add=x, add2=xn)

        layernorm_T(x, xn, xT)
        with ExitStack() as c:
            gh = sbuf(c, "gh", [128, 12, CHUNKS[0][1]])
            gh_sums = sbuf(c, "gh_sums", [128, 12])
            gh_mean = sbuf(c, "gh_mean", [128, KD])
            gh_wide = sbuf(c, "gh_wide", [128, KD, 128])
            g_all = sbuf(c, "g_all", [128, NE])
            gate_full = sbuf(c, "gate_full", [128, KD, NE])
            g_col = sbuf(c, "g_col", [NE, 1])
            g_wide = sbuf(c, "g_wide", [NE, TP])
            b1m = sbuf(c, "b1m", [128, 2])
            merged = sbuf(c, "merged", [128, 4 * D])
            tv_rows = sbuf(c, "tv_rows", [NE, 3, D])
            b2_all = sbuf(c, "b2_all", [TP, D])
            lng_all = sbuf(c, "lng_all", [TP, D])
            lnb_all = sbuf(c, "lnb_all", [TP, D])
            hT = sbuf(c, "h2T", [128, 2, 2, N], F16)
            merged_split = sbuf(c, "merged_split", [128, 2, 4 * D], F16)
            res = sbuf(c, "res", [TP, NT, D])
            n0 = first["L2_gfc1"]
            cb = COL0["L2_gfc1_b"]
            pr, _dst, src_of = feat_units(n0, None, xT, KD)
            gemm(12, pr, lambda act, u, b, link: act.activation(
                gh[:, u, 0:CHUNKS[u % 3][1]], src_of(u, b), ACT.Relu, bias=cols[:, cb + u // 3:cb + u // 3 + 1],
                accum_out=gh_sums[:, u:u + 1]),
                weights={0: [n0]}, frees={11: 1})
            nb, nt = first["L2_base"], first["L2_tv"]

            def skip_split(dve, n):
                dve.sem_inc(ring.high_done, 1)
                dve.sem_inc(ring.split_done, 1)
                dve.sem_inc(ring.freed[n % SLOTS], 1)

            with Stage("tv_in", "mean_ready", "gate_ready", "wide_ready", "rows_ready", "dve_chain", "merged_ready",
                       "merged_high", "gate_in") as (block, tv_in, mean_ready, gate_ready, wide_ready, rows_ready, dve_chain,
                                          merged_ready, merged_high, gate_in):
                @block.scalar
                def _(act):
                    act.wait_ge(merged_ready, 1)
                    act.activation(merged_split[:, 0, :], merged[:], ACT.Copy).then_inc(merged_high, 1)

                g0 = GATE0["L2_gfc2"]

                @block.sync
                def _(sp):
                    sp.dma_start(gate_full[:], I["gatew"][:, g0:g0 + KD, :]).then_inc(gate_in, 16)
                    for r, nme in enumerate(("L2_ffn_tv_b2", "L2_ffn_tv_ln_g", "L2_ffn_tv_ln_b")):
                        sp.dma_start(tv_rows[:, r, :], I[nme]).then_inc(tv_in, 16)
                    ring.issue(sp, nb + 1 + NE + SLOTS, over_plain=True)

                @block.vector
                def _(dve):
                    link = chain(dve, dve_chain)
                    link(dve.tensor_reduce(gh_mean[:], gh_sums[:].rearrange("p (f c) -> p f c", c=3), AX.X, ALU.add))
                    link(dve.tensor_scalar(gh_mean[:], gh_mean[:], 1.0 / N, None, ALU.mult))
                    for k in range(KD):
                        last = dve.tensor_scalar(gh_wide[:, k, :], ones[:, :], gh_mean[:, k:k + 1], None, ALU.mult)
                    last.then_inc(mean_ready, 1)
                    dve.wait_ge(gate_ready, 1)
                    link(dve.tensor_tensor(g_all[:], ps[:, 0, 0:NE], gateb[:, 2, :], ALU.add))
                    link(dve.tensor_tensor(g_col[:], ps[0:NE, 1, 0:1], gfc2_col[:], ALU.add))
                    dve.tensor_scalar(g_wide[:], ones[0:NE, 0:TP], g_col[:, 0:1], None, ALU.mult).then_inc(wide_ready, 1)
                    link(dve.tensor_copy(b1m[:], cols[:, COL0["L2_b1"]:COL0["L2_b1"] + 2]))
                    for e in range(NE):
                        cc = COL0["L2_tv_b1"] + 2 * e
                        link(dve.scalar_tensor_tensor(out=b1m[:], in0=cols[:, cc:cc + 2], scalar=g_all[:, e:e + 1],
                                                      in1=b1m[:], op0=ALU.mult, op1=ALU.add))
                    dve.wait_ge(ring.loaded[nb % SLOTS], ring.count[nb])
                    link(dve.tensor_copy(merged[:], ring.raw[:, nb % SLOTS, :]))
                    skip_split(dve, nb)
                    for e in range(NE):
                        dve.wait_ge(ring.loaded[(nt + e) % SLOTS], ring.count[nt + e])
                        link(dve.scalar_tensor_tensor(out=merged[:], in0=ring.raw[:, (nt + e) % SLOTS, :],
                                                      scalar=g_all[:, e:e + 1], in1=merged[:], op0=ALU.mult, op1=ALU.add))
                        skip_split(dve, nt + e)
                    dve.sem_inc(merged_ready, 1)
                    dve.wait_ge(merged_high, 1)
                    dve.tensor_tensor(merged_split[:, 1, :], merged[:], merged_split[:, 0, :], ALU.subtract)
                    dve.wait_ge(rows_ready, 1)
                    dve.tensor_copy(b2_all[:], bank(2))
                    for dst, a, b in ((lng_all, 3, 4), (lnb_all, 5, 6)):
                        link(dve.tensor_scalar(dst[:], bank(b), 0.03, None, ALU.mult))
                        dve.scalar_tensor_tensor(out=dst[:], in0=bank(a), scalar=1.0 - 0.03 * NE, in1=dst[:],
                                                 op0=ALU.mult, op1=ALU.add)

                @block.tensor
                def _(pe):
                    pe.wait_ge(mean_ready, 1)
                    pe.wait_ge(gate_in, 16)
                    for k in range(KD):
                        pe.matmul(ps[:, 0, 0:NE], gh_wide[:, k, :], gate_full[:, k, :], start=k == 0, stop=k == KD - 1)
                    for k in range(KD):
                        last = pe.matmul(ps[0:NE, 1, 0:1], gate_full[:, k, :], gh_mean[:, k:k + 1], start=k == 0, stop=k == KD - 1)
                    last.then_inc(gate_ready, 1)
                    pe.wait_ge(wide_ready, 1)
                    pe.wait_ge(tv_in, 48)
                    pe.matmul(bank(2), g_wide[:, :], tv_rows[:, 0, :], start=True, stop=False)
                    for bk, name in ((2, "L2_b2"), (3, "L2_ln_g"), (5, "L2_ln_b")):
                        pe.matmul(bank(bk), pick[:, ROWS.index(name), :], rows[:], start=bk != 2, stop=True)
                    pe.matmul(bank(4), ones[0:NE, 0:TP], tv_rows[:, 1, :], start=True, stop=True)
                    pe.matmul(bank(6), ones[0:NE, 0:TP], tv_rows[:, 2, :], start=True, stop=True).then_inc(rows_ready, 1)
            ring.used += 1 + NE
            ring.high = ring.low = ring.used
            w1 = merged_split[:, :, 0:2 * D].rearrange("p s (k n) -> p s k n", k=4)
            w2 = merged_split[:, :, 2 * D:4 * D].rearrange("p s (k n) -> p s k n", k=2)

            def up(pe, u, b):
                f, (lo, w) = u // 3, CHUNKS[u % 3]
                return feat_product(pe, ps[:, b, 0:w], w1, f, xT, lo, w, KD)
            gemm(6, up, *split_evac(ACT.Relu, chunk_view, pair_of(hT), lambda u: b1m[:, u // 3:u // 3 + 1]))

            def residual(dve, t, b, link):
                link(dve.tensor_tensor(res[:, t, :], bank(b), xn[:, t, :], ALU.add))
                return dve.tensor_tensor(res[:, t, :], res[:, t, :], b2_all[:], ALU.add)

            def add_ln_b(block):
                @block.gpsimd
                def _(pool):
                    for t in range(NT):
                        pool.tensor_tensor(x[:, t, :], x[:, t, :], lnb_all[:], ALU.add)
            gemm(NT, lambda pe, t, b: tok_product(pe, bank(b), hT, t, w2, 2), residual, evac_on="vector", extra=add_ln_b)
            with Stage("stats_ready", "std_ready", "dve_chain") as (block, stats_ready, std_ready, dve_chain):
                @block.vector
                def _(dve):
                    link = chain(dve, dve_chain)
                    for t in range(NT):
                        last = dve.bn_stats(stats[:, t, :], res[:, t, :])
                    link(last)
                    for t in range(NT):
                        last = dve.bn_aggr(mv[:, t, :], stats[:, t, :])
                    link(last)
                    dve.tensor_scalar(rstd[:], mv[:, :, 1], 1e-5, None, ALU.add).then_inc(stats_ready, 1)
                    for t in range(NT):
                        last = dve.scalar_tensor_tensor(out=res[:, t, :], in0=res[:, t, :], scalar=mv[:, t, 0:1],
                                                        in1=lng_all[:], op0=ALU.subtract, op1=ALU.mult)
                    link(last)
                    dve.wait_ge(std_ready, 1)
                    link(dve.reciprocal(rstd[:], rstd[:]))
                    for t in range(NT):
                        dve.scalar_tensor_tensor(out=x[:, t, :], in0=res[:, t, :], scalar=rstd[:, t:t + 1], in1=x[:, t, :],
                                                 op0=ALU.mult, op1=ALU.add)

                @block.scalar
                def _(act):
                    act.wait_ge(stats_ready, 1)
                    act.activation(rstd[:], rstd[:], ACT.Sqrt).then_inc(std_ready, 1)

        with ExitStack() as c:
            agg = sbuf(c, "agg", [TP, NT, D])
            aggT = sbuf(c, "agg3T", [128, 2, KD, N], F16)

            def clear_sums(block):
                @block.gpsimd
                def _(pool):
                    pool.memset(agg[:], 0.0)
            layernorm_to_table(x, xn, xn_table, 1e-5, clear_sums)
            messages(xn_table, F_SRCI, agg, F_W, "L3")
            transposes(agg, aggT, KD)
            dense(aggT, first["L3_gnn"], x, row="L3_gnn_b", add=x)

        M = 256
        with ExitStack() as c:
            v = sbuf(c, "v3", [TP, NT, D])
            y = sbuf(c, "y3", [TP, NT, D])
            yT = xT
            kp = sbuf(c, "kp", [TP, NT, M])
            qpT = sbuf(c, "qpT", [128, 2, N])
            hT = sbuf(c, "h3T", [128, 2, KD, N], F16)
            sq = sbuf(c, "sq", [TP, NT])
            sq_out = sbuf(c, "sq_out", [TP, D])
            kv = sbuf(c, "kv3", [128, 2, D])
            ksum = sbuf(c, "ksum", [128, 2])
            den = sbuf(c, "den3", [TP, NT])
            layernorm_T(xn, y, hT, 1e-3, COL0["L3_n1_g"], COL0["L3_n1_b"])
            n0, nw = first["L3_kqv"], first["L3_w"]

            q3 = xn
            sqq = sbuf(c, "sqq", [TP, NT])

            def with_square(dst, acc):
                def evac(act, t, b, link):
                    link(act.activation(dst[:, t, :], bank(b), ACT.Copy))
                    return act.activation(sq_out[:], dst[:, t, :], ACT.Square, accum_out=acc[:, t:t + 1])
                return evac
            for j, (dst, acc, row) in enumerate(((y, sq, "L3_kb"), (q3, sqq, "L3_qb"))):
                gemm(NT, lambda pe, t, b, j=j, row=row: tok_product(pe, bank(b), hT, t, ring.mat(n0 + j), KD, row),
                     with_square(dst, acc), weights={0: [n0 + j]}, frees={NT - 1: 1})
            dense(hT, n0 + 2, v, row="L3_vb")
            with Stage("halved") as (block, halved):
                @block.vector
                def _(dve):
                    dve.tensor_scalar(sq[:], sq[:], -0.5, None, ALU.mult)
                    dve.tensor_scalar(sqq[:], sqq[:], -0.5, None, ALU.mult)

            def random_features(src, acc, dst, free):
                transposes(src, yT, KD)
                w = ring.mat(nw, 0, 2 * D)
                gemm(NT, lambda pe, t, b: tok_product(pe, ps[0:TP, b, 0:M], yT, t, w, KD),
                     lambda act, t, b, link: act.activation(dst[:, t, :], ps[0:TP, b, 0:M], ACT.Exp, bias=acc[:, t:t + 1]),
                     weights={0: [nw]}, frees={NT - 1: 1} if free else None)
            random_features(y, sq, kp, False)
            qp = y[:].rearrange("p t d -> p (t d)")[:, 0:NT * M].rearrange("p (t m) -> p t m", m=M)
            random_features(q3, sqq, qp, True)
            transposes(qp, qpT, 2)
            with Stage("kv_ready", "kv_in", "den_ready", "product_ready", "drained", "dve_chain") as (
                    block, kv_ready, kv_in, den_ready, product_ready, drained, dve_chain):
                @block.tensor
                def _(pe):
                    for m in range(2):
                        for t in range(NT):
                            pe.matmul(ps[:, m, 0:D], kp[:, t, m * 128:(m + 1) * 128], v[:, t, :], start=t == 0, stop=t == NT - 1)
                        for t in range(NT):
                            last = pe.matmul(ps[:, 2 + m, 0:1], kp[:, t, m * 128:(m + 1) * 128], ones[0:TP, 0:1],
                                             start=t == 0, stop=t == NT - 1)
                    last.then_inc(kv_ready, 1)
                    pe.wait_ge(kv_in, 1)
                    for t in range(NT):
                        for m in range(2):
                            last = pe.matmul(ps[0:TP, 4, t:t + 1], qpT[:, m, tile_of(t)], ksum[:, m:m + 1],
                                             start=m == 0, stop=m == 1)
                    last.then_inc(den_ready, 1)
                    for t in range(NT):
                        if t >= 3:
                            pe.wait_ge(drained, t - 2)
                        for m in range(2):
                            last = pe.matmul(bank(5 + t % 3), qpT[:, m, tile_of(t)], kv[:, m, :], start=m == 0, stop=m == 1)
                        last.then_inc(product_ready, 1)

                @block.vector
                def _(dve):
                    link = chain(dve, dve_chain)
                    dve.wait_ge(kv_ready, 1)
                    dve.tensor_copy(kv[:], ps[:, 0:2, :])
                    dve.tensor_copy(ksum[:], ps[:, 2:4, 0]).then_inc(kv_in, 1)
                    dve.wait_ge(den_ready, 1)
                    link(dve.tensor_scalar(den[:], ps[0:TP, 4, 0:NT], 1.0 / M, 1e-8, ALU.mult, ALU.add))
                    link(dve.reciprocal(den[:], den[:]))
                    for t in range(NT):
                        dve.wait_ge(product_ready, t + 1)
                        dve.tensor_scalar(q3[:, t, :], bank(5 + t % 3), 1.0 / M, den[:, t:t + 1], ALU.mult,
                                          ALU.mult).then_inc(drained, 1)
            transposes(q3, yT, KD)
            dense(yT, first["L3_proj"], y, row="L3_proj_b", add=v)
            layernorm_T(y, v, yT, 1e-3, COL0["L3_n2_g"], COL0["L3_n2_b"])
            pr, dst, src_of = feat_units(first["L3_mlp1"], hT, yT, KD)
            cb = COL0["L3_mlp_b1"]
            gemm(12, pr, *split_evac(ACT.Gelu, src_of, pair_of(hT), lambda u: cols[:, cb + u // 3:cb + u // 3 + 1]),
                 weights={0: [first["L3_mlp1"]]}, frees={11: 1})
            dense(hT, first["L3_mlp2"], x, row="L3_mlp_b2", add=x, add2=y)

        layernorm_T(x, xn, xT)
        with ExitStack() as c:
            comb = sbuf(c, "comb3", [TP, NT, NE])
            pk = sbuf(c, "picks3", [TP, NT, 2, NE])
            pick_w = sbuf(c, "pick_weights3", [TP, 2, NT])
            place = sbuf(c, "place", [TP, 2, NT], I32)
            group_expert = sbuf(c, "group_expert", [1, PG], I32)
            with ExitStack() as c2:
                gT = sbuf(c2, "gate_hT", [128, 2, 2, N], F16)
                n = first["L3_gw1"]
                cb = COL0["L3_gb1"]

                def gate_up(pe, u, b):
                    f, (lo, w) = u // 3, CHUNKS[u % 3]
                    return feat_product(pe, ps[:, b, 0:w], ring.mat(n, 0, 2 * D), f, xT, lo, w, KD)
                gemm(6, gate_up, *split_evac(ACT.Relu, chunk_view, pair_of(gT), lambda u: cols[:, cb + u // 3:cb + u // 3 + 1]),
                     weights={0: [n]}, frees={5: 1})
                top_two(c2, "L3_gw2", 1, gT, 2, comb, True, pk, pick_w)
            with ExitStack() as c2:
                picked = sbuf(c2, "picked3", [TP, NT, NE])
                tile_sum = sbuf(c2, "tile_sum", [TP, NT, NE])
                before = sbuf(c2, "before", [TP, NT, NE])
                total = sbuf(c2, "expert_total", [TP, NE])
                expert_groups = sbuf(c2, "expert_groups", [TP, NE])
                groups_to = sbuf(c2, "groups_to", [TP, NE])
                start_row = sbuf(c2, "start_row", [TP, NE])
                place_f = sbuf(c2, "place_f", [TP, 2, NT])
                expert_f = sbuf(c2, "expert_f", [1, PG])
                picks_out = ctx.enter_context(nc.semaphore("picks_out"))
                with Stage("picked_ready", "ranks_ready", "dve_chain") as (block, picked_ready, ranks_ready, dve_chain):
                    @block.tensor
                    def _(pe):
                        pe.wait_ge(picked_ready, 1)
                        pe.matmul(ps[0:TP, 0, 0:NT * NE], below[:], picked[:].rearrange("p t e -> p (t e)"), start=True, stop=True)
                        pe.matmul(ps[0:TP, 1, 0:NT * NE], ones[0:TP, 0:TP], picked[:].rearrange("p t e -> p (t e)"),
                                  start=True, stop=True).then_inc(ranks_ready, 1)

                    @block.vector
                    def _(dve):
                        link = chain(dve, dve_chain)
                        dve.memset(expert_f[:], 0.0)
                        dve.memset(expert_groups[:], 0.0)
                        dve.memset(before[:], 0.0)
                        dve.tensor_tensor(picked[:], pk[:, :, 0, :], pk[:, :, 1, :], ALU.add).then_inc(picked_ready, 1)
                        dve.wait_ge(ranks_ready, 1)
                        link(dve.tensor_copy(tile_sum[:], ps[0:TP, 1, 0:NT * NE].rearrange("p (t e) -> p t e", e=NE)))
                        for t in range(1, NT):
                            link(dve.tensor_tensor(before[:, t, :], before[:, t - 1, :], tile_sum[:, t - 1, :], ALU.add))
                        link(dve.tensor_tensor(total[:], before[:, NT - 1, :], tile_sum[:, NT - 1, :], ALU.add))
                        for m in range(-(-N // GR)):
                            link(dve.scalar_tensor_tensor(out=expert_groups[:], in0=total[:], scalar=float(m * GR),
                                                          in1=expert_groups[:], op0=ALU.is_gt, op1=ALU.add))
                        link(dve.tensor_tensor_scan(out=groups_to[:], data0=ones[0:TP, 0:NE], data1=expert_groups[:],
                                                    initial=0.0, op0=ALU.mult, op1=ALU.add))
                        link(dve.tensor_tensor(start_row[:], groups_to[:], expert_groups[:], ALU.subtract))
                        link(dve.tensor_scalar(start_row[:], start_row[:], float(GR), None, ALU.mult))
                        link(dve.tensor_tensor(before[:], before[:], start_row[:].rearrange("p (o e) -> p o e", o=1)
                                               .to_broadcast([TP, NT, NE]), ALU.add))
                        link(dve.tensor_tensor(before[:], ps[0:TP, 0, 0:NT * NE].rearrange("p (t e) -> p t e", e=NE),
                                               before[:], ALU.add))
                        for q in range(2):
                            link(dve.tensor_tensor(picked[:], before[:], pk[:, :, q, :], ALU.mult))
                            link(dve.tensor_reduce(place_f[:, q, :], picked[:], AX.X, ALU.add))
                        dve.tensor_copy(place[:], place_f[:])
                        for e in range(NE - 1):
                            link(dve.scalar_tensor_tensor(out=expert_f[:], in0=iota_tile[0:1, 0:PG],
                                                          scalar=groups_to[0:1, e:e + 1], in1=expert_f[:],
                                                          op0=ALU.is_ge, op1=ALU.add))
                        dve.tensor_copy(group_expert[:], expert_f[:])

                def scatter_picks(block):
                    @block.gpsimd
                    def _(pool):
                        for q in range(2):
                            for t in range(NT):
                                pool.indirect_dma_start(rel_table, bass.IndirectOffsetOnAxis(ap=place[:, q, t:t + 1], axis=0),
                                                        xn[:, t, :], None).then_inc(picks_out, 16)
                        pool.wait_ge(picks_out, 16 * 2 * NT)
                add_expert_biases(c2, comb, 1, extra=scatter_picks)

            with ExitStack() as c2:
                S0 = len(loads)
                base = [sum(16 * len(parts) for m, parts in enumerate(loads) if m % SLOTS == s) for s in range(SLOTS)]
                UP = 2 * KD
                PER = UP + KD
                rows3 = sbuf(c2, "group_rows", [128, 2, GT, D])
                gxT = sbuf(c2, "group_xT", [128, 2, KD, GR], F16)
                hT = sbuf(c2, "group_hT", [128, 2, UP, GR], F16)
                outs = sbuf(c2, "group_out", [128, 2, GT, D])
                bias_now = sbuf(c2, "bias_now3", [128, UP])
                we = (I["L3_ffn_we1"], I["L3_ffn_we1"], I["L3_ffn_we2"], I["L3_ffn_we2"])

                def slot_of(m):
                    return (S0 + m) % SLOTS

                def rows_at(table, g):
                    return table[bass.ds(GR * g, GR), :].rearrange("(t p) d -> p t d", p=128)

                with Stage("rows_in0", "rows_in1", "feat_ready", "feat_drained", "hidden_ready", "out_ready", "out_free",
                           "bias_ready", "act_chain", "stored0", "stored1") as (
                        block, rows_in0, rows_in1, feat_ready, feat_drained, hidden_ready, out_ready, out_free, bias_ready,
                        act_chain, *stored):
                    rows_in = (rows_in0, rows_in1)

                    def sp_turn(sp, i, more):
                        for b in range(2):
                            g = 2 * i + b
                            e = sp.value_load(group_expert[0:1, bass.ds(g, 1)], min_val=0, max_val=NE - 1)
                            for j in range(4):
                                m = 4 * b + j
                                if j == 2 and (more or b == 0):
                                    sp.wait_ge(feat_ready, PER * g + KD)
                                    sp.dma_start(rows3[:, 1 - b], rows_at(rel_table, g + 1)).then_inc(rows_in[1 - b], 16)
                                sp.wait_ge(ring.split_done, 8 * i + (S0 + m - SLOTS + 1))
                                sp.dma_start(ring.raw[:, slot_of(m), :].rearrange("p (k n) -> p k n", k=4),
                                             we[j][bass.ds(e * 2 + j % 2, 1)].rearrange("o (k p) n -> p (o k) n", p=128)
                                             ).then_inc(ring.loaded[slot_of(m)], 16)

                    @block.sync
                    def _(sp):
                        sp.dma_start(rows3[:, 0], rows_at(rel_table, 0)).then_inc(rows_in[0], 16)
                        with sp.Fori(0, PG // 2 - 1) as i:
                            sp_turn(sp, i, True)
                        sp_turn(sp, PG // 2 - 1, False)

                    def turn_rows(pe, v0, v, b):
                        for k in range(KD):
                            pe.wait_ge(feat_drained, v0 + v + k + 1)
                            for t in range(GT):
                                last = pe.transpose(ps[:, (v + k) % 4, t * 128:(t + 1) * 128],
                                                    rows3[:, b, t, k * 128:(k + 1) * 128], ident[:, :])
                            last.then_inc(feat_ready, 1)

                    def pe_turn(pe, i, more):
                        v0 = 2 * PER * i
                        for b in range(2):
                            v = PER * b + KD
                            pe.wait_ge(hidden_ready, v0 + v + 4)
                            for h in range(2):
                                pe.wait_ge(ring.split_done, 8 * i + (S0 + 4 * b + h + 1))
                                for f in range(KD):
                                    pe.wait_ge(feat_drained, v0 + v + 1)
                                    feat_product(pe, ps[:, v % 4, 0:GR], ring.mat(S0 + 4 * b + h), f, gxT, 0, GR,
                                                 KD).then_inc(feat_ready, 1)
                                    v += 1
                            if more or b == 0:
                                pe.wait_ge(rows_in[1 - b], 16 * i + 16 * (1 + b))
                                turn_rows(pe, v0, v, 1 - b)
                            for h in range(2):
                                pe.wait_ge(ring.split_done, 8 * i + (S0 + 4 * b + 3 + h))
                                pe.wait_ge(hidden_ready, v0 + PER * b + KD + KD * (h + 1) + 4)
                                wd = ring.mat(S0 + 4 * b + 2 + h)
                                for t in range(GT):
                                    if h == 0:
                                        pe.wait_ge(out_free, 2 * GT * i + GT * b + t + 1)
                                    for k in range(KD):
                                        for pa, pb in PASSES:
                                            last = pe.matmul(
                                                bank(4 + t, 128), hT[:, pa, KD * h + k, t * 128:(t + 1) * 128], wd[:, pb, k, :],
                                                start=h == 0 and k + pa + pb == 0, stop=h == 1 and k == KD - 1 and pa == 1)
                                    if h == 1:
                                        last.then_inc(out_ready, 1)
                                if h == 0:
                                    last.then_inc(ring.freed[slot_of(4 * b + 2)], 1)

                    @block.tensor
                    def _(pe):
                        pe.wait_ge(rows_in[0], 16)
                        turn_rows(pe, 0, 0, 0)
                        with pe.Fori(0, PG // 2 - 1) as i:
                            pe_turn(pe, i, True)
                        pe_turn(pe, PG // 2 - 1, False)

                    def high(act, m, i=0):
                        s = slot_of(m)
                        act.wait_ge(ring.freed[s], 4 * i + (S0 + m) // SLOTS)
                        act.wait_ge(ring.loaded[s], 64 * i + (base[s] + 16 * (m // SLOTS + 1)))
                        act.activation(ring.buf[:, s, 0, :], ring.raw[:, s, :], ACT.Copy).then_inc(ring.high_done, 1)

                    def low(dve, m, i=0):
                        s = slot_of(m)
                        dve.wait_ge(ring.high_done, 8 * i + (S0 + m + 1))
                        dve.tensor_tensor(ring.buf[:, s, 1, :], ring.raw[:, s, :], ring.buf[:, s, 0, :],
                                          ALU.subtract).then_inc(ring.split_done, 1)

                    def act_unit(act, v0, v, dst, func, **bias):
                        link = chain(act, act_chain, v0 + v)
                        act.wait_ge(feat_ready, v0 + v + 1)
                        act.wait_ge(hidden_ready, v0 + v + 1)
                        link(act.activation(staging[:, v % 4, 0:GR], ps[:, v % 4, 0:GR], func, **bias))
                        act.activation(dst, staging[:, v % 4, 0:GR], ACT.Copy).then_inc(feat_drained, 1)

                    def act_turn(act, i, more):
                        v0 = 2 * PER * i
                        for b in range(2):
                            g = 2 * i + b
                            e = act.value_load(group_expert[0:1, bass.ds(g, 1)], min_val=0, max_val=NE - 1)
                            act.activation(bias_now[:], cols[:, bass.ds(e * UP + COL0["L3_be1"], UP)],
                                           ACT.Copy).then_inc(bias_ready, 1)
                            act.wait_ge(bias_ready, g + 1)
                            v = PER * b + KD
                            for h in range(2):
                                for f in range(KD):
                                    act_unit(act, v0, v, hT[:, 0, KD * h + f, :], ACT.Gelu,
                                             bias=bias_now[:, KD * h + f:KD * h + f + 1])
                                    v += 1
                                act.sem_inc(ring.freed[slot_of(4 * b + h)], 1)
                                high(act, 4 * b + 2 + h, i)
                            if more or b == 0:
                                for k in range(KD):
                                    act_unit(act, v0, v, gxT[:, 0, k, :], ACT.Copy)
                                    v += 1
                                high(act, 4 * b + 4, i)
                                high(act, 4 * b + 5, i)
                            act.wait_ge(out_free, 2 * GT * i + GT * (b + 2))
                            act.dma_start(rows_at(pick_table, g), outs[:, b]).then_inc(stored[b], 16)

                    @block.scalar
                    def _(act):
                        act.sem_inc(feat_drained, 4)
                        for k in range(KD):
                            act_unit(act, 0, k, gxT[:, 0, k, :], ACT.Copy)
                        high(act, 0)
                        high(act, 1)
                        with act.Fori(0, PG // 2 - 1) as i:
                            act_turn(act, i, True)
                        act_turn(act, PG // 2 - 1, False)
                        for b in range(2):
                            act.wait_ge(stored[b], 16 * (PG // 2 + 1))

                    def dve_unit(dve, v0, v, high_part, low_part):
                        dve.wait_ge(feat_drained, v0 + v + 1 + 4)
                        dve.tensor_tensor(low_part, staging[:, v % 4, 0:GR], high_part, ALU.subtract).then_inc(hidden_ready, 1)

                    def dve_turn(dve, i, more):
                        v0 = 2 * PER * i
                        for b in range(2):
                            go_on = more or b == 0
                            v = PER * b + KD
                            for h in range(2):
                                for f in range(KD):
                                    dve_unit(dve, v0, v, hT[:, 0, KD * h + f, :], hT[:, 1, KD * h + f, :])
                                    v += 1
                                low(dve, 4 * b + 2 + h, i)
                            if go_on:
                                for k in range(KD):
                                    dve_unit(dve, v0, v, gxT[:, 0, k, :], gxT[:, 1, k, :])
                                    v += 1
                                low(dve, 4 * b + 4, i)
                            dve.wait_ge(stored[b], 16 * i + 16)
                            for t in range(GT):
                                dve.wait_ge(out_ready, 2 * GT * i + GT * b + t + 1)
                                dve.tensor_copy(outs[:, b, t, :], bank(4 + t, 128)).then_inc(out_free, 1)
                            dve.sem_inc(ring.freed[slot_of(4 * b + 3)], 1)
                            if go_on:
                                low(dve, 4 * b + 5, i)

                    @block.vector
                    def _(dve):
                        dve.sem_inc(hidden_ready, 4)
                        dve.sem_inc(out_free, GT)
                        for q in stored:
                            dve.sem_inc(q, 16)
                        for k in range(KD):
                            dve_unit(dve, 0, k, gxT[:, 0, k, :], gxT[:, 1, k, :])
                        low(dve, 0)
                        low(dve, 1)
                        with dve.Fori(0, PG // 2 - 1) as i:
                            dve_turn(dve, i, True)
                        dve_turn(dve, PG // 2 - 1, False)

            with ExitStack() as c2:
                back = sbuf(c2, "picks_back", [TP, 2, NT, D])
                results_in = [ctx.enter_context(nc.semaphore(f"results_in{h}")) for h in range(2)]
                with Stage("first_added", "half_added", "x_out") as (block, first_added, half_added, x_out):
                    @block.gpsimd
                    def _(pool):
                        for t in range(NT):
                            for q in range(2):
                                pool.indirect_dma_start(back[:, q, t, :], None, pick_table, bass.IndirectOffsetOnAxis(
                                    ap=place[:, q, t:t + 1], axis=0)).then_inc(results_in[t // (NT // 2)], 16)

                    @block.vector
                    def _(dve):
                        for h in range(2):
                            tiles = range(h * (NT // 2), (h + 1) * (NT // 2))
                            dve.wait_ge(results_in[h], 16 * NT)
                            for q in range(2):
                                for t in tiles:
                                    last = dve.scalar_tensor_tensor(out=x[:, t, :], in0=back[:, q, t, :],
                                                                    scalar=pick_w[:, q, t:t + 1], in1=x[:, t, :],
                                                                    op0=ALU.mult, op1=ALU.add)
                                last.then_inc(half_added if q else first_added, 1)
                                if q == 0:
                                    dve.wait_ge(first_added, h + 1)

                    @block.sync
                    def _(sp):
                        for h in range(2):
                            tiles = slice(h * (NT // 2), (h + 1) * (NT // 2))
                            sp.wait_ge(half_added, h + 1)
                            sp.dma_start(out.rearrange("(t p) d -> p t d", p=TP)[:, tiles, :], x[:, tiles, :]).then_inc(x_out, 16)
                        sp.wait_ge(x_out, 32)



def kernel(**inputs):
    import numpy as np
    import concourse.bacc as bacc
    from concourse import mybir as mb
    from concourse.bass_utils import run_bass_kernel_spmd as run

    a = {n: np.asarray(v) for n, v in inputs.items()}
    given = {n: a[n] for n in ("x", "src", "dst", "edge_type_8", "edge_weight1",
                               "L0_gnn_W_self", "L0_gnn_W_neigh", "L0_ffn_experts", "L1_gnn_W1", "L1_gnn_W2",
                               "L1_mix_w_qkv", "L1_mix_w_proj", "L1_ffn_W1", "L1_ffn_W2", "L1_ffn_Ws1", "L1_ffn_Ws2",
                               "L1_ffn_b2", "L2_ffn_tv_b2", "L2_ffn_tv_ln_g", "L2_ffn_tv_ln_b",
                               "L3_mix_kqv_w", "L3_mix_proj_w", "L3_mix_mlp_w1", "L3_mix_mlp_w2",
                               "L3_ffn_gw1", "L3_ffn_be2")}
    given["L3_ffn_we1"] = a["L3_ffn_we1"].reshape(NE, D, 2, D).transpose(0, 2, 1, 3).reshape(2 * NE, D, D)
    given["L3_ffn_we2"] = a["L3_ffn_we2"].reshape(2 * NE, D, D)
    for n in ("L0_mix_Wq", "L0_mix_Wkv", "L2_gnn_W_self", "L2_mix_qkv_w", "L2_mix_out_w", "L2_ffn_gfc1_w",
              "L2_ffn_W1", "L2_ffn_W2", "L3_gnn_W", "L3_mix_w"):
        given[n] = a[n].T
    for n in ("L2_gnn_W_rel", "L2_ffn_tv_W1", "L2_ffn_tv_W2"):
        given[n] = a[n].transpose(0, 2, 1)
    qb, kb = a["L2_mix_qkv_b"], a["L3_mix_kqv_b"]
    row = {"L0_b0": a["L0_gnn_b"][0], "L0_b1": a["L0_gnn_b"][1], "L0_b2": a["L0_gnn_b"][2],
           "L1_gnn_b2": a["L1_gnn_b2"], "L1_mix_b": a["L1_mix_b_proj"], "L1_bs2": a["L1_ffn_bs2"],
           "L2_bias": a["L2_gnn_bias"], "L2_kb": qb[D:2 * D], "L2_vb": qb[2 * D:], "L2_out_b": a["L2_mix_out_b"],
           "L2_b2": a["L2_ffn_b2"], "L2_ln_g": a["L2_ffn_ln_g"], "L2_ln_b": a["L2_ffn_ln_b"],
           "L3_gnn_b": a["L3_gnn_b"], "L3_kb": kb[0:D], "L3_qb": kb[D:2 * D], "L3_vb": kb[2 * D:],
           "L3_proj_b": a["L3_mix_proj_b"], "L3_mlp_b2": a["L3_mix_mlp_b2"]}
    given["rows"] = np.stack([row[n] for n in ROWS])
    col = {"L1_gnn_b1": a["L1_gnn_b1"], "L1_ffn_b1": a["L1_ffn_b1"].reshape(-1), "L1_bs1": a["L1_ffn_bs1"],
           "L2_qb": qb[0:D], "L2_g": a["L2_mix_ln_gamma"], "L2_bt": a["L2_mix_ln_beta"],
           "L2_gfc1_b": a["L2_ffn_gfc1_b"], "L2_b1": a["L2_ffn_b1"], "L2_tv_b1": a["L2_ffn_tv_b1"].reshape(-1),
           "L3_n1_g": a["L3_mix_n1_g"], "L3_n1_b": a["L3_mix_n1_b"], "L3_n2_g": a["L3_mix_n2_g"],
           "L3_n2_b": a["L3_mix_n2_b"], "L3_mlp_b1": a["L3_mix_mlp_b1"], "L3_gb1": a["L3_ffn_gb1"],
           "L3_be1": a["L3_ffn_be1"].reshape(-1)}
    given["cols"] = np.concatenate([col[n] for n in COLS]).reshape(NCOL, 128).T
    gate = {"L0_gate": a["L0_ffn_gate_w"][0], "L1_Wg": a["L1_ffn_Wg"], "L2_gfc2": a["L2_ffn_gfc2_w"].T,
            "L3_gw2": a["L3_ffn_gw2"]}
    given["gatew"] = np.concatenate([gate[n] for n in GATES]).reshape(NGATE, 128, NE).transpose(1, 0, 2)
    given["gateb"] = np.stack([a["L1_ffn_bg"], a["L3_ffn_gb2"], a["L2_ffn_gfc2_b"]])
    given["gfc2_col"] = a["L2_ffn_gfc2_b"].reshape(NE, 1)

    nc = bacc.Bacc("TRN2", target_bir_lowering=False, num_devices=1)
    arrays, ins = {}, {}
    for n, v in given.items():
        v = np.ascontiguousarray(v)
        arrays[f"in_{n}"] = v
        ins[n] = nc.dram_tensor(f"in_{n}", v.shape, mb.dt.from_np(v.dtype), kind="ExternalInput").ap()
    out = nc.dram_tensor("out_x", (N, D), mb.dt.float32, kind="ExternalOutput").ap()
    build(nc, ins, out)
    return run(nc, [arrays], core_ids=[0]).results[0]["out_x"]
```
